# Optimizing a Trainium2 kernel written in Bass

```python
import numpy as np
import jax
import jax.numpy as jnp

def _softmax(x, axis=-1):
    return jax.nn.softmax(x, axis=axis)

def _gelu(x):
    return jax.nn.gelu(x, approximate=True)

def _silu(x):
    return jax.nn.silu(x)

def _sigmoid(x):
    return jax.nn.sigmoid(x)

def _layernorm(x, axis=-1, eps=1e-05):
    m = jnp.mean(x, axis=axis, keepdims=True)
    v = jnp.var(x, axis=axis, keepdims=True)
    return (x - m) / jnp.sqrt(v + eps)

def _scatter_add(tgt, idx, src, axis=0):
    return tgt.at[idx].add(src)

def _segment_sum(src, seg, n):
    return jax.ops.segment_sum(src, seg, n)
kernel_name = 'mk_flamingo_gated_d2_seqx_r8_f4d450'

def setup_inputs(seed: int=0):
    np.random.seed(seed)
    _w = jnp.asarray

    def _rec_inputs():
        import jax
        import jax.numpy as jnp
        _rk = jax.random.key(seed)
        x = -0.0002928 + 1 * jax.random.normal(jax.random.fold_in(_rk, 1), (8, 56, 256), jnp.float32)
        _lenS = 56 - jax.random.randint(jax.random.fold_in(_rk, 7), (8,), 0, max(1, 56 // 4) + 1, jnp.int32)
        _lenS2 = 1500 - jax.random.randint(jax.random.fold_in(_rk, 8), (8,), 0, max(1, 1500 // 4) + 1, jnp.int32)
        _ctx_2048P = jax.random.normal(jax.random.fold_in(_rk, 11), (8, 16, 256), jnp.float32)
        _ctx_2048c = jax.random.dirichlet(jax.random.fold_in(_rk, 511), 0.3 * jnp.ones((16,), jnp.float32), (8, 1500))
        _ctx_2048t = jnp.einsum('bsk,bkd->bsd', _ctx_2048c, _ctx_2048P)
        _ctx_2048t = _ctx_2048t * jax.lax.rsqrt(jnp.mean(jnp.square(_ctx_2048t)) + 1e-12) * 0.953939
        ctx_2048 = 4.13588e-05 + 0.999923 * (_ctx_2048t + 0.3 * jax.random.normal(jax.random.fold_in(_rk, 611), (8, 1500, 256), jnp.float32))
        _validS = jnp.arange(56)[None, :] < _lenS[:, None]
        _validS2 = jnp.arange(1500)[None, :] < _lenS2[:, None]
        _causal = jnp.tril(jnp.ones((56, 56), dtype=bool))
        mask_1xSxS2_ff0 = jnp.where(jnp.ones((1, 56, 1500), dtype=bool), 0.0, -1000000000.0).astype(jnp.float32)
        mask_BxS2_ik0 = jnp.where(jnp.broadcast_to(_validS2[:, :], (8, 1500)), 0, 1).astype(jnp.int32)
        _g = jax.random.normal(jax.random.fold_in(_rk, 9001), (2, 2), jnp.float32)
        _g = jnp.sign(_g) * jnp.maximum(jnp.abs(_g), 1.0) + (_g == 0) * 1.0
        g_xattn = _g[0]
        g_ffn = _g[1]
        return (x, ctx_2048, mask_1xSxS2_ff0, mask_BxS2_ik0, g_xattn, g_ffn)
    x, ctx_2048, mask_1xSxS2_ff0, mask_BxS2_ik0, g_xattn, g_ffn = _rec_inputs()

    def _L0_xattn_setup():
        import jax, jax.numpy as jnp
        import numpy as np
        H = 256
        NH = 16
        NKV = 4
        HD = 128
        GROUPS = NH // NKV
        EPS = 1e-06
        B, S, SE = (1, 256, 512)

        def _rmsnorm(x, w, eps=EPS):
            xf = x.astype(jnp.float32)
            var = jnp.mean(xf * xf, axis=-1, keepdims=True)
            return (xf * jax.lax.rsqrt(var + eps)).astype(x.dtype) * w
        key = jax.random.key(seed)
        ks = jax.random.split(key, 12)
        sc = 0.02
        return {'hidden_states': jax.random.normal(ks[0], (B, S, H), jnp.float32), 'encoder_hidden_states': jax.random.normal(ks[1], (B, SE, H), jnp.float32), 'attention_mask': jnp.zeros((B, S, SE), jnp.float32), 'Wq': jax.random.normal(ks[2], (H, NH * HD), jnp.float32) * sc, 'bq': jax.random.normal(ks[3], (NH * HD,), jnp.float32) * sc, 'Wk': jax.random.normal(ks[4], (H, NKV * HD), jnp.float32) * sc, 'bk': jax.random.normal(ks[5], (NKV * HD,), jnp.float32) * sc, 'Wv': jax.random.normal(ks[6], (H, NKV * HD), jnp.float32) * sc, 'bv': jax.random.normal(ks[7], (NKV * HD,), jnp.float32) * sc, 'Wo': jax.random.normal(ks[8], (NH * HD, H), jnp.float32) * sc, 'qn_w': jnp.ones((HD,), jnp.float32), 'kn_w': jnp.ones((HD,), jnp.float32)}
    _L0_xattn_all = _L0_xattn_setup()
    _L0_xattn_in = {k: v for k, v in _L0_xattn_all.items() if k in ('Wq', 'bq', 'Wk', 'bk', 'Wv', 'bv', 'Wo', 'qn_w', 'kn_w')}
    del _L0_xattn_all

    def _L0_ffn_setup():
        import jax, jax.numpy as jnp
        import numpy as np
        ACT_BITS = 8
        EPS = 1e-05

        def act_quant(x, bits=ACT_BITS):
            qb = float(2 ** (bits - 1))
            scale = qb / jnp.clip(jnp.max(jnp.abs(x), axis=-1, keepdims=True), EPS)
            xq = jnp.clip(jnp.round(x * scale), -qb, qb - 1) / scale
            return x + jax.lax.stop_gradient(xq - x)

        def weight_quant(w):
            scale = 1.0 / jnp.clip(jnp.mean(jnp.abs(w)), EPS)
            wq = jnp.clip(jnp.round(w * scale), -1.0, 1.0) / scale
            return w + jax.lax.stop_gradient(wq - w)

        def fwht(x):
            shape = x.shape
            n = shape[-1]
            x = x.reshape(-1, n)
            h = 1
            while h < n:
                x = x.reshape(-1, n // (2 * h), 2, h)
                a, b = (x[..., 0, :], x[..., 1, :])
                x = jnp.stack([a + b, a - b], axis=-2).reshape(-1, n)
                h *= 2
            return (x * (1.0 / np.sqrt(n)).astype(np.float32)).reshape(shape)

        def bitlinear(x, w):
            return jnp.einsum('bsh,oh->bso', act_quant(x), weight_quant(w))

        def h_bitlinear(x, w):
            return jnp.einsum('bsh,oh->bso', act_quant(fwht(x)), weight_quant(w))
        key = jax.random.key(seed)
        k1, k2, k3, k4 = jax.random.split(key, 4)
        H, I = (256, 1024)
        B, S = (4, 256)
        std_in = 1.0 / np.sqrt(H)
        std_mid = 1.0 / np.sqrt(I)
        return {'x': jax.random.normal(k1, (B, S, H), dtype=jnp.float32), 'w_gate': jax.random.normal(k2, (I, H), dtype=jnp.float32) * std_in, 'w_up': jax.random.normal(k3, (I, H), dtype=jnp.float32) * std_in, 'w_down': jax.random.normal(k4, (H, I), dtype=jnp.float32) * std_mid}
    _L0_ffn_all = _L0_ffn_setup()
    _L0_ffn_in = {k: v for k, v in _L0_ffn_all.items() if k in ('w_gate', 'w_up', 'w_down')}
    del _L0_ffn_all

    def _L1_xattn_setup():
        import jax, jax.numpy as jnp
        import numpy as np
        import math
        H = 256
        NH = 16
        HD = H // NH
        EPS_LN = 1e-05
        RES_SCALE_MAX = 0.3

        def _nan_clean(x, lim=10000.0):
            return jnp.nan_to_num(x, nan=0.0, posinf=lim, neginf=-lim)
        key = jax.random.key(seed)
        ks = jax.random.split(key, 12)
        B, S, T = (4, 256, 32)
        std = 1.0 / math.sqrt(H)
        return {'hidden_states': jax.random.normal(ks[0], (B, S, H), jnp.float32), 'audio_tokens': jax.random.normal(ks[1], (B, T, H), jnp.float32), 'attention_mask': jax.random.randint(ks[2], (B, T), 0, 2, jnp.int32), 'Wq': jax.random.normal(ks[3], (H, H), jnp.float32) * std, 'bq': jnp.zeros((H,), jnp.float32), 'Wk': jax.random.normal(ks[4], (H, H), jnp.float32) * std, 'bk': jnp.zeros((H,), jnp.float32), 'Wv': jax.random.normal(ks[5], (H, H), jnp.float32) * std, 'bv': jnp.zeros((H,), jnp.float32), 'Wo': jax.random.normal(ks[6], (H, H), jnp.float32) * std, 'bo': jnp.zeros((H,), jnp.float32), 'ln_gamma': jnp.ones((H,), jnp.float32), 'ln_beta': jnp.zeros((H,), jnp.float32), 'residual_scale': jnp.float32(0.05)}
    _L1_xattn_all = _L1_xattn_setup()
    _L1_xattn_in = {k: v for k, v in _L1_xattn_all.items() if k in ('Wq', 'bq', 'Wk', 'bk', 'Wv', 'bv', 'Wo', 'bo', 'ln_gamma', 'ln_beta', 'residual_scale')}
    del _L1_xattn_all

    def _L1_ffn_setup():
        import jax, jax.numpy as jnp
        import numpy as np
        D_MODEL = 256
        D_HIDDEN = 176
        NUM_SHARED = 2
        NUM_ROUTED = 32
        TOP_K = 6

        def _expert_apply(xf, w1, b1, w2, b2):
            return jnp.maximum(xf @ w1 + b1, 0.0) @ w2 + b2
        key = jax.random.key(seed)
        ks = jax.random.split(key, 11)
        d, h = (D_MODEL, D_HIDDEN)
        s1 = 1.0 / np.sqrt(d)
        s2 = 1.0 / np.sqrt(h)
        x = jax.random.normal(ks[0], (2, 256, d), dtype=jnp.float32)
        sw1 = jax.random.uniform(ks[1], (NUM_SHARED, d, h), jnp.float32, -s1, s1)
        sb1 = jax.random.uniform(ks[2], (NUM_SHARED, h), jnp.float32, -s1, s1)
        sw2 = jax.random.uniform(ks[3], (NUM_SHARED, h, d), jnp.float32, -s2, s2)
        sb2 = jax.random.uniform(ks[4], (NUM_SHARED, d), jnp.float32, -s2, s2)
        rw1 = jax.random.uniform(ks[5], (NUM_ROUTED, d, h), jnp.float32, -s1, s1)
        rb1 = jax.random.uniform(ks[6], (NUM_ROUTED, h), jnp.float32, -s1, s1)
        rw2 = jax.random.uniform(ks[7], (NUM_ROUTED, h, d), jnp.float32, -s2, s2)
        rb2 = jax.random.uniform(ks[8], (NUM_ROUTED, d), jnp.float32, -s2, s2)
        router_w = jax.random.uniform(ks[9], (d, NUM_ROUTED), jnp.float32, -s1, s1)
        router_b = jax.random.uniform(ks[10], (NUM_ROUTED,), jnp.float32, -s1, s1)
        return {'x': x, 'sw1': sw1, 'sb1': sb1, 'sw2': sw2, 'sb2': sb2, 'rw1': rw1, 'rb1': rb1, 'rw2': rw2, 'rb2': rb2, 'router_w': router_w, 'router_b': router_b}
    _L1_ffn_all = _L1_ffn_setup()
    _L1_ffn_in = {k: v for k, v in _L1_ffn_all.items() if k in ('sw1', 'sb1', 'sw2', 'sb2', 'rw1', 'rb1', 'rw2', 'rb2', 'router_w', 'router_b')}
    del _L1_ffn_all
    return {'x': x, 'ctx_2048': ctx_2048, 'mask_1xSxS2_ff0': mask_1xSxS2_ff0, 'mask_BxS2_ik0': mask_BxS2_ik0, 'g_xattn': g_xattn, 'g_ffn': g_ffn, 'L0_xattn_Wq': _L0_xattn_in['Wq'], 'L0_xattn_bq': _L0_xattn_in['bq'], 'L0_xattn_Wk': _L0_xattn_in['Wk'], 'L0_xattn_bk': _L0_xattn_in['bk'], 'L0_xattn_Wv': _L0_xattn_in['Wv'], 'L0_xattn_bv': _L0_xattn_in['bv'], 'L0_xattn_Wo': _L0_xattn_in['Wo'], 'L0_xattn_qn_w': _L0_xattn_in['qn_w'], 'L0_xattn_kn_w': _L0_xattn_in['kn_w'], 'L0_ffn_w_gate': _L0_ffn_in['w_gate'], 'L0_ffn_w_up': _L0_ffn_in['w_up'], 'L0_ffn_w_down': _L0_ffn_in['w_down'], 'L1_xattn_Wq': _L1_xattn_in['Wq'], 'L1_xattn_bq': _L1_xattn_in['bq'], 'L1_xattn_Wk': _L1_xattn_in['Wk'], 'L1_xattn_bk': _L1_xattn_in['bk'], 'L1_xattn_Wv': _L1_xattn_in['Wv'], 'L1_xattn_bv': _L1_xattn_in['bv'], 'L1_xattn_Wo': _L1_xattn_in['Wo'], 'L1_xattn_bo': _L1_xattn_in['bo'], 'L1_xattn_ln_gamma': _L1_xattn_in['ln_gamma'], 'L1_xattn_ln_beta': _L1_xattn_in['ln_beta'], 'L1_xattn_residual_scale': _L1_xattn_in['residual_scale'], 'L1_ffn_sw1': _L1_ffn_in['sw1'], 'L1_ffn_sb1': _L1_ffn_in['sb1'], 'L1_ffn_sw2': _L1_ffn_in['sw2'], 'L1_ffn_sb2': _L1_ffn_in['sb2'], 'L1_ffn_rw1': _L1_ffn_in['rw1'], 'L1_ffn_rb1': _L1_ffn_in['rb1'], 'L1_ffn_rw2': _L1_ffn_in['rw2'], 'L1_ffn_rb2': _L1_ffn_in['rb2'], 'L1_ffn_router_w': _L1_ffn_in['router_w'], 'L1_ffn_router_b': _L1_ffn_in['router_b']}

def reference(x, ctx_2048, mask_1xSxS2_ff0, mask_BxS2_ik0, g_xattn, g_ffn, L0_xattn_Wq, L0_xattn_bq, L0_xattn_Wk, L0_xattn_bk, L0_xattn_Wv, L0_xattn_bv, L0_xattn_Wo, L0_xattn_qn_w, L0_xattn_kn_w, L0_ffn_w_gate, L0_ffn_w_up, L0_ffn_w_down, L1_xattn_Wq, L1_xattn_bq, L1_xattn_Wk, L1_xattn_bk, L1_xattn_Wv, L1_xattn_bv, L1_xattn_Wo, L1_xattn_bo, L1_xattn_ln_gamma, L1_xattn_ln_beta, L1_xattn_residual_scale, L1_ffn_sw1, L1_ffn_sb1, L1_ffn_sw2, L1_ffn_sb2, L1_ffn_rw1, L1_ffn_rb1, L1_ffn_rw2, L1_ffn_rb2, L1_ffn_router_w, L1_ffn_router_b):
    import jax
    import jax.numpy as jnp

    def _L0_xattn_ref(hidden_states, encoder_hidden_states, attention_mask, Wq, bq, Wk, bk, Wv, bv, Wo, qn_w, kn_w):
        import jax, jax.numpy as jnp
        import numpy as np
        H = 256
        NH = 16
        NKV = 4
        HD = 128
        GROUPS = NH // NKV
        EPS = 1e-06
        B, S, SE = (1, 256, 512)

        def _rmsnorm(x, w, eps=EPS):
            xf = x.astype(jnp.float32)
            var = jnp.mean(xf * xf, axis=-1, keepdims=True)
            return (xf * jax.lax.rsqrt(var + eps)).astype(x.dtype) * w
        b, s, _ = hidden_states.shape
        se = encoder_hidden_states.shape[1]
        q = (hidden_states @ Wq + bq).reshape(b, s, NH, HD).transpose(0, 2, 1, 3)
        k = (encoder_hidden_states @ Wk + bk).reshape(b, se, NKV, HD).transpose(0, 2, 1, 3)
        v = (encoder_hidden_states @ Wv + bv).reshape(b, se, NKV, HD).transpose(0, 2, 1, 3)
        k = jnp.repeat(k, GROUPS, axis=1)
        v = jnp.repeat(v, GROUPS, axis=1)
        q = _rmsnorm(q, qn_w)
        k = _rmsnorm(k, kn_w)
        scale = 1.0 / np.sqrt(HD).astype(np.float32)
        scores = jnp.einsum('bhsd,bhed->bhse', q, k) * scale
        scores = scores + attention_mask[:, None, :, :]
        probs = jax.nn.softmax(scores.astype(jnp.float32), axis=-1).astype(q.dtype)
        out = jnp.einsum('bhse,bhed->bhsd', probs, v)
        out = out.transpose(0, 2, 1, 3).reshape(b, s, NH * HD)
        return out @ Wo

    def _L0_ffn_ref(x, w_gate, w_up, w_down):
        import jax, jax.numpy as jnp
        import numpy as np
        ACT_BITS = 8
        EPS = 1e-05

        def act_quant(x, bits=ACT_BITS):
            qb = float(2 ** (bits - 1))
            scale = qb / jnp.clip(jnp.max(jnp.abs(x), axis=-1, keepdims=True), EPS)
            xq = jnp.clip(jnp.round(x * scale), -qb, qb - 1) / scale
            return x + jax.lax.stop_gradient(xq - x)

        def weight_quant(w):
            scale = 1.0 / jnp.clip(jnp.mean(jnp.abs(w)), EPS)
            wq = jnp.clip(jnp.round(w * scale), -1.0, 1.0) / scale
            return w + jax.lax.stop_gradient(wq - w)

        def fwht(x):
            shape = x.shape
            n = shape[-1]
            x = x.reshape(-1, n)
            h = 1
            while h < n:
                x = x.reshape(-1, n // (2 * h), 2, h)
                a, b = (x[..., 0, :], x[..., 1, :])
                x = jnp.stack([a + b, a - b], axis=-2).reshape(-1, n)
                h *= 2
            return (x * (1.0 / np.sqrt(n)).astype(np.float32)).reshape(shape)

        def bitlinear(x, w):
            return jnp.einsum('bsh,oh->bso', act_quant(x), weight_quant(w))

        def h_bitlinear(x, w):
            return jnp.einsum('bsh,oh->bso', act_quant(fwht(x)), weight_quant(w))
        gate = bitlinear(x, w_gate)
        up = bitlinear(x, w_up)
        intermediate = jax.nn.silu(gate) * up
        return h_bitlinear(intermediate, w_down)

    def _L1_xattn_ref(hidden_states, audio_tokens, attention_mask, Wq, bq, Wk, bk, Wv, bv, Wo, bo, ln_gamma, ln_beta, residual_scale):
        import jax, jax.numpy as jnp
        import numpy as np
        import math
        H = 256
        NH = 16
        HD = H // NH
        EPS_LN = 1e-05
        RES_SCALE_MAX = 0.3

        def _nan_clean(x, lim=10000.0):
            return jnp.nan_to_num(x, nan=0.0, posinf=lim, neginf=-lim)
        B, S, _ = hidden_states.shape
        T = audio_tokens.shape[1]
        hs = _nan_clean(hidden_states).astype(jnp.float32)
        at = _nan_clean(audio_tokens).astype(jnp.float32)

        def proj(x, W, b, L):
            y = x @ W.T + b
            return y.reshape(B, L, NH, HD).transpose(0, 2, 1, 3)
        q = _nan_clean(proj(hs, Wq, bq, S))
        k = _nan_clean(proj(at, Wk, bk, T))
        v = _nan_clean(proj(at, Wv, bv, T))
        scale = max(math.sqrt(HD), 1e-08)
        scores = jnp.einsum('bhsd,bhtd->bhst', q, k) / scale
        scores = jnp.clip(scores, -50.0, 50.0)
        scores = jnp.nan_to_num(scores, nan=0.0, posinf=50.0, neginf=-50.0)
        attend = (attention_mask.astype(jnp.float32) > 0.5)[:, None, None, :]
        scores = jnp.where(attend, scores, -10000.0)
        scores = jnp.clip(scores, -50.0, 50.0)
        probs = jax.nn.softmax(scores, axis=-1)
        probs = jnp.nan_to_num(probs, nan=0.0, posinf=1.0, neginf=0.0)
        probs = probs / (probs.sum(axis=-1, keepdims=True) + 1e-08)
        ctx = jnp.einsum('bhst,bhtd->bhsd', probs, v)
        ctx = ctx.transpose(0, 2, 1, 3).reshape(B, S, H)
        delta = _nan_clean(ctx @ Wo.T + bo)
        rs = jnp.clip(residual_scale, 0.0, RES_SCALE_MAX)
        delta = rs * delta
        mu = delta.mean(axis=-1, keepdims=True)
        var = jnp.mean((delta - mu) ** 2, axis=-1, keepdims=True)
        delta = (delta - mu) / jnp.sqrt(var + EPS_LN) * ln_gamma + ln_beta
        return delta

    def _L1_ffn_ref(x, sw1, sb1, sw2, sb2, rw1, rb1, rw2, rb2, router_w, router_b):
        import jax, jax.numpy as jnp
        import numpy as np
        D_MODEL = 256
        D_HIDDEN = 176
        NUM_SHARED = 2
        NUM_ROUTED = 32
        TOP_K = 6

        def _expert_apply(xf, w1, b1, w2, b2):
            return jnp.maximum(xf @ w1 + b1, 0.0) @ w2 + b2
        B, S, d = x.shape
        flat = x.reshape(-1, d)
        T = flat.shape[0]

        def sh_body(acc, p):
            w1, b1, w2, b2 = p
            return (acc + _expert_apply(flat, w1, b1, w2, b2), None)
        shared_out, _ = jax.lax.scan(sh_body, jnp.zeros_like(flat), (sw1, sb1, sw2, sb2))
        shared_out = shared_out / NUM_SHARED
        logits = flat @ router_w + router_b
        probs = jax.nn.softmax(logits, axis=-1)
        topk_p, topk_i = jax.lax.top_k(probs, TOP_K)
        topk_p = topk_p / jnp.sum(topk_p, axis=-1, keepdims=True)
        gates = jnp.zeros((T, NUM_ROUTED), dtype=flat.dtype)
        gates = gates.at[jnp.arange(T)[:, None], topk_i].add(topk_p)

        def r_body(acc, p):
            w1, b1, w2, b2, g = p
            return (acc + g[:, None] * _expert_apply(flat, w1, b1, w2, b2), None)
        routed_out, _ = jax.lax.scan(r_body, jnp.zeros_like(flat), (rw1, rb1, rw2, rb2, gates.T))
        return (shared_out + routed_out).reshape(B, S, d)
    x = x + jnp.tanh(g_xattn[0]) * _L0_xattn_ref(_layernorm(x, axis=-1), ctx_2048, mask_1xSxS2_ff0, L0_xattn_Wq, L0_xattn_bq, L0_xattn_Wk, L0_xattn_bk, L0_xattn_Wv, L0_xattn_bv, L0_xattn_Wo, L0_xattn_qn_w, L0_xattn_kn_w)
    x = x + jnp.tanh(g_ffn[0]) * _L0_ffn_ref(_layernorm(x, axis=-1), L0_ffn_w_gate, L0_ffn_w_up, L0_ffn_w_down)
    x = x + jnp.tanh(g_xattn[1]) * _L1_xattn_ref(_layernorm(x, axis=-1), ctx_2048, mask_BxS2_ik0, L1_xattn_Wq, L1_xattn_bq, L1_xattn_Wk, L1_xattn_bk, L1_xattn_Wv, L1_xattn_bv, L1_xattn_Wo, L1_xattn_bo, L1_xattn_ln_gamma, L1_xattn_ln_beta, L1_xattn_residual_scale)
    x = x + jnp.tanh(g_ffn[1]) * _L1_ffn_ref(_layernorm(x, axis=-1), L1_ffn_sw1, L1_ffn_sb1, L1_ffn_sw2, L1_ffn_sb2, L1_ffn_rw1, L1_ffn_rb1, L1_ffn_rw2, L1_ffn_rb2, L1_ffn_router_w, L1_ffn_router_b)
    return x

_drawn_inputs = setup_inputs


def setup_inputs(seed=0):
    import zlib

    import numpy as np

    out = dict(_drawn_inputs(seed))
    spreads = {'g_ffn': (-1.0, 0.6),
     'L0_xattn_qn_w': (1.0, 0.6),
     'L0_xattn_kn_w': (1.0, 0.6),
     'L1_xattn_bq': (0.0, 0.271),
     'L1_xattn_bk': (0.0, 0.8),
     'L1_xattn_bv': (0.0, 0.1),
     'L1_xattn_bo': (0.0, 0.1),
     'L1_xattn_ln_gamma': (1.0, 0.2),
     'L1_xattn_ln_beta': (0.0, 0.1)}
    factors = {'L0_xattn_bq': 8.0,
     'L0_xattn_bk': 8.0,
     'L0_xattn_bv': 4.94,
     'L1_ffn_sb1': 8.0,
     'L1_ffn_sb2': 3.557,
     'L1_ffn_rb1': 8.0,
     'L1_ffn_rb2': 5.253,
     'L1_ffn_router_b': 5.154}
    for name, (base, spread) in spreads.items():
        noise = np.random.default_rng([zlib.crc32(name.encode()), seed]).standard_normal(out[name].shape)
        drawn = base * np.exp(spread * noise) if base else spread * noise
        out[name] = jnp.asarray(drawn.astype(out[name].dtype))
    for name, factor in factors.items():
        out[name] = (out[name] * factor).astype(out[name].dtype)
    return out
```

```python
import math
from contextlib import ExitStack

import concourse.bass as bass
from concourse import mybir

ALU = mybir.AluOpType
ACT = mybir.ActivationFunctionType
AX = mybir.AxisListType
F32 = mybir.dt.float32
F32R = mybir.dt.float32r
BF16 = mybir.dt.bfloat16
I32 = mybir.dt.int32

B, S, H = 8, 56, 256
S2 = 1500
T = B * S
P = 128
KC = H // P
TT = 2 * S
NT = T // TT
CH = 125
NC = S2 // CH
PIECES = 4
CPP = NC // PIECES
PW = CPP * CH
NH, NKV, HD = 16, 4, 128
QG = NH // NKV * S
SB = 500
NSB = S2 // SB
F0 = 1024
FC0 = F0 // P
H1, D1 = 16, 16
HPG = 4
NG1 = H1 // HPG
GW = HPG * D1
BIG = 1.5 * 2.0 ** 23
E_LO, E_HI = math.exp(-50.0), math.exp(50.0)


def wait_for(eng, sem, value):
    if isinstance(value, int) and value <= 0:
        return
    eng.wait_ge(sem, value)


class Chain:

    def __init__(self, eng, sem, base=0):
        self.eng, self.sem, self.base, self.n = eng, sem, base, 0

    def link(self, ins):
        ins.then_inc(self.sem, 1)
        self.n += 1
        self.eng.wait_ge(self.sem, self.base + self.n)


def query_phase(nc, sem, keep, x_in, wq_in, bq_in, qw_in, kw_in, ident_in, q_scratch):
    with ExitStack() as ctx:
        sb = lambda name, shape, dt=F32: ctx.enter_context(nc.sbuf_tensor(name, shape, dt))
        x, ident, mhalf = keep["x"], keep["ident"], keep["mhalf"]
        wq = sb("wq", [P, KC, NH * HD])
        bq = sb("bq", [TT, NH * HD])
        qw = sb("qw", [P, 1])
        kw = sb("kw", [P, 1])
        qkw = sb("qkw", [P, 1])
        stats = sb("qa_stats", [TT, NT, 6])
        mv = sb("qa_mv", [TT, NT, 2])
        var = sb("qa_var", [TT, NT])
        rstd = sb("qa_rstd", [TT, NT])
        xn = sb("qa_xn", [TT, NT, H])
        xnT = sb("qa_xnT", [P, KC, T])
        q = sb("qa_q", [TT, NT, NH * HD])
        sq = sb("qa_sq", [TT, 2, 512])
        ssq = sb("qa_ssq", [TT, NT, NH])
        qvar = sb("qa_qvar", [TT, NT, NH])
        qr = sb("qa_qr", [TT, NT, NH])
        qT = sb("qa_qT", [P, 2, 2, NH, S])
        ps = [ctx.enter_context(nc.psum_tensor(f"qa_ps{i}", [P, 512], F32)) for i in range(8)]
        loaded_x, loaded_id, loaded_w, loaded_b, loaded_n = (sem(n) for n in (
            "a_x_loaded", "a_ident_loaded", "a_wq_loaded", "a_bq_loaded", "a_norm_w_loaded"))
        dve_chain, var_ready, rstd_ready, xn_ready, xt_done, xt_copied = (sem(n) for n in (
            "a_dve_chain", "a_var_ready", "a_rstd_ready", "a_xn_ready", "a_xT_done", "a_xT_copied"))
        q_done, q_biased, q_squared, sq_reduced, qvar_ready, qr_ready, q_scaled = (sem(n) for n in (
            "a_q_done", "a_q_biased", "a_q_squared", "a_sq_reduced", "a_qvar_ready", "a_qr_ready", "a_q_scaled"))
        qt_done, qt_copied, mhalf_set = (sem(n) for n in ("a_qT_done", "a_qT_copied", "a_mhalf_set"))
        stored = [sem(f"a_qT_stored{i}") for i in range(2)]
        block = ctx.enter_context(nc.Block())

        @block.sync
        def _(sp):
            sp.dma_start(x[:, :, :], x_in.rearrange("(t p) h -> p t h", p=TT)).then_inc(loaded_x, 16)
            sp.dma_start(ident[:, :], ident_in).then_inc(loaded_id, 16)
            sp.dma_start(wq[:, :, :], wq_in.rearrange("(c p) n -> p c n", p=P)).then_inc(loaded_w, 16)
            sp.dma_start(bq[:, :], bq_in.partition_broadcast(TT)).then_inc(loaded_b, 16)
            sp.dma_start(qw[:, :], qw_in).then_inc(loaded_n, 16)
            sp.dma_start(kw[:, :], kw_in).then_inc(loaded_n, 16)
            for t in range(NT):
                sp.wait_ge(qt_copied, 4 * (t + 1))
                sp.dma_start(q_scratch[2 * t:2 * t + 2].rearrange("b p h s -> p b (h s)"),
                             qT[:, t % 2].rearrange("p b h s -> p b (h s)")).then_inc(stored[t % 2], 16)
            for i in range(2):
                sp.wait_ge(stored[i], 16 * (NT // 2))

        @block.gpsimd
        def _(pool):
            pool.memset(mhalf[:, :], -0.5).then_inc(mhalf_set, 1)
            pool.wait_ge(mhalf_set, 1)
            pool.wait_ge(var_ready, 1)
            pool.tensor_tensor(rstd[:, :], var[:, :], mhalf[:TT, 0:NT], ALU.pow).then_inc(rstd_ready, 1)
            for t in range(NT):
                pool.wait_ge(qvar_ready, t + 1)
                pool.tensor_tensor(qr[:, t, :], qvar[:, t, :], mhalf[:TT, 0:NH], ALU.pow).then_inc(qr_ready, 1)

        @block.scalar
        def _(act):
            for t in range(NT):
                act.wait_ge(xt_done, t + 1)
                act.copy(xnT[:, :, t * TT:(t + 1) * TT],
                         ps[t % 2][:, 0:KC * TT].rearrange("p (c s) -> p c s", c=KC)).then_inc(xt_copied, 1)
            for t in range(NT):
                for n in range(4):
                    k = 4 * t + n
                    act.wait_ge(q_biased, k + 1)
                    wait_for(act, sq_reduced, k - 1)
                    act.activation(sq[:, k % 2, :], q[:, t, n * 512:(n + 1) * 512], ACT.Square).then_inc(q_squared, 1)

        @block.tensor
        def _(pe):
            pe.wait_ge(loaded_id, 16)
            for t in range(NT):
                pe.wait_ge(xn_ready, t + 1)
                wait_for(pe, xt_copied, t - 1)
                for c in range(KC):
                    mm = pe.transpose(ps[t % 2][:, c * TT:(c + 1) * TT], xn[:, t, c * P:(c + 1) * P],
                                      ident[:TT, :TT])
                mm.then_inc(xt_done, 1)
            pe.wait_ge(loaded_w, 16)

            def heads_to_columns(t):
                pe.wait_ge(q_scaled, t + 1)
                for n in range(4):
                    k = 4 * t + n
                    wait_for(pe, qt_copied, k - 1)
                    for j in range(4):
                        h = 4 * n + j
                        mm = pe.transpose(ps[6 + k % 2][:, j * TT:(j + 1) * TT],
                                          q[:, t, h * HD:(h + 1) * HD], ident[:TT, :TT])
                    mm.then_inc(qt_done, 1)

            for t in range(NT):
                pe.wait_ge(xt_copied, t + 1)
                for n in range(4):
                    k = 4 * t + n
                    wait_for(pe, q_biased, k - 3)
                    for c in range(KC):
                        mm = pe.matmul(ps[2 + n][:TT, :], xnT[:, c, t * TT:(t + 1) * TT],
                                       wq[:, c, n * 512:(n + 1) * 512], start=c == 0, stop=c == KC - 1)
                    mm.then_inc(q_done, 1)
                if t:
                    heads_to_columns(t - 1)
            heads_to_columns(NT - 1)

        @block.vector
        def _(dve):
            ch = Chain(dve, dve_chain)
            dve.wait_ge(loaded_x, 16)
            for t in range(NT):
                last = dve.bn_stats(stats[:, t, :], x[:, t, :])
            ch.link(last)
            for t in range(NT):
                last = dve.bn_aggr(mv[:, t, :], stats[:, t, :])
            ch.link(last)
            dve.tensor_scalar(var[:, :], mv[:, :, 1], 1e-5, None, ALU.add).then_inc(var_ready, 1)
            dve.wait_ge(rstd_ready, 1)
            for t in range(NT):
                dve.tensor_scalar(xn[:, t, :], x[:, t, :], mv[:, t, 0:1], rstd[:, t:t + 1],
                                  ALU.subtract, ALU.mult).then_inc(xn_ready, 1)
            dve.wait_ge(loaded_n, 32)
            ch.link(dve.scalar_tensor_tensor(out=qkw[:, :], in0=qw[:, :], scalar=float(HD) ** -0.5, in1=kw[:, :],
                                             op0=ALU.mult, op1=ALU.mult))
            dve.wait_ge(loaded_b, 16)

            def columns_out(t):
                for n in range(4):
                    k = 4 * t + n
                    dve.wait_ge(qt_done, k + 1)
                    if t >= 2 and n == 0:
                        dve.wait_ge(stored[t % 2], 16 * (t // 2))
                    for bb in range(2):
                        src = ps[6 + k % 2][:, 0:4 * TT].rearrange("p (h b s) -> p b h s", h=4, b=2)[:, bb]
                        last = dve.tensor_scalar(qT[:, t % 2, bb, 4 * n:4 * n + 4, :], src, qkw[:, 0:1], None, ALU.mult)
                    last.then_inc(qt_copied, 1)

            for t in range(NT):
                for n in range(4):
                    k = 4 * t + n
                    dve.wait_ge(q_done, k + 1)
                    dve.tensor_tensor(q[:, t, n * 512:(n + 1) * 512], ps[2 + n][:TT, :],
                                      bq[:, n * 512:(n + 1) * 512], ALU.add).then_inc(q_biased, 1)
                for n in range(4):
                    k = 4 * t + n
                    dve.wait_ge(q_squared, k + 1)
                    dve.tensor_reduce(ssq[:, t, 4 * n:4 * n + 4],
                                      sq[:, k % 2, :].rearrange("p (h d) -> p h d", h=4),
                                      AX.X, ALU.add).then_inc(sq_reduced, 1)
                dve.wait_ge(sq_reduced, 4 * t + 4)
                dve.tensor_scalar(qvar[:, t, :], ssq[:, t, :], 1.0 / HD, 1e-6, ALU.mult, ALU.add).then_inc(qvar_ready, 1)
                if t:
                    columns_out(t - 1)
                dve.wait_ge(qr_ready, t + 1)
                heads = q[:, t, :].rearrange("p (h d) -> p h d", h=NH)
                dve.tensor_tensor(heads, heads, qr[:, t, :].unsqueeze(2).broadcast_to([TT, NH, HD]),
                                  ALU.mult).then_inc(q_scaled, 1)
            columns_out(NT - 1)


def attention0_phase(nc, sem, keep, ctx_in, mask_in, wk_in, bk_in, wv_in, bv_in, q_scratch, o_scratch):
    with ExitStack() as ctx:
        sb = lambda name, shape, dt=F32: ctx.enter_context(nc.sbuf_tensor(name, shape, dt))
        ident, mhalf = keep["ident"], keep["mhalf"]
        wkv = sb("b_wkv", [P, KC, 2, 512])
        whi = sb("b_whi", [P, KC, 2, 512], F32R)
        wlo = sb("b_wlo", [P, KC, 2, 512], F32R)
        bk = sb("b_bk", [CH, 512])
        bv = sb("b_bv", [P, NKV])
        mask = sb("b_mask", [TT, S2])
        raw = sb("b_ctx", [P, 2, KC, PW])
        chi = sb("b_ctx_hi", [P, 2, KC, PW], F32R)
        clo = sb("b_ctx_lo", [P, 2, KC, PW], F32R)
        ktok = sb("b_k_tok", [CH, 2, CPP, 512])
        ksq = sb("b_k_sq", [CH, 2, 512])
        kss = sb("b_k_ss", [CH, 2, CPP, NKV])
        kvar = sb("b_k_var", [CH, 2, CPP, NKV])
        kr = sb("b_k_r", [CH, 2, CPP, NKV])
        kT = [sb(f"b_kT{i}", [P, NKV, S2]) for i in range(2)]
        V = [sb(f"b_v{i}", [CH, NC, 512]) for i in range(2)]
        probs = [sb(f"b_probs{i}", [TT, S2]) for i in range(4)]
        pT = [sb(f"b_probsT{i}", [CH, 2, QG]) for i in range(2)]
        fence = sb("b_fence", [TT, 2 * NSB * PIECES])
        mx = sb("b_max", [TT, 2, 2, NSB])
        nmx = sb("b_neg_max", [TT, 2, 2])
        rs = sb("b_row_sum", [TT, 2, 2])
        rr = sb("b_row_recip", [TT, 2, 2])
        qcur = [sb(f"b_q{i}", [P, NH * S]) for i in range(2)]
        oT = sb("b_oT", [P, NH, 2, S])
        bank = lambda name: ctx.enter_context(nc.psum_tensor(name, [P, 512], F32))
        ps_s = [bank(f"b_ps_scores{i}") for i in range(2)]
        ps_k, ps_v = bank("b_ps_k"), bank("b_ps_v")
        ps_t = [bank(f"b_ps_T{i}") for i in range(2)]
        ps_o = [bank(f"b_ps_o{i}") for i in range(2)]
        w_loaded, misc_loaded, w_hi, w_lo = (sem(n) for n in ("b_w_loaded", "b_misc_loaded", "b_w_hi", "b_w_lo"))
        ctx_loaded = [sem(f"b_ctx_loaded{i}") for i in range(2)]
        q_loaded = [sem(f"b_q_loaded{i}") for i in range(2)]
        o_writable = sem("b_o_writable")
        ctx_hi, ctx_lo, k_done, v_done, k_biased, v_copied, k_squared, k_reduced = (sem(n) for n in (
            "b_ctx_hi", "b_ctx_lo", "b_k_done", "b_v_done", "b_k_biased", "b_v_copied", "b_k_squared", "b_k_reduced"))
        kvar_ready, kr_ready, k_scaled, kt_done, kt_copied = (sem(n) for n in (
            "b_kvar_ready", "b_kr_ready", "b_k_scaled", "b_kT_done", "b_kT_copied"))
        s_done, s_masked, max_ready, exp_done, recip_ready, p_ready, pt_done, pt_copied, o_done, o_copied = (
            sem(n) for n in ("b_scores_done", "b_scores_masked", "b_max_ready", "b_exp_done", "b_recip_ready",
                             "b_probs_ready", "b_pT_done", "b_pT_copied", "b_o_done", "b_o_copied"))
        block = ctx.enter_context(nc.Block())
        G = range(PIECES)

        def batches(eng, attend, project):
            project(0)
            with eng.Fori(0, B // 2 - 1) as i:
                for par in range(2):
                    attend(i * 2 + par, par, False, i)
            for par in range(2):
                attend(B - 2 + par, par, par == 1, B // 2 - 1)

        @block.sync
        def _(sp):
            sp.dma_start(wkv[:, :, 0, :], wk_in.rearrange("(c p) n -> p c n", p=P)).then_inc(w_loaded, 16)
            sp.dma_start(wkv[:, :, 1, :], wv_in.rearrange("(c p) n -> p c n", p=P)).then_inc(w_loaded, 16)

            def load(b, par):
                for g in G:
                    wait_for(sp, ctx_lo, 4 * b + g - 1)
                    sp.dma_start(raw[:, g % 2, :, :],
                                 ctx_in[b, :, g * PW:(g + 1) * PW].rearrange("(c p) s -> p c s", p=P)
                                 ).then_inc(ctx_loaded[g % 2], 16)

            def load_queries(b, par):
                sp.dma_start(qcur[par][:, :], q_scratch[b].rearrange("p h s -> p (h s)")).then_inc(q_loaded[par], 16)

            def project(_):
                sp.dma_start(bk[:, :], bk_in.partition_broadcast(CH)).then_inc(misc_loaded, 16)
                sp.dma_start(bv[:, :], bv_in).then_inc(o_writable, 16)
                for j in range(2):
                    sp.dma_start(mask[j * S:(j + 1) * S, :], mask_in).then_inc(misc_loaded, 16)
                load_queries(0, 0)
                load(0, 0)

            def attend(b, par, last, pair):
                if not last:
                    load(b + 1, 1 - par)
                    sp.wait_ge(s_done, b * 24 + 1)
                    load_queries(b + 1, 1 - par)
                if par == 1:
                    sp.wait_ge(o_copied, b * 4 + 4)
                    sp.dma_start(o_scratch[pair], oT[:, :, :, :].rearrange("p h b s -> p (h b s)")).then_inc(o_writable, 16)

            batches(sp, attend, project)
            sp.wait_ge(o_writable, 16 * (NT + 1))

        @block.gpsimd
        def _(pool):
            def normalise_keys(b, g):
                n = b * 4 + g
                pool.wait_ge(kvar_ready, n + 1)
                pool.tensor_tensor(kr[:, g % 2].rearrange("p c g -> p (c g)"),
                                   kvar[:, g % 2].rearrange("p c g -> p (c g)"),
                                   mhalf[:CH, 0:CPP * NKV], ALU.pow).then_inc(kr_ready, 1)
                pool.wait_ge(kr_ready, n + 1)
                for c in range(CPP):
                    heads = ktok[:, g % 2, c, :].rearrange("p (g d) -> p g d", g=NKV)
                    pool.tensor_tensor(heads, heads, kr[:, g % 2, c, :].unsqueeze(2).broadcast_to([CH, NKV, HD]),
                                       ALU.mult).then_inc(k_scaled, 1)

            def attend(b, par, last, pair):
                for g in G:
                    if not last:
                        normalise_keys(b + 1, g)

            batches(pool, attend, lambda _: [normalise_keys(0, g) for g in G])

        @block.scalar
        def _(act):
            act.wait_ge(w_loaded, 32)
            act.copy(whi[:, :, :, :], wkv[:, :, :, :]).then_inc(w_hi, 1)

            def split(b, g):
                act.wait_ge(ctx_loaded[g % 2], b * 32 + 16 * (g // 2 + 1))
                wait_for(act, v_done, (b * 4 + g - 1) * CPP)
                act.copy(chi[:, g % 2, :, :], raw[:, g % 2, :, :]).then_inc(ctx_hi, 1)

            def project(b, g, par):
                for c in range(CPP):
                    n = b * NC + g * CPP + c
                    act.wait_ge(k_biased, n + 1)
                    wait_for(act, k_reduced, n - 1)
                    act.activation(ksq[:, (g * CPP + c) % 2, :], ktok[:, g % 2, c, :], ACT.Square).then_inc(k_squared, 1)
                    act.wait_ge(v_done, n + 1)
                    act.copy(V[par][:, g * CPP + c, :], ps_v[:CH, :]).then_inc(v_copied, 1)

            def exps(b, g):
                for j in range(2):
                    n = b * 8 + 2 * g + j
                    act.wait_ge(max_ready, n + 1)
                    act.activation(probs[2 * (g % 2) + j][:, :], probs[2 * (g % 2) + j][:, :], ACT.Exp,
                                   bias=nmx[:, g % 2, j:j + 1], accum_out=rs[:, g % 2, j:j + 1]).then_inc(exp_done, 1)

            def probs_out(b, g):
                for r in range(NC // 2):
                    act.wait_ge(pt_done, b * 24 + g * 6 + r + 1)
                    act.copy(pT[r % 2][:, :, :], ps_t[r % 2][:CH, 0:2 * QG].rearrange("p (c q) -> p c q", c=2)
                             ).then_inc(pt_copied, 1)

            def first(_):
                for g in G:
                    split(0, g)
                    if g:
                        project(0, g - 1, 0)
                project(0, PIECES - 1, 0)

            def attend(b, par, last, pair):
                if not last:
                    split(b + 1, 0)
                exps(b, 0)
                if not last:
                    project(b + 1, 0, 1 - par)
                for g in range(1, PIECES):
                    if not last:
                        split(b + 1, g)
                    probs_out(b, g - 1)
                    exps(b, g)
                    if not last:
                        project(b + 1, g, 1 - par)
                probs_out(b, PIECES - 1)

            batches(act, attend, first)

        @block.tensor
        def _(pe):
            def project(b, g):
                pe.wait_ge(ctx_lo, b * 4 + g + 1)
                for c in range(CPP):
                    n = b * NC + g * CPP + c
                    for kv, bank_kv, freed, done in ((0, ps_k, k_biased, k_done), (1, ps_v, v_copied, v_done)):
                        wait_for(pe, freed, n)
                        m = 0
                        for kc in range(KC):
                            for a, w in ((chi, whi), (chi, wlo), (clo, whi)):
                                mm = pe.matmul(bank_kv[:CH, :], a[:, g % 2, kc, c * CH:(c + 1) * CH], w[:, kc, kv, :],
                                               start=m == 0, stop=m == 3 * KC - 1)
                                m += 1
                        mm.then_inc(done, 1)

            def keys_to_columns(b, g, probs_before):
                pe.wait_ge(k_scaled, (b * 4 + g + 1) * CPP)
                wait_for(pe, pt_copied, probs_before)
                for kv in range(NKV):
                    wait_for(pe, kt_copied, b * 16 + g * 4 + kv - 1)
                    for c in range(CPP):
                        mm = pe.transpose(ps_t[kv % 2][:, c * CH:(c + 1) * CH],
                                          ktok[:, g % 2, c, kv * HD:(kv + 1) * HD], ident[:CH, :CH])
                    mm.then_inc(kt_done, 1)

            def scores(b, g, par):
                for j in range(2):
                    for n in range(NSB):
                        m = 6 * g + 3 * j + n
                        if m >= 2:
                            pe.wait_ge(s_masked, b * 24 + m - 1)
                        pe.matmul(ps_s[m % 2][:TT, 0:SB], qcur[par][:, (2 * g + j) * TT:(2 * g + j + 1) * TT],
                                  kT[par][:, g, n * SB:(n + 1) * SB], start=True, stop=True).then_inc(s_done, 1)

            def values(b, g, par, keys_before):
                wait_for(pe, kt_copied, keys_before)
                pe.wait_ge(p_ready, b * 8 + 2 * g + 2)

                def product(r):
                    pe.wait_ge(pt_copied, b * 24 + g * 6 + r + 1)
                    for cc in range(2):
                        c = 2 * r + cc
                        mm = pe.matmul(ps_o[g % 2][:, 0:QG], V[par][:, c, g * HD:(g + 1) * HD], pT[r % 2][:, cc, :],
                                       start=c == 0, stop=c == NC - 1)
                    return mm

                for r in range(NC // 2):
                    if r >= 2:
                        product(r - 2)
                    for cc in range(2):
                        for j in range(2):
                            c = 2 * r + cc
                            mm = pe.transpose(ps_t[r % 2][:CH, cc * QG + j * TT:cc * QG + (j + 1) * TT],
                                              probs[2 * (g % 2) + j][:, c * CH:(c + 1) * CH], ident[:TT, :TT])
                    mm.then_inc(pt_done, 1)
                product(NC // 2 - 2)
                product(NC // 2 - 1).then_inc(o_done, 1)

            def first(_):
                pe.wait_ge(w_lo, 1)
                project(0, 0)
                for g in range(1, PIECES):
                    project(0, g)
                    keys_to_columns(0, g - 1, 0)
                keys_to_columns(0, PIECES - 1, 0)

            def attend(b, par, last, pair):
                pe.wait_ge(kt_copied, b * 16 + 16)
                pe.wait_ge(q_loaded[par], (b - par) * 8 + 16)
                pe.wait_ge(v_copied, b * NC + NC)
                scores(b, 0, par)
                if not last:
                    project(b + 1, 0)
                for g in range(1, PIECES):
                    scores(b, g, par)
                    values(b, g - 1, par, (b + 1) * 16 + (g - 1) * 4 if not last else 0)
                    if not last:
                        keys_to_columns(b + 1, g - 1, b * 24 + g * 6)
                        project(b + 1, g)
                values(b, PIECES - 1, par, (b + 1) * 16 + 12 if not last else 0)
                if not last:
                    keys_to_columns(b + 1, PIECES - 1, b * 24 + 24)

            batches(pe, attend, first)

        @block.vector
        def _(dve):
            dve.wait_ge(w_hi, 1)
            dve.tensor_tensor(wlo[:, :, :, :], wkv[:, :, :, :], whi.bitcast(F32)[:, :, :, :], ALU.subtract).then_inc(w_lo, 1)

            def split(b, g):
                dve.wait_ge(ctx_hi, b * 4 + g + 1)
                dve.tensor_tensor(clo[:, g % 2, :, :], raw[:, g % 2, :, :], chi.bitcast(F32)[:, g % 2, :, :],
                                  ALU.subtract).then_inc(ctx_lo, 1)

            def keys(b, g):
                def reduce(c):
                    n = b * NC + g * CPP + c
                    dve.wait_ge(k_squared, n + 1)
                    dve.tensor_reduce(kss[:, g % 2, c, :],
                                      ksq[:, (g * CPP + c) % 2, :].rearrange("p (g d) -> p g d", g=NKV),
                                      AX.X, ALU.add).then_inc(k_reduced, 1)

                for c in range(CPP):
                    n = b * NC + g * CPP + c
                    dve.wait_ge(k_done, n + 1)
                    dve.tensor_tensor(ktok[:, g % 2, c, :], ps_k[:CH, :], bk[:, :], ALU.add).then_inc(k_biased, 1)
                    if c:
                        reduce(c - 1)
                reduce(CPP - 1)
                dve.wait_ge(k_reduced, b * NC + (g + 1) * CPP)
                dve.tensor_scalar(kvar[:, g % 2], kss[:, g % 2], 1.0 / HD, 1e-6, ALU.mult, ALU.add).then_inc(kvar_ready, 1)

            def key_columns(b, g, par):
                for kv in range(NKV):
                    dve.wait_ge(kt_done, b * 16 + g * 4 + kv + 1)
                    dve.tensor_copy(kT[par][:, kv, g * PW:(g + 1) * PW], ps_t[kv % 2][:, 0:PW]).then_inc(kt_copied, 1)

            def masks(b, g):
                for j in range(2):
                    for n in range(NSB):
                        m = 6 * g + 3 * j + n
                        dve.wait_ge(s_done, b * 24 + m + 1)
                        dve.memset(fence[:, m:m + 1], 0.0)
                        dve.tensor_tensor_reduce(out=probs[2 * (g % 2) + j][:, n * SB:(n + 1) * SB],
                                                 in0=ps_s[m % 2][:TT, 0:SB], in1=mask[:, n * SB:(n + 1) * SB],
                                                 scale=1.0, scalar=-3.0e38, op0=ALU.add, op1=ALU.max,
                                                 accum_out=mx[:, g % 2, j, n:n + 1]).then_inc(s_masked, 1)
                    dve.wait_ge(s_masked, b * 24 + 6 * g + 3 * j + 3)
                    dve.tensor_reduce(nmx[:, g % 2, j:j + 1], mx[:, g % 2, j, :], AX.X, ALU.max,
                                      negate=True).then_inc(max_ready, 1)

            def normalise(b, g):
                for j in range(2):
                    n = b * 8 + 2 * g + j
                    dve.wait_ge(exp_done, n + 1)
                    dve.reciprocal(rr[:, g % 2, j:j + 1], rs[:, g % 2, j:j + 1]).then_inc(recip_ready, 1)
                    dve.wait_ge(recip_ready, n + 1)
                    p = probs[2 * (g % 2) + j]
                    dve.tensor_scalar(p[:, :], p[:, :], rr[:, g % 2, j:j + 1], None, ALU.mult).then_inc(p_ready, 1)

            def outputs(b, g, par):
                dve.wait_ge(o_done, b * 4 + g + 1)
                if g == 0 and par == 0:
                    dve.wait_ge(o_writable, b * 8 + 16)
                dve.tensor_scalar(oT[:, g * NH // NKV:(g + 1) * NH // NKV, par, :],
                                  ps_o[g % 2][:, 0:QG].rearrange("p (h s) -> p h s", s=S), bv[:, g:g + 1], None,
                                  ALU.add).then_inc(o_copied, 1)

            def first(_):
                split(0, 0)
                dve.wait_ge(misc_loaded, 48)
                for g in G:
                    if g + 1 < PIECES:
                        split(0, g + 1)
                    keys(0, g)
                    if g:
                        key_columns(0, g - 1, 0)
                key_columns(0, PIECES - 1, 0)

            def attend(b, par, last, pair):
                if not last:
                    split(b + 1, 0)
                masks(b, 0)
                if not last:
                    keys(b + 1, 0)
                normalise(b, 0)
                for g in range(1, PIECES):
                    if not last:
                        split(b + 1, g)
                    masks(b, g)
                    outputs(b, g - 1, par)
                    normalise(b, g)
                    if not last:
                        key_columns(b + 1, g - 1, 1 - par)
                        keys(b + 1, g)
                outputs(b, PIECES - 1, par)
                if not last:
                    key_columns(b + 1, PIECES - 1, 1 - par)

            batches(dve, attend, first)


def layer_norm(dve, ch, x, stats, mv, var, var_ready, rstd_ready, rstd, out, out_ready, base):
    for t in range(NT):
        last = dve.bn_stats(stats[:, t, :], x[:, t, :])
    ch.link(last)
    for t in range(NT):
        last = dve.bn_aggr(mv[:, t, :], stats[:, t, :])
    ch.link(last)
    dve.tensor_scalar(var[:, :], mv[:, :, 1], 1e-5, None, ALU.add).then_inc(var_ready, 1)
    dve.wait_ge(rstd_ready, base + 1)
    for t in range(NT):
        dve.tensor_scalar(out[:, t, :], x[:, t, :], mv[:, t, 0:1], rstd[:, t:t + 1],
                          ALU.subtract, ALU.mult).then_inc(out_ready, 1)


def ffn0_phase(nc, sem, keep, o_scratch, wo_in, gates_in, identb_in, had_in, wg_in, wu_in, wd_in, wq1_in, bq1_in):
    with ExitStack() as ctx:
        sb = lambda name, shape, dt=F32: ctx.enter_context(nc.sbuf_tensor(name, shape, dt))
        x, ident, mhalf, gate = keep["x"], keep["ident"], keep["mhalf"], keep["gate"]
        q1T = keep["q1T"]
        oT = sb("c_oT", [P, NT, NH, TT])
        wo = sb("c_wo", [P, NH, H])
        w_raw = sb("c_w_raw", [P, 3, 2048])
        w3 = sb("c_w_ternary", [P, 3, 2048], BF16)
        wabs = sb("c_w_abs", [P, 4])
        wmean = sb("c_w_mean", [P, 4])
        wscale = sb("c_w_scale", [P, 4])
        ones = sb("c_ones", [P, P])
        gate_raw = sb("c_gate_raw", [P, 4])
        identb = sb("c_identb", [P, P], BF16)
        identf = sb("c_had", [P, P])
        stats = sb("c_stats", [TT, NT, 6])
        mv = sb("c_mv", [TT, NT, 2])
        var = sb("c_var", [TT, NT])
        rstd = sb("c_rstd", [TT, NT])
        xn = sb("c_xn", [TT, NT, H])
        amax = sb("c_amax", [TT, 2, NT])
        arec = sb("c_arec", [TT, 2, NT])
        ascale = sb("c_ascale", [TT, 2, NT])
        deq = sb("c_deq", [TT, 3, NT])
        xq_t = sb("c_xq_t", [TT, NT, H])
        xq = sb("c_xq", [TT, NT, H], BF16)
        xqT = sb("c_xqT", [P, NT, KC, TT], BF16)
        sg = sb("c_silu", [TT, NT, 2, 512])
        inter = sb("c_inter", [TT, NT, F0])
        iT = sb("c_interT", [P, NT, FC0, TT])
        u = [sb(f"c_had{i}", [TT, NT, FC0, P]) for i in range(1)]
        zq = sb("c_zq", [TT, NT, F0], BF16)
        zT = sb("c_zT", [P, NT, FC0, TT], BF16)
        xnT = sb("c_xnT", [P, KC, T])
        wq1 = sb("c_wq1", [P, KC, H])
        bq1 = sb("c_bq1", [P, KC])
        ps = [ctx.enter_context(nc.psum_tensor(f"c_ps{i}", [P, 512], F32)) for i in range(8)]
        (o_loaded, wo_loaded, w_loaded, c_loaded, q_w_loaded, gates_loaded) = (sem(n) for n in (
            "c_o_loaded", "c_wo_loaded", "c_w_loaded", "c_consts_loaded", "c_wq1_loaded", "c_gates_loaded"))
        (chain, pool_chain, ones_set, gate_ready, wabs_ready, wsum_done, w_ready, wo_done, x1_ready) = (sem(n) for n in (
            "c_chain", "c_pool_chain", "c_ones_set", "c_gate_ready", "c_wabs_ready", "c_wsum_done", "c_w_ready",
            "c_wo_done", "c_x1_ready"))
        (var_ready, rstd_ready, xn_ready, xq_ready, xqt_done, xqt_copied, gu_done, silu_done, inter_ready) = (
            sem(n) for n in ("c_var_ready", "c_rstd_ready", "c_xn_ready", "c_xq_ready", "c_xqT_done", "c_xqT_copied",
                             "c_gate_up_done", "c_silu_done", "c_inter_ready"))
        (it_done, it_copied, had_done, had_copied, zq_ready, zt_done, zt_copied, down_done, xnt_done, xnt_copied,
         q1_done, q1_copied) = (sem(n) for n in (
            "c_interT_done", "c_interT_copied", "c_had_done", "c_had_copied", "c_zq_ready", "c_zT_done",
            "c_zT_copied", "c_down_done", "c_xnT_done", "c_xnT_copied", "c_q1_done", "c_q1_copied"))
        block = ctx.enter_context(nc.Block())

        @block.sync
        def _(sp):
            sp.dma_start(oT[:, :, :, :], o_scratch.rearrange("t p (h s) -> p t h s", h=NH)).then_inc(o_loaded, 16)
            sp.dma_start(wo[:, :, :], wo_in.rearrange("(h d) n -> d h n", d=HD)).then_inc(wo_loaded, 16)
            for n, w in enumerate((wg_in, wu_in, wd_in)):
                sp.dma_start(w_raw[:, n, :].rearrange("p (c n) -> p c n", n=w.shape[1]),
                             w.rearrange("(c p) n -> p c n", p=P)).then_inc(w_loaded, 16)
            sp.dma_start(gate_raw[:, :], gates_in.partition_broadcast(P)).then_inc(gates_loaded, 16)
            sp.dma_start(identb[:, :], identb_in).then_inc(c_loaded, 16)
            sp.dma_start(identf[:, :], had_in).then_inc(c_loaded, 16)
            sp.dma_start(wq1[:, :, :], wq1_in.rearrange("(c p) n -> p c n", p=P)).then_inc(q_w_loaded, 16)
            sp.dma_start(bq1[:, :], bq1_in).then_inc(q_w_loaded, 16)

        @block.gpsimd
        def _(pool):
            pool.memset(ones[:, :], 1.0).then_inc(ones_set, 1)
            for n in range(2):
                pool.wait_ge(var_ready, n + 1)
                pool.tensor_tensor(rstd[:, :], var[:, :], mhalf[:TT, 0:NT], ALU.pow).then_inc(rstd_ready, 1)

        @block.scalar
        def _(act):
            act.wait_ge(gates_loaded, 16)
            act.activation(gate[:, :], gate_raw[:, :], ACT.Tanh).then_inc(gate_ready, 1)
            for t in range(NT):
                act.wait_ge(xqt_done, t + 1)
                act.copy(xqT[:, t, :, :], ps[2 * t].bitcast(BF16)[:, 0:KC * TT].rearrange("p (c s) -> p c s", c=KC)
                         ).then_inc(xqt_copied, 1)
            for n in range(2):
                for t in range(NT):
                    act.wait_ge(gu_done, n * NT + t + 1)
                    act.activation(sg[:, t, n, :], ps[2 * t][:TT, :], ACT.Silu,
                                   scale=deq[:, 0, t:t + 1]).then_inc(silu_done, 1)
            for t in range(NT):
                for n in range(2):
                    act.wait_ge(it_done, 2 * t + n + 1)
                    act.copy(iT[:, t, 4 * n:4 * n + 4, :],
                             ps[2 * t + n][:, 0:4 * TT].rearrange("p (c s) -> p c s", c=4)).then_inc(it_copied, 1)
            for t in range(NT):
                for n in range(2):
                    act.wait_ge(had_done, 2 * t + n + 1)
                    act.mul(u[0][:, t, 4 * n:4 * n + 4, :].rearrange("p c d -> p (c d)"), ps[2 * t + n][:TT, :],
                            float(F0) ** -0.5).then_inc(had_copied, 1)
            for t in range(NT):
                act.wait_ge(zt_done, t + 1)
                act.copy(zT[:, t, :, :], ps[2 * t].bitcast(BF16)[:, 0:FC0 * TT].rearrange("p (c s) -> p c s", c=FC0)
                         ).then_inc(zt_copied, 1)
            for t in range(NT):
                act.wait_ge(xnt_done, t + 1)
                act.copy(xnT[:, :, t * TT:(t + 1) * TT], ps[2 * t][:, 0:KC * TT].rearrange("p (c s) -> p c s", c=KC)
                         ).then_inc(xnt_copied, 1)

        @block.tensor
        def _(pe):
            pe.wait_ge(o_loaded, 16)
            pe.wait_ge(wo_loaded, 16)
            for t in range(NT):
                for h in range(NH):
                    mm = pe.matmul(ps[2 * t][:TT, 0:H], oT[:, t, h, :], wo[:, h, :],
                                   start=h == 0, stop=h == NH - 1)
                mm.then_inc(wo_done, 1)
            pe.wait_ge(ones_set, 1)
            pe.wait_ge(wabs_ready, 1)
            pe.matmul(ps[7][:, 0:3], ones[:, :], wabs[:, 0:3], start=True, stop=True).then_inc(wsum_done, 1)
            pe.wait_ge(c_loaded, 32)
            for t in range(NT):
                pe.wait_ge(xq_ready, t + 1)
                for c in range(KC):
                    mm = pe.transpose(ps[2 * t].bitcast(BF16)[:, c * TT:(c + 1) * TT], xq[:, t, c * P:(c + 1) * P],
                                      identb[:TT, :TT])
                mm.then_inc(xqt_done, 1)
            pe.wait_ge(w_ready, 2)
            for n in range(2):
                for t in range(NT):
                    if n == 0:
                        pe.wait_ge(xqt_copied, t + 1)
                    else:
                        pe.wait_ge(inter_ready, t + 1)
                    for k in range(2):
                        for c in range(KC):
                            mm = pe.matmul(ps[2 * t + k][:TT, :], xqT[:, t, c, :],
                                           w3[:, k, c * F0 + n * 512:c * F0 + (n + 1) * 512],
                                           start=c == 0, stop=c == KC - 1)
                    mm.then_inc(gu_done, 1)
            for t in range(NT):
                pe.wait_ge(inter_ready, NT + t + 1)
                for n in range(2):
                    for j in range(4):
                        c = 4 * n + j
                        mm = pe.transpose(ps[2 * t + n][:, j * TT:(j + 1) * TT], inter[:, t, c * P:(c + 1) * P],
                                          ident[:TT, :TT])
                    mm.then_inc(it_done, 1)
            for t in range(NT):
                pe.wait_ge(it_copied, 2 * t + 2)
                for n in range(2):
                    for j in range(4):
                        mm = pe.matmul(ps[2 * t + n][:TT, j * P:(j + 1) * P], iT[:, t, 4 * n + j, :], identf[:, :],
                                       start=True, stop=True)
                    mm.then_inc(had_done, 1)
            for t in range(NT):
                pe.wait_ge(zq_ready, t + 1)
                for c in range(FC0):
                    mm = pe.transpose(ps[2 * t].bitcast(BF16)[:, c * TT:(c + 1) * TT], zq[:, t, c * P:(c + 1) * P],
                                      identb[:TT, :TT])
                mm.then_inc(zt_done, 1)
            pe.wait_ge(w_ready, 3)
            for t in range(NT):
                pe.wait_ge(zt_copied, t + 1)
                for c in range(FC0):
                    mm = pe.matmul(ps[2 * t + 1][:TT, 0:H], zT[:, t, c, :], w3[:, 2, c * H:(c + 1) * H],
                                   start=c == 0, stop=c == FC0 - 1)
                mm.then_inc(down_done, 1)
            for t in range(NT):
                pe.wait_ge(xn_ready, NT + t + 1)
                for c in range(KC):
                    mm = pe.transpose(ps[2 * t][:, c * TT:(c + 1) * TT], xn[:, t, c * P:(c + 1) * P], ident[:TT, :TT])
                mm.then_inc(xnt_done, 1)
            pe.wait_ge(q_w_loaded, 32)
            pe.wait_ge(xnt_copied, NT)
            for o in range(KC):
                for c in range(KC):
                    mm = pe.matmul(ps[2 * o][:, 0:T], wq1[:, c, o * P:(o + 1) * P], xnT[:, c, :],
                                   start=c == 0, stop=c == KC - 1)
                mm.then_inc(q1_done, 1)

        @block.vector
        def _(dve):
            ch = Chain(dve, chain)
            dve.wait_ge(w_loaded, 48)
            dve.tensor_reduce(wabs[:, 0:3], w_raw[:, :, :], AX.X, ALU.add, apply_absolute_value=True
                              ).then_inc(wabs_ready, 1)
            dve.wait_ge(gate_ready, 1)
            for t in range(NT):
                dve.wait_ge(wo_done, t + 1)
                last = dve.scalar_tensor_tensor(out=x[:, t, :], in0=ps[2 * t][:TT, 0:H], scalar=gate[:TT, 0:1],
                                                in1=x[:, t, :], op0=ALU.mult, op1=ALU.add)
            ch.link(last)
            layer_norm(dve, ch, x, stats, mv, var, var_ready, rstd_ready, rstd, xn, xn_ready, 0)
            dve.wait_ge(wsum_done, 1)
            ch.link(dve.tensor_scalar(wmean[:, 0:3], ps[7][:, 0:3], 1.0 / (F0 * H), 1e-5, ALU.mult, ALU.max))
            ch.link(dve.reciprocal(wscale[:, 0:3], wmean[:, 0:3]))

            def scales(n, src):
                for t in range(NT):
                    last = dve.tensor_reduce(amax[:, n, t:t + 1], src(t), AX.X, ALU.max, apply_absolute_value=True)
                ch.link(last)
                ch.link(dve.tensor_scalar(amax[:, n, :], amax[:, n, :], 1e-5, None, ALU.max))
                ch.link(dve.reciprocal(arec[:, n, :], amax[:, n, :]))
                ch.link(dve.tensor_scalar(ascale[:, n, :], arec[:, n, :], 128.0, None, ALU.mult))

            dve.wait_ge(xn_ready, NT)
            scales(0, lambda t: xn[:, t, :])
            for k in range(2):
                last = dve.tensor_scalar(deq[:, k, :], amax[:, 0, :], 1.0 / 128, wmean[:TT, k:k + 1], ALU.mult, ALU.mult)
            ch.link(last)
            for t in range(NT):
                last = dve.tensor_scalar(xq_t[:, t, :], xn[:, t, :], ascale[:, 0, t:t + 1], BIG, ALU.mult, ALU.add)
            ch.link(last)
            for t in range(NT):
                dve.tensor_scalar(xq[:, t, :], xq_t[:, t, :], BIG, 127.0, ALU.subtract, ALU.min).then_inc(xq_ready, 1)
            for k in range(3):
                ch.link(dve.tensor_scalar(w_raw[:, k, :], w_raw[:, k, :], wscale[:, k:k + 1], BIG, ALU.mult, ALU.add))
                ch.link(dve.tensor_scalar(w_raw[:, k, :], w_raw[:, k, :], BIG, 1.0, ALU.subtract, ALU.min))
                dve.tensor_scalar(w3[:, k, :], w_raw[:, k, :], -1.0, None, ALU.max).then_inc(w_ready, 1)
            for n in range(2):
                for t in range(NT):
                    dve.wait_ge(silu_done, n * NT + t + 1)
                    dve.scalar_tensor_tensor(out=inter[:, t, n * 512:(n + 1) * 512], in0=ps[2 * t + 1][:TT, :],
                                             scalar=deq[:, 1, t:t + 1], in1=sg[:, t, n, :],
                                             op0=ALU.mult, op1=ALU.mult).then_inc(inter_ready, 1)
            for t in range(NT):
                dve.wait_ge(had_copied, 2 * t + 2)
                a, b = u[0][:, t], inter[:, t, :].rearrange("p (c d) -> p c d", d=P)
                for w in (4, 2, 1):
                    av, bv_ = (v.rearrange("p (g two w) d -> p g two (w d)", two=2, w=w) for v in (a, b))
                    dve.tensor_tensor(bv_[:, :, 0], av[:, :, 0], av[:, :, 1], ALU.add)
                    ch.link(dve.tensor_tensor(bv_[:, :, 1], av[:, :, 0], av[:, :, 1], ALU.subtract))
                    a, b = b, a
            scales(1, lambda t: inter[:, t, :])
            ch.link(dve.tensor_scalar(deq[:, 2, :], amax[:, 1, :], 1.0 / 128, wmean[:TT, 2:3], ALU.mult, ALU.mult))
            ch.link(dve.tensor_scalar(deq[:, 2, :], deq[:, 2, :], gate[:TT, 2:3], None, ALU.mult))
            for t in range(NT):
                last = dve.tensor_scalar(u[0][:, t].rearrange("p c d -> p (c d)"), inter[:, t, :],
                                         ascale[:, 1, t:t + 1], BIG, ALU.mult, ALU.add)
            ch.link(last)
            for t in range(NT):
                dve.tensor_scalar(zq[:, t, :], u[0][:, t].rearrange("p c d -> p (c d)"), BIG, 127.0,
                                  ALU.subtract, ALU.min).then_inc(zq_ready, 1)
            for t in range(NT):
                dve.wait_ge(down_done, t + 1)
                last = dve.scalar_tensor_tensor(out=x[:, t, :], in0=ps[2 * t + 1][:TT, 0:H], scalar=deq[:, 2, t:t + 1],
                                                in1=x[:, t, :], op0=ALU.mult, op1=ALU.add)
            ch.link(last)
            layer_norm(dve, ch, x, stats, mv, var, var_ready, rstd_ready, rstd, xn, xn_ready, 1)
            dve.wait_ge(q_w_loaded, 32)
            for o in range(KC):
                dve.wait_ge(q1_done, o + 1)
                dve.tensor_scalar(q1T[:, o, :], ps[2 * o][:, 0:T], bq1[:, o:o + 1], None, ALU.add).then_inc(q1_copied, 1)
            dve.wait_ge(q1_copied, KC)


def attention1_phase(nc, sem, keep, ctx_in, mask_in, wk_in, bk_in, wv_in, bv_in, eye8_in, eye4_in):
    with ExitStack() as ctx:
        sb = lambda name, shape, dt=F32: ctx.enter_context(nc.sbuf_tensor(name, shape, dt))
        q1T, o1T = keep["q1T"], keep["o1T"]
        PC1, CP1 = 3, 4
        W1 = CP1 * CH
        HW = 8 * S
        wkv = sb("d_wkv", [P, 2, KC, H])
        whi = sb("d_whi", [P, 2, KC, H], F32R)
        wlo = sb("d_wlo", [P, 2, KC, H], F32R)
        bk = sb("d_bk", [P, KC])
        bv = sb("d_bv", [GW, NG1])
        eye8 = sb("d_eye8", [P, 8])
        eye4 = sb("d_eye4", [GW, HPG])
        mask_i = sb("d_mask_i", [CH, B, NC], I32)
        att = sb("d_attend", [CH, B, NC])
        e_scale = sb("d_exp_scale", [CH, B, NC])
        e_bias = sb("d_exp_bias", [CH, B, NC])
        esc = sb("d_exp_scale_now", [CH, 2, NC])
        ebi = sb("d_exp_bias_now", [CH, 2, NC])
        raw = sb("d_ctx", [P, 2, KC, W1])
        chi = sb("d_ctx_hi", [P, 2, KC, W1], F32R)
        clo = sb("d_ctx_lo", [P, 2, KC, W1], F32R)
        kT = [sb(f"d_kT{i}", [P, KC, S2]) for i in range(2)]
        V = [sb(f"d_v{i}", [CH, NC, NG1, GW + 32]) for i in range(2)]
        qbd = [sb(f"d_q{i}", [P, 2, 8, S]) for i in range(2)]
        p = [sb(f"d_p{i}", [CH, HW]) for i in range(4)]
        ones = sb("d_ones", [P, GW])
        den = sb("d_den", [P, NG1, HPG * S])
        o_m = sb("d_o_masked", [GW, NG1, HPG, S])
        d_m = sb("d_den_masked", [GW, NG1, HPG, S])
        o_s = sb("d_o", [GW, NG1, S])
        d_s = sb("d_den_s", [GW, NG1, S])
        d_e = sb("d_den_e", [GW, NG1, S])
        d_r = sb("d_den_r", [GW, NG1, S])
        bank = lambda name: ctx.enter_context(nc.psum_tensor(name, [P, 512], F32))
        ps_s = [bank(f"d_ps_s{i}") for i in range(2)]
        ps_k, ps_v = bank("d_ps_k"), bank("d_ps_v")
        ps_o = [bank(f"d_ps_o{i}") for i in range(2)]
        ps_r = [bank(f"d_ps_r{i}") for i in range(2)]
        w_loaded, m_loaded, w_hi, w_lo, prep, now_ready, q_ready, chain = (sem(n) for n in (
            "d_w_loaded", "d_misc_loaded", "d_w_hi", "d_w_lo", "d_prepared", "d_now_ready", "d_q_ready", "d_chain"))
        ctx_loaded = [sem(f"d_ctx_loaded{i}") for i in range(2)]
        ctx_hi, ctx_lo, k_done, k_copied, v_done, v_copied, s_done, exp_done, p_ready = (sem(n) for n in (
            "d_ctx_hi", "d_ctx_lo", "d_k_done", "d_k_copied", "d_v_done", "d_v_copied", "d_s_done", "d_exp_done",
            "d_p_ready"))
        o_masked, den_copied, r_done, r_masked, o_ready, ones_set = (sem(n) for n in (
            "d_o_masked_ready", "d_den_copied", "d_den_spread", "d_den_masked_ready", "d_o_ready",
            "d_ones_set"))
        p_used, prep0 = sem("d_p_used"), sem("d_mask_read")
        block = ctx.enter_context(nc.Block())
        POST = 5

        def batches(eng, attend, first):
            first()
            with eng.Fori(0, B // 2 - 1) as i:
                for par in range(2):
                    attend(i * 2 + par, par, False)
            for par in range(2):
                attend(B - 2 + par, par, par == 1)

        def slot(par, pc):
            return (PC1 * par + pc) % 2

        @block.sync
        def _(sp):
            for k, w in enumerate((wk_in, wv_in)):
                sp.dma_start(wkv[:, k], w.rearrange("(c p) n -> p c n", p=P)).then_inc(w_loaded, 16)
            for dst, src in ((bk, bk_in), (bv, bv_in), (eye8, eye8_in), (eye4, eye4_in)):
                sp.dma_start(dst[:, :], src).then_inc(m_loaded, 16)
            sp.dma_start(mask_i[:, :, :], mask_in).then_inc(m_loaded, 16)

            def load(b, par):
                for pc in range(PC1):
                    wait_for(sp, ctx_lo, PC1 * b + pc - 1)
                    sp.dma_start(raw[:, slot(par, pc)],
                                 ctx_in[b, :, pc * W1:(pc + 1) * W1].rearrange("(c p) s -> p c s", p=P)
                                 ).then_inc(ctx_loaded[slot(par, pc)], 16)

            def attend(b, par, last):
                if not last:
                    load(b + 1, 1 - par)

            batches(sp, attend, lambda: load(0, 0))

        @block.gpsimd
        def _(pool):
            for i in range(2):
                pool.memset(V[i][:, :, :, GW:], 1.0).then_inc(ones_set, 1)
            pool.memset(ones[:, :], 1.0).then_inc(ones_set, 1)
            pool.wait_ge(prep, 1)

            def now(b, par):
                if not (isinstance(b, int) and b == 0):
                    pool.wait_ge(exp_done, (b - 1) * 24 + 1)
                pool.tensor_copy(esc[:, par, :], e_scale[:, b, :])
                pool.tensor_copy(ebi[:, par, :], e_bias[:, b, :]).then_inc(now_ready, 1)

            def attend(b, par, last):
                if not last:
                    now(b + 1, 1 - par)

            batches(pool, attend, lambda: now(0, 0))

        @block.scalar
        def _(act):
            act.wait_ge(w_loaded, 32)
            act.copy(whi[:, :, :, :], wkv[:, :, :, :]).then_inc(w_hi, 1)

            def split(b, par, pc):
                s = slot(par, pc)
                act.wait_ge(ctx_loaded[s], (b - par) * 24 + 16 * ((PC1 * par + pc) // 2 + 1))
                wait_for(act, v_done, 2 * (PC1 * b + pc - 1))
                act.copy(chi[:, s], raw[:, s]).then_inc(ctx_hi, 1)

            def values_out(b, par, pc):
                for k in range(2):
                    act.wait_ge(v_done, 2 * (PC1 * b + pc) + k + 1)
                    c = pc * CP1 + 2 * k
                    for cc in range(2):
                        last = act.copy(V[par][:, c + cc, :, 0:GW],
                                        ps_v[:CH, cc * H:(cc + 1) * H].rearrange("p (g d) -> p g d", g=NG1))
                    last.then_inc(v_copied, 1)

            def first():
                for pc in range(PC1):
                    split(0, 0, pc)
                    values_out(0, 0, pc)

            def attend(b, par, last):
                act.wait_ge(now_ready, b + 1)
                for third in range(PC1):
                    if not last:
                        split(b + 1, 1 - par, third)
                    for v in range(8 * third, 8 * third + 8):
                        act.wait_ge(s_done, b * 24 + v + 1)
                        if v >= 4:
                            act.wait_ge(p_used, b * 24 + v - 3)
                        act.activation(p[v % 4][:, :], ps_s[v % 2][:CH, 0:HW], ACT.Exp, bias=ebi[:, par, v // 2:v // 2 + 1],
                                       scale=esc[:, par, v // 2:v // 2 + 1]).then_inc(exp_done, 1)
                    if third == PC1 - 1:
                        for k in range(2):
                            act.wait_ge(p_used, b * 24 + 24)
                            act.copy(den[GW:GW + 1, 2 * k:2 * k + 2, :],
                                     ps_o[k][GW:GW + 1, 0:HW].rearrange("p (g q) -> p g q", g=2)).then_inc(den_copied, 1)
                    if not last:
                        values_out(b + 1, 1 - par, third)

            batches(act, attend, first)

        @block.tensor
        def _(pe):
            def project(b, par, pc):
                s = slot(par, pc)
                pe.wait_ge(ctx_lo, PC1 * b + pc + 1)
                for half in range(2):
                    n = 2 * (PC1 * b + pc) + half
                    wait_for(pe, k_copied, n)
                    m = 0
                    for c in range(KC):
                        for a, w in ((chi, whi), (chi, wlo), (clo, whi)):
                            mm = pe.matmul(ps_k[:, 0:W1], w[:, 0, c, half * P:(half + 1) * P], a[:, s, c, :],
                                           start=m == 0, stop=m == 3 * KC - 1)
                            m += 1
                    mm.then_inc(k_done, 1)
                    wait_for(pe, v_copied, n)
                    for cc in range(2):
                        ch_ = 2 * half + cc
                        m = 0
                        for c in range(KC):
                            for a, w in ((chi, whi), (chi, wlo), (clo, whi)):
                                mm = pe.matmul(ps_v[:CH, cc * H:(cc + 1) * H], a[:, s, c, ch_ * CH:(ch_ + 1) * CH],
                                               w[:, 1, c, :], start=m == 0, stop=m == 3 * KC - 1)
                                m += 1
                    mm.then_inc(v_done, 1)

            def scores(b, par, v):
                c, half = v // 2, v % 2
                if v >= 2:
                    pe.wait_ge(exp_done, b * 24 + v - 1)
                pe.matmul(ps_s[v % 2][:CH, 0:HW], kT[par][:, half, c * CH:(c + 1) * CH],
                          qbd[par][:, half].rearrange("p h s -> p (h s)"), start=True, stop=True).then_inc(s_done, 1)

            def values(b, par, v):
                c, half = v // 2, v % 2
                pe.wait_ge(p_ready, b * 24 + v + 1)
                for gg in range(2):
                    mm = pe.matmul(ps_o[half][:GW + 32, gg * HPG * S:(gg + 1) * HPG * S], V[par][:, c, 2 * half + gg, :],
                                   p[v % 4][:, gg * HPG * S:(gg + 1) * HPG * S],
                                   start=c == 0 and gg == 0, stop=c == NC - 1, skip_group_check=True)
                mm.then_inc(p_used, 1)

            def spread(b):
                pe.wait_ge(den_copied, b * 2 + 2)
                for k in range(2):
                    pe.matmul(ps_r[k][:GW, 0:HW], ones[GW:GW + 1, :], den[GW:GW + 1, 2 * k:2 * k + 2, :].rearrange("p g q -> p (g q)"),
                              start=True, stop=True).then_inc(r_done, 1)

            def first():
                pe.wait_ge(w_lo, 1)
                for pc in range(PC1):
                    project(0, 0, pc)
                pe.wait_ge(ones_set, 3)

            def attend(b, par, last):
                pe.wait_ge(k_copied, 6 * b + 6)
                pe.wait_ge(v_copied, 6 * b + 6)
                pe.wait_ge(q_ready, b + 1)
                scores(b, par, 0)
                scores(b, par, 1)
                for v in range(24):
                    if v + 2 < 24:
                        scores(b, par, v + 2)
                    values(b, par, v)
                    if v in (5, 13) and not last:
                        project(b + 1, 1 - par, v // 8)
                if not last:
                    project(b + 1, 1 - par, PC1 - 1)
                spread(b)

            batches(pe, attend, first)

        @block.vector
        def _(dve):
            dve.wait_ge(m_loaded, 80)
            ch0 = Chain(dve, prep0)
            ch0.link(dve.tensor_scalar(att[:, :, :], mask_i[:, :, :], 0.5, None, ALU.is_gt))
            dve.tensor_scalar(e_scale[:, :, :], att[:, :, :], float(D1) ** -0.5, None, ALU.mult)
            dve.tensor_scalar(e_bias[:, :, :], att[:, :, :], 1.0, 50.0, ALU.subtract, ALU.mult).then_inc(prep, 1)
            dve.wait_ge(w_hi, 1)
            dve.tensor_tensor(wlo[:, :, :, :], wkv[:, :, :, :], whi.bitcast(F32)[:, :, :, :], ALU.subtract).then_inc(w_lo, 1)

            def split(b, par, pc):
                s = slot(par, pc)
                dve.wait_ge(ctx_hi, PC1 * b + pc + 1)
                dve.tensor_tensor(clo[:, s], raw[:, s], chi.bitcast(F32)[:, s], ALU.subtract).then_inc(ctx_lo, 1)

            def keys_out(b, par, pc):
                for half in range(2):
                    dve.wait_ge(k_done, 2 * (PC1 * b + pc) + half + 1)
                    dve.tensor_scalar(kT[par][:, half, pc * W1:(pc + 1) * W1], ps_k[:, 0:W1], bk[:, half:half + 1], None,
                                      ALU.add).then_inc(k_copied, 1)

            def queries(b, par):
                for half in range(2):
                    last = dve.tensor_tensor(qbd[par][:, half],
                                             q1T[:, half, bass.ds(b * S, S)].unsqueeze(1).broadcast_to([P, 8, S]),
                                             eye8[:, :].unsqueeze(2).broadcast_to([P, 8, S]), ALU.mult)
                last.then_inc(q_ready, 1)

            def first():
                queries(0, 0)
                for pc in range(PC1):
                    split(0, 0, pc)
                    keys_out(0, 0, pc)

            def attend(b, par, last):
                if not last:
                    queries(b + 1, 1 - par)
                for third in range(PC1):
                    if not last:
                        split(b + 1, 1 - par, third)
                    for v in range(8 * third, 8 * third + 8):
                        dve.wait_ge(exp_done, b * 24 + v + 1)
                        dve.tensor_scalar(p[v % 4][:, :], p[v % 4][:, :], E_LO, E_HI, ALU.max, ALU.min).then_inc(p_ready, 1)
                    if third == PC1 - 1:
                        own4 = eye4[:, :].unsqueeze(2).broadcast_to([GW, HPG, S])
                        for k in range(2):
                            dve.wait_ge(p_used, b * 24 + 24)
                            for gg in range(2):
                                src = ps_o[k][:GW, gg * HPG * S:(gg + 1) * HPG * S].rearrange("p (j s) -> p j s", j=HPG)
                                last_ins = dve.tensor_tensor(o_m[:, 2 * k + gg], src, own4, ALU.mult)
                            last_ins.then_inc(o_masked, 1)
                    if not last:
                        keys_out(b + 1, 1 - par, third)
                ch = Chain(dve, chain, b * POST)
                dve.wait_ge(o_masked, b * 2 + 2)
                ch.link(dve.tensor_reduce(o_s[:, :, :], o_m[:, :, :, :].rearrange("p g j s -> p g s j"), AX.X, ALU.add))
                for k in range(2):
                    dve.wait_ge(r_done, b * 2 + 2)
                    for gg in range(2):
                        src = ps_r[k][:GW, gg * HPG * S:(gg + 1) * HPG * S].rearrange("p (j s) -> p j s", j=HPG)
                        last_ins = dve.tensor_tensor(d_m[:, 2 * k + gg], src, own4, ALU.mult)
                    last_ins.then_inc(r_masked, 1)
                dve.wait_ge(r_masked, b * 2 + 2)
                ch.link(dve.tensor_reduce(d_s[:, :, :], d_m[:, :, :, :].rearrange("p g j s -> p g s j"), AX.X, ALU.add))
                ch.link(dve.scalar_tensor_tensor(out=d_e[:, :, :], in0=d_s[:, :, :], scalar=1e-8, in1=d_s[:, :, :],
                                                 op0=ALU.mult, op1=ALU.add))
                ch.link(dve.reciprocal(d_r[:, :, :], d_e[:, :, :]))
                ch.link(dve.tensor_tensor(o_s[:, :, :], o_s[:, :, :], d_r[:, :, :], ALU.mult))
                dve.tensor_tensor(o1T[:, :, bass.ds(b * S, S)], o_s[:, :, :],
                                  bv[:, :].unsqueeze(2).broadcast_to([GW, NG1, S]), ALU.add).then_inc(o_ready, 1)
                dve.wait_ge(o_ready, b + 1)

            batches(dve, attend, first)


def experts_phase(nc, sem, keep, wo_in, bo_in, gamma_in, beta_in, rs_in, rw_in, rb_in, w1_in, b1_in, w2_in, b2_in, out):
    NE = w1_in.shape[0]
    NR, NSH = rw_in.shape[1], w1_in.shape[0] - rw_in.shape[1]
    HH = w1_in.shape[2] // 2
    TOPK = 6
    with ExitStack() as ctx:
        sb = lambda name, shape, dt=F32: ctx.enter_context(nc.sbuf_tensor(name, shape, dt))
        x, ident, mhalf, gate, o1T = (keep[n] for n in ("x", "ident", "mhalf", "gate", "o1T"))
        wo = sb("e_wo", [GW, NG1, H])
        bo = sb("e_bo", [TT, H])
        gamma = sb("e_gamma", [TT, H])
        beta = sb("e_beta", [TT, H])
        rs_raw = sb("e_rs_raw", [TT, 1])
        rs = sb("e_rs", [TT, 1])
        rw = sb("e_rw", [P, KC, NR])
        rb = sb("e_rb", [TT, NR])
        d = sb("e_delta", [TT, NT, H])
        fin = sb("e_finite", [TT, NT, H], I32)
        dn = sb("e_delta_norm", [TT, NT, H])
        stats = sb("e_stats", [TT, NT, 6])
        mv = sb("e_mv", [TT, NT, 2])
        var = sb("e_var", [TT, NT])
        rstd = sb("e_rstd", [TT, NT])
        xn = sb("e_xn", [TT, NT, H])
        xnT = sb("e_xnT", [P, KC, T])
        lg = sb("e_logits", [TT, NT, NR])
        nmx = sb("e_neg_max", [TT, NT])
        pr = sb("e_probs", [TT, NT, NR + 2])
        psum_ = sb("e_prob_sum", [TT, NT])
        prec = sb("e_prob_rec", [TT, NT])
        top = sb("e_top8", [TT, NT, 8])
        marked = sb("e_marked", [TT, NT, NR + 2])
        chosen = sb("e_chosen", [TT, NT, NR])
        gs = sb("e_gate_sum", [TT, NT])
        gr = sb("e_gate_rec", [TT, NT])
        g = sb("e_gates", [TT, NT, NE])
        gT = sb("e_gatesT", [NE, T])
        b2 = sb("e_b2", [NE, H])
        acc = sb("e_acc", [TT, NT, H])
        w1 = [sb(f"e_w1_{i}", [P, KC, 2 * HH]) for i in range(2)]
        w2 = [sb(f"e_w2_{i}", [HH, 2, H]) for i in range(2)]
        b1 = [sb(f"e_b1_{i}", [HH, 2]) for i in range(2)]
        gcol = [sb(f"e_gcol{i}", [TT, NT]) for i in range(2)]
        hT = [sb(f"e_hT{i}", [HH, 2, T]) for i in range(2)]
        ps = [ctx.enter_context(nc.psum_tensor(f"e_ps{i}", [P, 512], F32)) for i in range(8)]
        (wo_loaded, ln_loaded, r_loaded, b2_loaded, sent_set, var_ready, rstd_ready, xn_ready, wo_done, chain,
         xnt_done, xnt_copied, lg_done, max_ready, exp_done, gates_ready, gt_done, gt_copied, acc_done,
         x_ready, stored) = (sem("e_" + n) for n in (
            "wo_loaded", "ln_loaded", "router_loaded", "b2_loaded", "sentinels_set", "var_ready", "rstd_ready",
            "xn_ready", "wo_done", "chain", "xnT_done", "xnT_copied", "logits_done", "max_ready", "exp_done",
            "gates_ready", "gatesT_done", "gatesT_copied", "acc_done", "x_ready", "stored"))
        dn_ready = sem("e_delta_norm_ready")
        w_loaded = [sem(f"e_w_loaded{i}") for i in range(2)]
        gcol_ready, h_done, h_ready, y_done, y_added = (sem("e_" + n) for n in (
            "gcol_ready", "h_done", "h_ready", "y_done", "y_added"))
        block = ctx.enter_context(nc.Block())

        @block.sync
        def _(sp):
            sp.dma_start(wo[:, :, :], wo_in.rearrange("(g d) n -> d g n", d=GW)).then_inc(wo_loaded, 16)
            for dst, src in ((bo, bo_in), (gamma, gamma_in), (beta, beta_in), (rs_raw, rs_in)):
                sp.dma_start(dst[:, :], src.partition_broadcast(TT)).then_inc(ln_loaded, 16)
            sp.dma_start(rw[:, :, :], rw_in.rearrange("(c p) n -> p c n", p=P)).then_inc(r_loaded, 16)
            sp.dma_start(rb[:, :], rb_in.partition_broadcast(TT)).then_inc(r_loaded, 16)
            sp.dma_start(b2[:, :], b2_in).then_inc(b2_loaded, 16)

            def load(e, par):
                sp.dma_start(w1[par][:, :, :], w1_in[e].rearrange("(c p) n -> p c n", p=P)).then_inc(w_loaded[par], 16)
                sp.dma_start(w2[par][:, :, :], w2_in[e].rearrange("(k d) n -> d k n", d=HH)).then_inc(w_loaded[par], 16)
                sp.dma_start(b1[par][:, :], b1_in[e]).then_inc(w_loaded[par], 16)

            for par in range(2):
                load(par, par)
            with sp.Fori(0, NE // 2 - 1) as i:
                for par in range(2):
                    sp.wait_ge(y_done, i * 4 + 2 * par + 2)
                    load(i * 2 + 2 + par, par)
            for t in range(NT):
                sp.wait_ge(x_ready, t + 1)
                sp.dma_start(out[t * TT:(t + 1) * TT, :], x[:, t, :]).then_inc(stored, 16)
            sp.wait_ge(stored, 16 * NT)

        @block.gpsimd
        def _(pool):
            for k in range(2):
                pool.memset(pr[:, :, NR + k:NR + k + 1], -1.0 - k).then_inc(sent_set, 1)
            pool.memset(g[:, :, NR:], 1.0 / NSH).then_inc(sent_set, 1)
            for n in range(2):
                pool.wait_ge(var_ready, n + 1)
                pool.tensor_tensor(rstd[:, :], var[:, :], mhalf[:TT, 0:NT], ALU.pow).then_inc(rstd_ready, 1)
            pool.wait_ge(gates_ready, NT)

            def column(e, par):
                wait_for(pool, y_added, e * NT)
                pool.tensor_copy(gcol[par][:, :], g[:, :, bass.ds(e, 1)].rearrange("p t o -> p (t o)")).then_inc(gcol_ready, 1)

            for par in range(2):
                column(par, par)
            with pool.Fori(0, NE // 2 - 1) as i:
                for par in range(2):
                    column(i * 2 + 2 + par, par)

        @block.scalar
        def _(act):
            for t in range(NT):
                act.wait_ge(xnt_done, t + 1)
                act.copy(xnT[:, :, t * TT:(t + 1) * TT], ps[2 * t][:, 0:KC * TT].rearrange("p (c s) -> p c s", c=KC)
                         ).then_inc(xnt_copied, 1)
            act.wait_ge(sent_set, 3)
            for t in range(NT):
                act.wait_ge(max_ready, t + 1)
                act.activation(pr[:, t, 0:NR], lg[:, t, :], ACT.Exp, bias=nmx[:, t:t + 1],
                               accum_out=psum_[:, t:t + 1]).then_inc(exp_done, 1)

            def hidden(e, par):
                act.wait_ge(w_loaded[par], (e - par) * 24 + 48)
                for k in range(2):
                    act.wait_ge(h_done, e * 2 + k + 1)
                    act.activation(hT[par][:, k, :], ps[2 * par + k][:HH, 0:T], ACT.Relu,
                                   bias=b1[par][:, k:k + 1]).then_inc(h_ready, 1)

            with act.Fori(0, NE // 2) as i:
                for par in range(2):
                    hidden(i * 2 + par, par)

        @block.tensor
        def _(pe):
            pe.wait_ge(wo_loaded, 16)
            for t in range(NT):
                for k in range(NG1):
                    mm = pe.matmul(ps[2 * t][:TT, 0:H], o1T[:, k, t * TT:(t + 1) * TT], wo[:, k, :],
                                   start=k == 0, stop=k == NG1 - 1)
                mm.then_inc(wo_done, 1)
            for t in range(NT):
                pe.wait_ge(xn_ready, t + 1)
                for c in range(KC):
                    mm = pe.transpose(ps[2 * t][:, c * TT:(c + 1) * TT], xn[:, t, c * P:(c + 1) * P], ident[:TT, :TT])
                mm.then_inc(xnt_done, 1)
            pe.wait_ge(r_loaded, 32)
            for t in range(NT):
                pe.wait_ge(xnt_copied, t + 1)
                for c in range(KC):
                    mm = pe.matmul(ps[2 * t + 1][:TT, 0:NR], xnT[:, c, t * TT:(t + 1) * TT], rw[:, c, :],
                                   start=c == 0, stop=c == KC - 1)
                mm.then_inc(lg_done, 1)
            for t in range(NT):
                pe.wait_ge(gates_ready, t + 1)
                pe.transpose(ps[2 * t][:NE, 0:TT], g[:, t, :], ident[:TT, :TT]).then_inc(gt_done, 1)
            pe.wait_ge(b2_loaded, 16)
            for t in range(NT):
                pe.wait_ge(gt_copied, t + 1)
                pe.matmul(ps[2 * t + 1][:TT, 0:H], gT[:, t * TT:(t + 1) * TT], b2[:, :],
                          start=True, stop=True).then_inc(acc_done, 1)
            pe.wait_ge(y_added, NT)

            def hidden(e, par):
                pe.wait_ge(w_loaded[par], (e - par) * 24 + 48)
                for k in range(2):
                    for c in range(KC):
                        mm = pe.matmul(ps[2 * par + k][:HH, 0:T], w1[par][:, c, k * HH:(k + 1) * HH], xnT[:, c, :],
                                       start=c == 0, stop=c == KC - 1)
                    mm.then_inc(h_done, 1)

            def outputs(e, par):
                pe.wait_ge(h_ready, e * 2 + 2)
                for b in range(2):
                    wait_for(pe, y_added, e * NT)
                    for tt in range(2):
                        t = 2 * b + tt
                        for k in range(2):
                            mm = pe.matmul(ps[4 + 2 * par + b][:TT, tt * H:(tt + 1) * H], hT[par][:, k, t * TT:(t + 1) * TT],
                                           w2[par][:, k, :], start=k == 0, stop=k == 1)
                    mm.then_inc(y_done, 1)

            hidden(0, 0)
            hidden(1, 1)
            outputs(0, 0)
            with pe.Fori(0, NE // 2 - 1) as i:
                hidden(i * 2 + 2, 0)
                outputs(i * 2 + 1, 1)
                hidden(i * 2 + 3, 1)
                outputs(i * 2 + 2, 0)
            outputs(NE - 1, 1)

        @block.vector
        def _(dve):
            ch = Chain(dve, chain)
            dve.wait_ge(ln_loaded, 64)
            ch.link(dve.tensor_scalar(rs[:, :], rs_raw[:, :], 0.0, 0.3, ALU.max, ALU.min))
            for t in range(NT):
                dve.wait_ge(wo_done, t + 1)
                last = dve.tensor_tensor(d[:, t, :], ps[2 * t][:TT, 0:H], bo[:, :], ALU.add)
            ch.link(last)
            ch.link(dve.tensor_tensor(fin[:, :, :], d[:, :, :], d[:, :, :], ALU.is_equal))
            ch.link(dve.memset(dn[:, :, :], 0.0))
            ch.link(dve.copy_predicated(dn[:, :, :], fin[:, :, :], d[:, :, :]))
            for sign in (1.0, -1.0):
                ch.link(dve.tensor_scalar(fin[:, :, :], dn[:, :, :], sign * 3.4028235e38, None,
                                          ALU.is_gt if sign > 0 else ALU.is_lt))
                ch.link(dve.memset(d[:, :, :], sign * 1e4))
                ch.link(dve.copy_predicated(dn[:, :, :], fin[:, :, :], d[:, :, :]))
            ch.link(dve.tensor_scalar(d[:, :, :], dn[:, :, :], rs[:, 0:1], None, ALU.mult))
            layer_norm(dve, ch, d, stats, mv, var, var_ready, rstd_ready, rstd, dn, dn_ready, 0)
            dve.wait_ge(dn_ready, NT)
            bc = lambda v: v[:, :].unsqueeze(1).broadcast_to([TT, NT, H])
            ch.link(dve.tensor_tensor(dn[:, :, :], dn[:, :, :], bc(gamma), ALU.mult))
            ch.link(dve.tensor_tensor(dn[:, :, :], dn[:, :, :], bc(beta), ALU.add))
            ch.link(dve.scalar_tensor_tensor(out=x[:, :, :], in0=dn[:, :, :], scalar=gate[:TT, 1:2], in1=x[:, :, :],
                                             op0=ALU.mult, op1=ALU.add))
            layer_norm(dve, ch, x, stats, mv, var, var_ready, rstd_ready, rstd, xn, xn_ready, 1)
            dve.wait_ge(r_loaded, 32)
            for t in range(NT):
                dve.wait_ge(lg_done, t + 1)
                last = dve.tensor_tensor(lg[:, t, :], ps[2 * t + 1][:TT, 0:NR], rb[:, :], ALU.add)
            ch.link(last)
            for t in range(NT):
                dve.tensor_reduce(nmx[:, t:t + 1], lg[:, t, :], AX.X, ALU.max, negate=True).then_inc(max_ready, 1)
            dve.wait_ge(exp_done, NT)
            ch.link(dve.reciprocal(prec[:, :], psum_[:, :]))
            for t in range(NT):
                last = dve.tensor_scalar(pr[:, t, 0:NR], pr[:, t, 0:NR], prec[:, t:t + 1], None, ALU.mult)
            ch.link(last)
            for t in range(NT):
                last = dve.max(top[:, t, :], pr[:, t, 0:NR])
            ch.link(last)
            for k in range(8 - TOPK):
                last = dve.memset(top[:, :, TOPK + k:TOPK + k + 1], -1.0 - k)
            ch.link(last)
            for t in range(NT):
                last = dve.match_replace(marked[:, t, :], top[:, t, :], pr[:, t, :], -5.0)
            ch.link(last)
            ch.link(dve.tensor_scalar(chosen[:, :, :], marked[:, :, 0:NR], -5.0, None, ALU.is_equal))
            ch.link(dve.tensor_tensor(chosen[:, :, :], chosen[:, :, :], pr[:, :, 0:NR], ALU.mult))
            ch.link(dve.tensor_reduce(gs[:, :], chosen[:, :, :], AX.X, ALU.add))
            ch.link(dve.reciprocal(gr[:, :], gs[:, :]))
            for t in range(NT):
                dve.tensor_scalar(g[:, t, 0:NR], chosen[:, t, :], gr[:, t:t + 1], None, ALU.mult).then_inc(gates_ready, 1)
            for t in range(NT):
                dve.wait_ge(gt_done, t + 1)
                dve.tensor_copy(gT[:, t * TT:(t + 1) * TT], ps[2 * t][:NE, 0:TT]).then_inc(gt_copied, 1)
            for t in range(NT):
                dve.wait_ge(acc_done, t + 1)
                dve.tensor_copy(acc[:, t, :], ps[2 * t + 1][:TT, 0:H]).then_inc(y_added, 1)

            with dve.Fori(0, NE // 2) as i:
                for par in range(2):
                    e = i * 2 + par
                    dve.wait_ge(gcol_ready, e + 1)
                    dve.wait_ge(y_added, e * NT + NT)
                    for t in range(NT):
                        if t % 2 == 0:
                            dve.wait_ge(y_done, e * 2 + t // 2 + 1)
                        dve.scalar_tensor_tensor(out=acc[:, t, :], in0=ps[4 + 2 * par + t // 2][:TT, (t % 2) * H:(t % 2 + 1) * H],
                                                 scalar=gcol[par][:, t:t + 1], in1=acc[:, t, :],
                                                 op0=ALU.mult, op1=ALU.add).then_inc(y_added, 1)
            dve.wait_ge(y_added, NE * NT + NT)
            for t in range(NT):
                dve.scalar_tensor_tensor(out=x[:, t, :], in0=acc[:, t, :], scalar=gate[:TT, 3:4], in1=x[:, t, :],
                                         op0=ALU.mult, op1=ALU.add).then_inc(x_ready, 1)


def flamingo_program(nc, a, out):
    with ExitStack() as ctx:
        names = set()

        def sem(name):
            assert name not in names
            names.add(name)
            return ctx.enter_context(nc.semaphore(name))

        sb = lambda name, shape, dt=F32: ctx.enter_context(nc.sbuf_tensor(name, shape, dt))
        keep = {
            "x": sb("x", [TT, NT, H]),
            "ident": sb("ident", [P, P]),
            "mhalf": sb("minus_half", [P, 48]),
            "gate": sb("gate", [P, 4]),
        }
        q_scratch = nc.dram_tensor("q_scratch", [B, P, NH, S], F32).ap()
        o_scratch = nc.dram_tensor("o_scratch", [NT, P, NH * TT], F32).ap()
        query_phase(nc, sem, keep, a["x"], a["L0_xattn_Wq"], a["L0_xattn_bq"], a["L0_xattn_qn_w"],
                    a["L0_xattn_kn_w"], a["ident"], q_scratch)
        attention0_phase(nc, sem, keep, a["ctxT"], a["mask_f"], a["L0_xattn_Wk"], a["L0_xattn_bk"],
                         a["L0_xattn_Wv"], a["L0_xattn_bv"], q_scratch, o_scratch)
        keep["q1T"] = sb("q1T", [P, KC, T])
        keep["o1T"] = sb("o1T", [GW, NG1, T])
        ffn0_phase(nc, sem, keep, o_scratch, a["L0_xattn_Wo"], a["gates"], a["ident_b"], a["hadamard"],
                   a["L0_ffn_w_gateT"], a["L0_ffn_w_upT"], a["L0_ffn_w_downT"], a["L1_xattn_WqT"], a["L1_xattn_bq"])
        attention1_phase(nc, sem, keep, a["ctxT"], a["mask_i"], a["L1_xattn_WkT"], a["L1_xattn_bk"],
                         a["L1_xattn_WvT"], a["L1_xattn_bv"], a["eye8"], a["eye4"])
        experts_phase(nc, sem, keep, a["L1_xattn_WoT"], a["L1_xattn_bo"], a["L1_xattn_ln_gamma"],
                      a["L1_xattn_ln_beta"], a["L1_xattn_residual_scale"], a["L1_ffn_router_w"],
                      a["L1_ffn_router_b"], a["L1_ffn_w1"], a["L1_ffn_b1"], a["L1_ffn_w2"], a["L1_ffn_b2"], out)


def laid_out(i):
    import numpy as np

    i = {k: np.asarray(v) for k, v in i.items()}
    a = {
        "x": i["x"].reshape(T, H),
        "ctxT": i["ctx_2048"].transpose(0, 2, 1),
        "mask_f": i["mask_1xSxS2_ff0"][0],
        "mask_i": i["mask_BxS2_ik0"].reshape(B, NC, CH).transpose(2, 0, 1),
        "gates": np.concatenate([i["g_xattn"], i["g_ffn"]]),
    }
    for n in ("Wq", "bq", "Wk", "bk", "Wv", "Wo"):
        a["L0_xattn_" + n] = i["L0_xattn_" + n]
    a["L0_xattn_bv"] = i["L0_xattn_bv"].reshape(NKV, HD).T
    for n in ("qn_w", "kn_w"):
        a["L0_xattn_" + n] = i["L0_xattn_" + n].reshape(HD, 1)
    for n in ("w_gate", "w_up", "w_down"):
        a["L0_ffn_" + n + "T"] = i["L0_ffn_" + n].T
    for n in ("Wq", "Wk", "Wv", "Wo"):
        a["L1_xattn_" + n + "T"] = i["L1_xattn_" + n].T
    for n in ("bq", "bk"):
        a["L1_xattn_" + n] = i["L1_xattn_" + n].reshape(KC, P).T
    a["L1_xattn_bv"] = i["L1_xattn_bv"].reshape(NG1, GW).T
    for n in ("bo", "ln_gamma", "ln_beta"):
        a["L1_xattn_" + n] = i["L1_xattn_" + n]
    a["L1_xattn_residual_scale"] = i["L1_xattn_residual_scale"].reshape(1)
    a["L1_ffn_router_w"] = i["L1_ffn_router_w"]
    a["L1_ffn_router_b"] = i["L1_ffn_router_b"]
    for n in ("w1", "b1", "w2", "b2"):
        a["L1_ffn_" + n] = np.concatenate([i["L1_ffn_r" + n], i["L1_ffn_s" + n]])
    b1 = a["L1_ffn_b1"]
    a["L1_ffn_b1"] = b1.reshape(b1.shape[0], 2, b1.shape[1] // 2).transpose(0, 2, 1)
    a["ident"] = np.eye(P, dtype=np.float32)
    a["ident_b"] = np.eye(P, dtype=mybir.dt.np(BF16))
    a["eye8"] = np.kron(np.eye(8, dtype=np.float32), np.ones((D1, 1), np.float32))
    a["eye4"] = np.kron(np.eye(HPG, dtype=np.float32), np.ones((D1, 1), np.float32))
    had = np.ones((1, 1), np.float32)
    while had.shape[0] < P:
        had = np.block([[had, had], [had, -had]])
    a["hadamard"] = had.astype(np.float32)
    return {"in_" + k: np.ascontiguousarray(v) for k, v in a.items()}


def kernel(**inputs):
    import numpy as np
    import concourse.bacc as bacc
    from concourse.bass_utils import run_bass_kernel_spmd

    nc = bacc.Bacc("TRN2", target_bir_lowering=False, num_devices=1)
    arrays = laid_out(inputs)
    a = {k[3:]: nc.dram_tensor(k, v.shape, mybir.dt.from_np(v.dtype), kind="ExternalInput").ap()
         for k, v in arrays.items()}
    out = nc.dram_tensor("out", (T, H), F32, kind="ExternalOutput").ap()
    flamingo_program(nc, a, out)
    r = run_bass_kernel_spmd(nc, [arrays], core_ids=[0])
    return r.results[0]["out"].reshape(B, S, H)
```

```python
import math
from contextlib import ExitStack

import concourse.bass as bass
from concourse import mybir

ALU = mybir.AluOpType
ACT = mybir.ActivationFunctionType
AX = mybir.AxisListType
F32 = mybir.dt.float32
F32R = mybir.dt.float32r
BF16 = mybir.dt.bfloat16
I32 = mybir.dt.int32

B, S, H = 8, 56, 256
S2 = 1500
T = B * S
P = 128
KC = H // P
TT = 2 * S
NT = T // TT
CH = 125
NC = S2 // CH
PIECES = 4
CPP = NC // PIECES
PW = CPP * CH
NH, NKV, HD = 16, 4, 128
QG = NH // NKV * S
SB = 500
NSB = S2 // SB
F0 = 1024
FC0 = F0 // P
H1, D1 = 16, 16
HPG = 4
NG1 = H1 // HPG
GW = HPG * D1
BIG = 1.5 * 2.0 ** 23
E_LO, E_HI = math.exp(-50.0), math.exp(50.0)


def wait_for(eng, sem, value):
    if isinstance(value, int) and value <= 0:
        return
    eng.wait_ge(sem, value)


class Chain:

    def __init__(self, eng, sem, base=0):
        self.eng, self.sem, self.base, self.n = eng, sem, base, 0

    def link(self, ins):
        ins.then_inc(self.sem, 1)
        self.n += 1
        self.eng.wait_ge(self.sem, self.base + self.n)


def query_phase(nc, sem, keep, x_in, wq_in, bq_in, qw_in, kw_in, ident_in, q_scratch):
    with ExitStack() as ctx:
        sb = lambda name, shape, dt=F32: ctx.enter_context(nc.sbuf_tensor(name, shape, dt))
        x, ident, mhalf = keep["x"], keep["ident"], keep["mhalf"]
        wq = sb("wq", [P, KC, NH * HD])
        bq = sb("bq", [TT, NH * HD])
        qw = sb("qw", [P, 1])
        kw = sb("kw", [P, 1])
        qkw = sb("qkw", [P, 1])
        stats = sb("qa_stats", [TT, NT, 6])
        mv = sb("qa_mv", [TT, NT, 2])
        var = sb("qa_var", [TT, NT])
        rstd = sb("qa_rstd", [TT, NT])
        xn = sb("qa_xn", [TT, NT, H])
        xnT = sb("qa_xnT", [P, KC, T])
        q = sb("qa_q", [TT, NT, NH * HD])
        sq = sb("qa_sq", [TT, 2, 512])
        ssq = sb("qa_ssq", [TT, NT, NH])
        qvar = sb("qa_qvar", [TT, NT, NH])
        qr = sb("qa_qr", [TT, NT, NH])
        qT = sb("qa_qT", [P, 2, 2, NH, S])
        ps = [ctx.enter_context(nc.psum_tensor(f"qa_ps{i}", [P, 512], F32)) for i in range(8)]
        loaded_x, loaded_id, loaded_w, loaded_b = (sem(n) for n in (
            "a_x_loaded", "a_ident_loaded", "a_wq_loaded", "a_bias_norms_loaded"))
        dve_chain, var_ready, rstd_ready, xn_ready, xt_done, xt_copied = (sem(n) for n in (
            "a_dve_chain", "a_var_ready", "a_rstd_ready", "a_xn_ready", "a_xT_done", "a_xT_copied"))
        q_done, q_biased, q_squared, sq_reduced, qvar_ready, qr_ready, q_scaled = (sem(n) for n in (
            "a_q_done", "a_q_biased", "a_q_squared", "a_sq_reduced", "a_qvar_ready", "a_qr_ready", "a_q_scaled"))
        qt_done, qt_copied, mhalf_set = (sem(n) for n in ("a_qT_done", "a_qT_copied", "a_mhalf_set"))
        stored = [sem(f"a_qT_stored{i}") for i in range(2)]
        block = ctx.enter_context(nc.Block())

        @block.sync
        def _(sp):
            sp.dma_start(x[:, :, :], x_in.rearrange("(t p) h -> p t h", p=TT)).then_inc(loaded_x, 16)
            sp.dma_start(ident[:, :], ident_in).then_inc(loaded_id, 16)
            sp.dma_start(wq[:, :, :], wq_in.rearrange("(c p) n -> p c n", p=P)).then_inc(loaded_w, 16)
            sp.dma_start(bq[:, :], bq_in.partition_broadcast(TT)).then_inc(loaded_b, 16)
            sp.dma_start(qw[:, :], qw_in).then_inc(loaded_b, 16)
            sp.dma_start(kw[:, :], kw_in).then_inc(loaded_b, 16)
            for t in range(NT):
                sp.wait_ge(qt_copied, 4 * (t + 1))
                sp.dma_start(q_scratch[2 * t:2 * t + 2].rearrange("b p h s -> p b (h s)"),
                             qT[:, t % 2].rearrange("p b h s -> p b (h s)")).then_inc(stored[t % 2], 16)
            for i in range(2):
                sp.wait_ge(stored[i], 16 * (NT // 2))

        @block.gpsimd
        def _(pool):
            pool.memset(mhalf[:, :], -0.5).then_inc(mhalf_set, 1)
            pool.wait_ge(mhalf_set, 1)
            pool.wait_ge(var_ready, 1)
            pool.tensor_tensor(rstd[:, :], var[:, :], mhalf[:TT, 0:NT], ALU.pow).then_inc(rstd_ready, 1)
            for t in range(NT):
                pool.wait_ge(qvar_ready, t + 1)
                pool.tensor_tensor(qr[:, t, :], qvar[:, t, :], mhalf[:TT, 0:NH], ALU.pow).then_inc(qr_ready, 1)

        @block.scalar
        def _(act):
            for t in range(NT):
                act.wait_ge(xt_done, t + 1)
                act.copy(xnT[:, :, t * TT:(t + 1) * TT],
                         ps[t % 2][:, 0:KC * TT].rearrange("p (c s) -> p c s", c=KC)).then_inc(xt_copied, 1)
            for t in range(NT):
                for n in range(4):
                    k = 4 * t + n
                    act.wait_ge(q_biased, k + 1)
                    wait_for(act, sq_reduced, k - 1)
                    act.activation(sq[:, k % 2, :], q[:, t, n * 512:(n + 1) * 512], ACT.Square).then_inc(q_squared, 1)

        @block.tensor
        def _(pe):
            pe.wait_ge(loaded_id, 16)
            for t in range(NT):
                pe.wait_ge(xn_ready, t + 1)
                wait_for(pe, xt_copied, t - 1)
                for c in range(KC):
                    mm = pe.transpose(ps[t % 2][:, c * TT:(c + 1) * TT], xn[:, t, c * P:(c + 1) * P],
                                      ident[:TT, :TT])
                mm.then_inc(xt_done, 1)
            pe.wait_ge(loaded_w, 16)

            def heads_to_columns(t):
                pe.wait_ge(q_scaled, t + 1)
                for n in range(4):
                    k = 4 * t + n
                    wait_for(pe, qt_copied, k - 1)
                    for j in range(4):
                        h = 4 * n + j
                        mm = pe.transpose(ps[6 + k % 2][:, j * TT:(j + 1) * TT],
                                          q[:, t, h * HD:(h + 1) * HD], ident[:TT, :TT])
                    mm.then_inc(qt_done, 1)

            for t in range(NT):
                pe.wait_ge(xt_copied, t + 1)
                for n in range(4):
                    k = 4 * t + n
                    wait_for(pe, q_biased, k - 3)
                    for c in range(KC):
                        mm = pe.matmul(ps[2 + n][:TT, :], xnT[:, c, t * TT:(t + 1) * TT],
                                       wq[:, c, n * 512:(n + 1) * 512], start=c == 0, stop=c == KC - 1)
                    mm.then_inc(q_done, 1)
                if t:
                    heads_to_columns(t - 1)
            heads_to_columns(NT - 1)

        @block.vector
        def _(dve):
            ch = Chain(dve, dve_chain)
            dve.wait_ge(loaded_x, 16)
            for t in range(NT):
                last = dve.bn_stats(stats[:, t, :], x[:, t, :])
            ch.link(last)
            for t in range(NT):
                last = dve.bn_aggr(mv[:, t, :], stats[:, t, :])
            ch.link(last)
            dve.tensor_scalar(var[:, :], mv[:, :, 1], 1e-5, None, ALU.add).then_inc(var_ready, 1)
            dve.wait_ge(rstd_ready, 1)
            for t in range(NT):
                dve.tensor_scalar(xn[:, t, :], x[:, t, :], mv[:, t, 0:1], rstd[:, t:t + 1],
                                  ALU.subtract, ALU.mult).then_inc(xn_ready, 1)
            dve.wait_ge(loaded_b, 48)
            ch.link(dve.scalar_tensor_tensor(out=qkw[:, :], in0=qw[:, :], scalar=float(HD) ** -0.5, in1=kw[:, :],
                                             op0=ALU.mult, op1=ALU.mult))

            def columns_out(t):
                for n in range(4):
                    k = 4 * t + n
                    dve.wait_ge(qt_done, k + 1)
                    if t >= 2 and n == 0:
                        dve.wait_ge(stored[t % 2], 16 * (t // 2))
                    for bb in range(2):
                        src = ps[6 + k % 2][:, 0:4 * TT].rearrange("p (h b s) -> p b h s", h=4, b=2)[:, bb]
                        last = dve.tensor_scalar(qT[:, t % 2, bb, 4 * n:4 * n + 4, :], src, qkw[:, 0:1], None, ALU.mult)
                    last.then_inc(qt_copied, 1)

            for t in range(NT):
                for n in range(4):
                    k = 4 * t + n
                    dve.wait_ge(q_done, k + 1)
                    dve.tensor_tensor(q[:, t, n * 512:(n + 1) * 512], ps[2 + n][:TT, :],
                                      bq[:, n * 512:(n + 1) * 512], ALU.add).then_inc(q_biased, 1)
                for n in range(4):
                    k = 4 * t + n
                    dve.wait_ge(q_squared, k + 1)
                    dve.tensor_reduce(ssq[:, t, 4 * n:4 * n + 4],
                                      sq[:, k % 2, :].rearrange("p (h d) -> p h d", h=4),
                                      AX.X, ALU.add).then_inc(sq_reduced, 1)
                dve.wait_ge(sq_reduced, 4 * t + 4)
                dve.tensor_scalar(qvar[:, t, :], ssq[:, t, :], 1.0 / HD, 1e-6, ALU.mult, ALU.add).then_inc(qvar_ready, 1)
                if t:
                    columns_out(t - 1)
                dve.wait_ge(qr_ready, t + 1)
                heads = q[:, t, :].rearrange("p (h d) -> p h d", h=NH)
                dve.tensor_tensor(heads, heads, qr[:, t, :].unsqueeze(2).broadcast_to([TT, NH, HD]),
                                  ALU.mult).then_inc(q_scaled, 1)
            columns_out(NT - 1)


def attention0_phase(nc, sem, keep, ctx_in, mask_in, wk_in, bk_in, wv_in, bv_in, q_scratch, o_scratch):
    with ExitStack() as ctx:
        sb = lambda name, shape, dt=F32: ctx.enter_context(nc.sbuf_tensor(name, shape, dt))
        ident, mhalf = keep["ident"], keep["mhalf"]
        wkv = sb("b_wkv", [P, KC, 2, 512])
        whi = sb("b_whi", [P, KC, 2, 512], F32R)
        wlo = sb("b_wlo", [P, KC, 2, 512], F32R)
        bk = sb("b_bk", [CH, 512])
        bv = sb("b_bv", [P, NKV])
        mask = sb("b_mask", [TT, S2])
        raw = sb("b_ctx", [P, 2, KC, PW])
        chi = sb("b_ctx_hi", [P, 2, KC, PW], F32R)
        clo = sb("b_ctx_lo", [P, 2, KC, PW], F32R)
        ktok = sb("b_k_tok", [CH, 2, CPP, 512])
        ksq = sb("b_k_sq", [CH, 2, 512])
        kss = sb("b_k_ss", [CH, 2, CPP, NKV])
        kvar = sb("b_k_var", [CH, 2, CPP, NKV])
        kr = sb("b_k_r", [CH, 2, CPP, NKV])
        kT = [sb(f"b_kT{i}", [P, NKV, S2]) for i in range(2)]
        V = [sb(f"b_v{i}", [CH, NC, 512]) for i in range(2)]
        probs = [sb(f"b_probs{i}", [TT, S2]) for i in range(4)]
        pT = [sb(f"b_probsT{i}", [CH, 2, QG]) for i in range(2)]
        fence = sb("b_fence", [TT, 2 * NSB * PIECES])
        mx = sb("b_max", [TT, 2, 2, NSB])
        nmx = sb("b_neg_max", [TT, 2, 2])
        rs = sb("b_row_sum", [TT, 2, 2])
        rr = sb("b_row_recip", [TT, 2, 2])
        qcur = [sb(f"b_q{i}", [P, NH * S]) for i in range(2)]
        oT = sb("b_oT", [P, NH, 2, S])
        bank = lambda name: ctx.enter_context(nc.psum_tensor(name, [P, 512], F32))
        ps_s = [bank(f"b_ps_scores{i}") for i in range(3)]
        ps_k, ps_v = bank("b_ps_k"), bank("b_ps_v")
        ps_t = [bank(f"b_ps_T{i}") for i in range(2)]
        ps_o = bank("b_ps_o")
        w_loaded, misc_loaded, w_hi, w_lo = (sem(n) for n in ("b_w_loaded", "b_misc_loaded", "b_w_hi", "b_w_lo"))
        ctx_loaded = [sem(f"b_ctx_loaded{i}") for i in range(2)]
        q_loaded = [sem(f"b_q_loaded{i}") for i in range(2)]
        o_writable = sem("b_o_writable")
        ctx_hi, ctx_lo, k_done, v_done, k_biased, v_copied, k_squared, k_reduced = (sem(n) for n in (
            "b_ctx_hi", "b_ctx_lo", "b_k_done", "b_v_done", "b_k_biased", "b_v_copied", "b_k_squared", "b_k_reduced"))
        kvar_ready, kr_ready, k_scaled, kt_done, kt_copied = (sem(n) for n in (
            "b_kvar_ready", "b_kr_ready", "b_k_scaled", "b_kT_done", "b_kT_copied"))
        s_done, s_masked, max_ready, exp_done, recip_ready, p_ready, pt_done, pt_copied, o_done, o_copied = (
            sem(n) for n in ("b_scores_done", "b_scores_masked", "b_max_ready", "b_exp_done", "b_recip_ready",
                             "b_probs_ready", "b_pT_done", "b_pT_copied", "b_o_done", "b_o_copied"))
        block = ctx.enter_context(nc.Block())
        G = range(PIECES)

        def batches(eng, attend, project):
            project(0)
            with eng.Fori(0, B // 2 - 1) as i:
                for par in range(2):
                    attend(i * 2 + par, par, False, i)
            for par in range(2):
                attend(B - 2 + par, par, par == 1, B // 2 - 1)

        @block.sync
        def _(sp):
            sp.dma_start(wkv[:, :, 0, :], wk_in.rearrange("(c p) n -> p c n", p=P)).then_inc(w_loaded, 16)
            sp.dma_start(wkv[:, :, 1, :], wv_in.rearrange("(c p) n -> p c n", p=P)).then_inc(w_loaded, 16)

            def load(b, par):
                for g in G:
                    wait_for(sp, ctx_lo, 4 * b + g - 1)
                    sp.dma_start(raw[:, g % 2, :, :],
                                 ctx_in[b, :, g * PW:(g + 1) * PW].rearrange("(c p) s -> p c s", p=P)
                                 ).then_inc(ctx_loaded[g % 2], 16)

            def load_queries(b, par):
                sp.dma_start(qcur[par][:, :], q_scratch[b].rearrange("p h s -> p (h s)")).then_inc(q_loaded[par], 16)

            def project(_):
                sp.dma_start(bk[:, :], bk_in.partition_broadcast(CH)).then_inc(misc_loaded, 16)
                sp.dma_start(bv[:, :], bv_in).then_inc(o_writable, 16)
                for j in range(2):
                    sp.dma_start(mask[j * S:(j + 1) * S, :], mask_in).then_inc(misc_loaded, 16)
                load_queries(0, 0)
                load(0, 0)

            def attend(b, par, last, pair):
                if not last:
                    load(b + 1, 1 - par)
                    sp.wait_ge(s_done, b * 24 + 1)
                    load_queries(b + 1, 1 - par)
                if par == 1:
                    sp.wait_ge(o_copied, b * 4 + 4)
                    sp.dma_start(o_scratch[pair], oT[:, :, :, :].rearrange("p h b s -> p (h b s)")).then_inc(o_writable, 16)

            batches(sp, attend, project)
            sp.wait_ge(o_writable, 16 * (NT + 1))

        @block.gpsimd
        def _(pool):
            def normalise_keys(b, g):
                n = b * 4 + g
                pool.wait_ge(kvar_ready, n + 1)
                pool.tensor_tensor(kr[:, g % 2].rearrange("p c g -> p (c g)"),
                                   kvar[:, g % 2].rearrange("p c g -> p (c g)"),
                                   mhalf[:CH, 0:CPP * NKV], ALU.pow).then_inc(kr_ready, 1)
                pool.wait_ge(kr_ready, n + 1)
                for c in range(CPP):
                    heads = ktok[:, g % 2, c, :].rearrange("p (g d) -> p g d", g=NKV)
                    pool.tensor_tensor(heads, heads, kr[:, g % 2, c, :].unsqueeze(2).broadcast_to([CH, NKV, HD]),
                                       ALU.mult).then_inc(k_scaled, 1)

            def attend(b, par, last, pair):
                for g in G:
                    if not last:
                        normalise_keys(b + 1, g)

            batches(pool, attend, lambda _: [normalise_keys(0, g) for g in G])

        @block.scalar
        def _(act):
            act.wait_ge(w_loaded, 32)
            act.copy(whi[:, :, :, :], wkv[:, :, :, :]).then_inc(w_hi, 1)

            def split(b, g):
                act.wait_ge(ctx_loaded[g % 2], b * 32 + 16 * (g // 2 + 1))
                wait_for(act, v_done, (b * 4 + g - 1) * CPP)
                act.copy(chi[:, g % 2, :, :], raw[:, g % 2, :, :]).then_inc(ctx_hi, 1)

            def project(b, g, par):
                for c in range(CPP):
                    n = b * NC + g * CPP + c
                    act.wait_ge(k_biased, n + 1)
                    wait_for(act, k_reduced, n - 1)
                    act.activation(ksq[:, (g * CPP + c) % 2, :], ktok[:, g % 2, c, :], ACT.Square).then_inc(k_squared, 1)
                    act.wait_ge(v_done, n + 1)
                    act.copy(V[par][:, g * CPP + c, :], ps_v[:CH, :]).then_inc(v_copied, 1)

            def exps(b, g):
                for j in range(2):
                    n = b * 8 + 2 * g + j
                    act.wait_ge(max_ready, n + 1)
                    act.activation(probs[2 * (g % 2) + j][:, :], probs[2 * (g % 2) + j][:, :], ACT.Exp,
                                   bias=nmx[:, g % 2, j:j + 1], accum_out=rs[:, g % 2, j:j + 1]).then_inc(exp_done, 1)

            def probs_out(b, g):
                for r in range(NC // 2):
                    act.wait_ge(pt_done, b * 24 + g * 6 + r + 1)
                    act.copy(pT[r % 2][:, :, :], ps_t[r % 2][:CH, 0:2 * QG].rearrange("p (c q) -> p c q", c=2)
                             ).then_inc(pt_copied, 1)

            def first(_):
                for g in G:
                    split(0, g)
                    if g:
                        project(0, g - 1, 0)
                project(0, PIECES - 1, 0)

            def attend(b, par, last, pair):
                if not last:
                    split(b + 1, 0)
                exps(b, 0)
                if not last:
                    project(b + 1, 0, 1 - par)
                for g in range(1, PIECES):
                    if not last:
                        split(b + 1, g)
                    probs_out(b, g - 1)
                    exps(b, g)
                    if not last:
                        project(b + 1, g, 1 - par)
                probs_out(b, PIECES - 1)

            batches(act, attend, first)

        @block.tensor
        def _(pe):
            def project(b, g):
                pe.wait_ge(ctx_lo, b * 4 + g + 1)
                for c in range(CPP):
                    n = b * NC + g * CPP + c
                    for kv, bank_kv, freed, done in ((0, ps_k, k_biased, k_done), (1, ps_v, v_copied, v_done)):
                        wait_for(pe, freed, n)
                        m = 0
                        for kc in range(KC):
                            for a, w in ((chi, whi), (chi, wlo), (clo, whi)):
                                mm = pe.matmul(bank_kv[:CH, :], a[:, g % 2, kc, c * CH:(c + 1) * CH], w[:, kc, kv, :],
                                               start=m == 0, stop=m == 3 * KC - 1)
                                m += 1
                        mm.then_inc(done, 1)

            def keys_to_columns(b, g, probs_before):
                pe.wait_ge(k_scaled, (b * 4 + g + 1) * CPP)
                wait_for(pe, pt_copied, probs_before)
                for kv in range(NKV):
                    wait_for(pe, kt_copied, b * 16 + g * 4 + kv - 1)
                    for c in range(CPP):
                        mm = pe.transpose(ps_t[kv % 2][:, c * CH:(c + 1) * CH],
                                          ktok[:, g % 2, c, kv * HD:(kv + 1) * HD], ident[:CH, :CH])
                    mm.then_inc(kt_done, 1)

            def scores(b, g, par):
                for j in range(2):
                    for n in range(NSB):
                        m = 6 * g + 3 * j + n
                        if m >= 3:
                            pe.wait_ge(s_masked, b * 24 + m - 2)
                        pe.matmul(ps_s[m % 3][:TT, 0:SB], qcur[par][:, (2 * g + j) * TT:(2 * g + j + 1) * TT],
                                  kT[par][:, g, n * SB:(n + 1) * SB], start=True, stop=True).then_inc(s_done, 1)

            def values(b, g, par, keys_before):
                wait_for(pe, kt_copied, keys_before)
                pe.wait_ge(p_ready, b * 8 + 2 * g + 2)

                def product(r):
                    pe.wait_ge(pt_copied, b * 24 + g * 6 + r + 1)
                    for cc in range(2):
                        c = 2 * r + cc
                        mm = pe.matmul(ps_o[:, 0:QG], V[par][:, c, g * HD:(g + 1) * HD], pT[r % 2][:, cc, :],
                                       start=c == 0, stop=c == NC - 1)
                    return mm

                for r in range(NC // 2):
                    if r >= 2:
                        product(r - 2)
                    for cc in range(2):
                        for j in range(2):
                            c = 2 * r + cc
                            mm = pe.transpose(ps_t[r % 2][:CH, cc * QG + j * TT:cc * QG + (j + 1) * TT],
                                              probs[2 * (g % 2) + j][:, c * CH:(c + 1) * CH], ident[:TT, :TT])
                    mm.then_inc(pt_done, 1)
                product(NC // 2 - 2)
                product(NC // 2 - 1).then_inc(o_done, 1)

            def first(_):
                pe.wait_ge(w_lo, 1)
                project(0, 0)
                for g in range(1, PIECES):
                    project(0, g)
                    keys_to_columns(0, g - 1, 0)
                keys_to_columns(0, PIECES - 1, 0)

            def attend(b, par, last, pair):
                pe.wait_ge(kt_copied, b * 16 + 16)
                pe.wait_ge(q_loaded[par], (b - par) * 8 + 16)
                pe.wait_ge(v_copied, b * NC + NC)
                scores(b, 0, par)
                if not last:
                    project(b + 1, 0)
                for g in range(1, PIECES):
                    scores(b, g, par)
                    values(b, g - 1, par, (b + 1) * 16 + (g - 1) * 4 if not last else 0)
                    if not last:
                        keys_to_columns(b + 1, g - 1, b * 24 + g * 6)
                        project(b + 1, g)
                values(b, PIECES - 1, par, (b + 1) * 16 + 12 if not last else 0)
                if not last:
                    keys_to_columns(b + 1, PIECES - 1, b * 24 + 24)

            batches(pe, attend, first)

        @block.vector
        def _(dve):
            dve.wait_ge(w_hi, 1)
            dve.tensor_tensor(wlo[:, :, :, :], wkv[:, :, :, :], whi.bitcast(F32)[:, :, :, :], ALU.subtract).then_inc(w_lo, 1)

            def split(b, g):
                dve.wait_ge(ctx_hi, b * 4 + g + 1)
                dve.tensor_tensor(clo[:, g % 2, :, :], raw[:, g % 2, :, :], chi.bitcast(F32)[:, g % 2, :, :],
                                  ALU.subtract).then_inc(ctx_lo, 1)

            def reduce_squares(b, g, c):
                n = b * NC + g * CPP + c
                dve.wait_ge(k_squared, n + 1)
                dve.tensor_reduce(kss[:, g % 2, c, :],
                                  ksq[:, (g * CPP + c) % 2, :].rearrange("p (g d) -> p g d", g=NKV),
                                  AX.X, ALU.add).then_inc(k_reduced, 1)

            def keys(b, g, before_reduce=None):
                for c in range(CPP):
                    n = b * NC + g * CPP + c
                    dve.wait_ge(k_done, n + 1)
                    dve.tensor_tensor(ktok[:, g % 2, c, :], ps_k[:CH, :], bk[:, :], ALU.add).then_inc(k_biased, 1)
                    if c:
                        reduce_squares(b, g, c - 1)
                    if c < 2 and before_reduce:
                        before_reduce(c)

            def key_norms(b, g):
                reduce_squares(b, g, CPP - 1)
                dve.wait_ge(k_reduced, b * NC + (g + 1) * CPP)
                dve.tensor_scalar(kvar[:, g % 2], kss[:, g % 2], 1.0 / HD, 1e-6, ALU.mult, ALU.add).then_inc(kvar_ready, 1)

            def key_columns(b, g, par):
                for kv in range(NKV):
                    dve.wait_ge(kt_done, b * 16 + g * 4 + kv + 1)
                    dve.tensor_copy(kT[par][:, kv, g * PW:(g + 1) * PW], ps_t[kv % 2][:, 0:PW]).then_inc(kt_copied, 1)

            def masks(b, g):
                for j in range(2):
                    for n in range(NSB):
                        m = 6 * g + 3 * j + n
                        dve.wait_ge(s_done, b * 24 + m + 1)
                        dve.memset(fence[:, m:m + 1], 0.0)
                        dve.tensor_tensor_reduce(out=probs[2 * (g % 2) + j][:, n * SB:(n + 1) * SB],
                                                 in0=ps_s[m % 3][:TT, 0:SB], in1=mask[:, n * SB:(n + 1) * SB],
                                                 scale=1.0, scalar=-3.0e38, op0=ALU.add, op1=ALU.max,
                                                 accum_out=mx[:, g % 2, j, n:n + 1]).then_inc(s_masked, 1)
                    dve.wait_ge(s_masked, b * 24 + 6 * g + 3 * j + 3)
                    dve.tensor_reduce(nmx[:, g % 2, j:j + 1], mx[:, g % 2, j, :], AX.X, ALU.max,
                                      negate=True).then_inc(max_ready, 1)

            def normalise(b, g, tiles=range(2)):
                for j in tiles:
                    n = b * 8 + 2 * g + j
                    dve.wait_ge(exp_done, n + 1)
                    dve.reciprocal(rr[:, g % 2, j:j + 1], rs[:, g % 2, j:j + 1]).then_inc(recip_ready, 1)
                    dve.wait_ge(recip_ready, n + 1)
                    p = probs[2 * (g % 2) + j]
                    dve.tensor_scalar(p[:, :], p[:, :], rr[:, g % 2, j:j + 1], None, ALU.mult).then_inc(p_ready, 1)

            def attend_and_keys(b, g, last):
                if last:
                    normalise(b, g)
                else:
                    keys(b + 1, g, lambda j: normalise(b, g, [j]))

            def outputs(b, g, par):
                dve.wait_ge(o_done, b * 4 + g + 1)
                if g == 0 and par == 0:
                    dve.wait_ge(o_writable, b * 8 + 16)
                dve.tensor_scalar(oT[:, g * NH // NKV:(g + 1) * NH // NKV, par, :],
                                  ps_o[:, 0:QG].rearrange("p (h s) -> p h s", s=S), bv[:, g:g + 1], None,
                                  ALU.add).then_inc(o_copied, 1)

            def first(_):
                split(0, 0)
                dve.wait_ge(misc_loaded, 48)
                for g in G:
                    if g + 1 < PIECES:
                        split(0, g + 1)
                    keys(0, g)
                    key_norms(0, g)
                    if g:
                        key_columns(0, g - 1, 0)
                key_columns(0, PIECES - 1, 0)

            def attend(b, par, last, pair):
                if not last:
                    split(b + 1, 0)
                masks(b, 0)
                attend_and_keys(b, 0, last)
                for g in range(1, PIECES):
                    if not last:
                        split(b + 1, g)
                    masks(b, g)
                    if not last:
                        key_norms(b + 1, g - 1)
                    outputs(b, g - 1, par)
                    if not last:
                        key_columns(b + 1, g - 1, 1 - par)
                    attend_and_keys(b, g, last)
                if not last:
                    key_norms(b + 1, PIECES - 1)
                outputs(b, PIECES - 1, par)
                if not last:
                    key_columns(b + 1, PIECES - 1, 1 - par)

            batches(dve, attend, first)


def layer_norm(dve, ch, x, stats, mv, var, var_ready, rstd_ready, rstd, out, out_ready, base):
    for t in range(NT):
        last = dve.bn_stats(stats[:, t, :], x[:, t, :])
    ch.link(last)
    for t in range(NT):
        last = dve.bn_aggr(mv[:, t, :], stats[:, t, :])
    ch.link(last)
    dve.tensor_scalar(var[:, :], mv[:, :, 1], 1e-5, None, ALU.add).then_inc(var_ready, 1)
    dve.wait_ge(rstd_ready, base + 1)
    for t in range(NT):
        dve.tensor_scalar(out[:, t, :], x[:, t, :], mv[:, t, 0:1], rstd[:, t:t + 1],
                          ALU.subtract, ALU.mult).then_inc(out_ready, 1)


def ffn0_phase(nc, sem, keep, o_scratch, wo_in, gates_in, identb_in, had_in, wg_in, wu_in, wd_in, wq1_in, bq1_in):
    with ExitStack() as ctx:
        sb = lambda name, shape, dt=F32: ctx.enter_context(nc.sbuf_tensor(name, shape, dt))
        x, ident, mhalf, gate = keep["x"], keep["ident"], keep["mhalf"], keep["gate"]
        q1T = keep["q1T"]
        oT = sb("c_oT", [P, NT, NH, TT])
        wo = sb("c_wo", [P, NH, H])
        w_raw = sb("c_w_raw", [P, 3, 2048])
        w3 = sb("c_w_ternary", [P, 3, 2048], BF16)
        wabs = sb("c_w_abs", [P, 4])
        wmean = sb("c_w_mean", [P, 4])
        wscale = sb("c_w_scale", [P, 4])
        ones = sb("c_ones", [P, P])
        gate_raw = sb("c_gate_raw", [P, 4])
        identb = sb("c_identb", [P, P], BF16)
        identf = sb("c_had", [P, P])
        stats = sb("c_stats", [TT, NT, 6])
        mv = sb("c_mv", [TT, NT, 2])
        var = sb("c_var", [TT, NT])
        rstd = sb("c_rstd", [TT, NT])
        xn = sb("c_xn", [TT, NT, H])
        amax = sb("c_amax", [TT, 2, NT])
        arec = sb("c_arec", [TT, 2, NT])
        ascale = sb("c_ascale", [TT, 2, NT])
        deq = sb("c_deq", [TT, 3, NT])
        xq_t = sb("c_xq_t", [TT, NT, H])
        xq = sb("c_xq", [TT, NT, H], BF16)
        xqT = sb("c_xqT", [P, NT, KC, TT], BF16)
        sg = sb("c_silu", [TT, NT, 2, 512])
        inter = sb("c_inter", [TT, NT, F0])
        iT = sb("c_interT", [P, NT, FC0, TT])
        u = [sb(f"c_had{i}", [TT, NT, FC0, P]) for i in range(1)]
        zq = sb("c_zq", [TT, NT, F0], BF16)
        zT = sb("c_zT", [P, NT, FC0, TT], BF16)
        xnT = sb("c_xnT", [P, KC, T])
        wq1 = sb("c_wq1", [P, KC, H])
        bq1 = sb("c_bq1", [P, KC])
        ps = [ctx.enter_context(nc.psum_tensor(f"c_ps{i}", [P, 512], F32)) for i in range(8)]
        o_loaded = [sem(f"c_o_loaded{t}") for t in range(NT)]
        (wo_loaded, w_loaded, c_loaded, gates_loaded) = (sem(n) for n in (
            "c_wo_loaded", "c_w_loaded", "c_others_loaded", "c_gates_loaded"))
        (chain, ones_set, gate_ready, wabs_ready, wsum_done, w_ready, wo_done) = (sem(n) for n in (
            "c_chain", "c_ones_set", "c_gate_ready", "c_wabs_ready", "c_wsum_done", "c_w_ready", "c_wo_done"))
        (var_ready, rstd_ready, xn_ready, xq_ready, xqt_done, xqt_copied, gu_done, silu_done, inter_ready) = (
            sem(n) for n in ("c_var_ready", "c_rstd_ready", "c_xn_ready", "c_xq_ready", "c_xqT_done", "c_xqT_copied",
                             "c_gate_up_done", "c_silu_done", "c_inter_ready"))
        (it_done, it_copied, had_done, had_copied, zq_ready, zt_done, zt_copied, down_done, xnt_done, xnt_copied,
         q1_done, q1_copied) = (sem(n) for n in (
            "c_interT_done", "c_interT_copied", "c_had_done", "c_had_copied", "c_zq_ready", "c_zT_done",
            "c_zT_copied", "c_down_done", "c_xnT_done", "c_xnT_copied", "c_q1_done", "c_q1_copied"))
        block = ctx.enter_context(nc.Block())

        @block.sync
        def _(sp):
            sp.dma_start(wo[:, :, :], wo_in.rearrange("(h d) n -> d h n", d=HD)).then_inc(wo_loaded, 16)
            for t in range(NT):
                sp.dma_start(oT[:, t], o_scratch[t].rearrange("p (h s) -> p h s", h=NH)).then_inc(o_loaded[t], 16)
                if t == 0:
                    sp.dma_start(gate_raw[:, :], gates_in.partition_broadcast(P)).then_inc(gates_loaded, 16)
            for n, w in enumerate((wg_in, wu_in, wd_in)):
                sp.dma_start(w_raw[:, n, :].rearrange("p (c n) -> p c n", n=w.shape[1]),
                             w.rearrange("(c p) n -> p c n", p=P)).then_inc(w_loaded, 16)
            sp.dma_start(identb[:, :], identb_in).then_inc(c_loaded, 16)
            sp.dma_start(identf[:, :], had_in).then_inc(c_loaded, 16)
            sp.dma_start(wq1[:, :, :], wq1_in.rearrange("(c p) n -> p c n", p=P)).then_inc(c_loaded, 16)
            sp.dma_start(bq1[:, :], bq1_in).then_inc(c_loaded, 16)

        @block.gpsimd
        def _(pool):
            pool.memset(ones[:, :], 1.0).then_inc(ones_set, 1)
            for n in range(2):
                pool.wait_ge(var_ready, n + 1)
                pool.tensor_tensor(rstd[:, :], var[:, :], mhalf[:TT, 0:NT], ALU.pow).then_inc(rstd_ready, 1)

        @block.scalar
        def _(act):
            act.wait_ge(gates_loaded, 16)
            act.activation(gate[:, :], gate_raw[:, :], ACT.Tanh).then_inc(gate_ready, 1)
            for t in range(NT):
                act.wait_ge(xqt_done, t + 1)
                act.copy(xqT[:, t, :, :], ps[2 * t].bitcast(BF16)[:, 0:KC * TT].rearrange("p (c s) -> p c s", c=KC)
                         ).then_inc(xqt_copied, 1)
            for n in range(2):
                for t in range(NT):
                    act.wait_ge(gu_done, n * NT + t + 1)
                    act.activation(sg[:, t, n, :], ps[2 * t][:TT, :], ACT.Silu,
                                   scale=deq[:, 0, t:t + 1]).then_inc(silu_done, 1)
            for t in range(NT):
                for n in range(2):
                    act.wait_ge(it_done, 2 * t + n + 1)
                    act.copy(iT[:, t, 4 * n:4 * n + 4, :],
                             ps[2 * t + n][:, 0:4 * TT].rearrange("p (c s) -> p c s", c=4)).then_inc(it_copied, 1)
            for t in range(NT):
                for n in range(2):
                    act.wait_ge(had_done, 2 * t + n + 1)
                    act.mul(u[0][:, t, 4 * n:4 * n + 4, :].rearrange("p c d -> p (c d)"), ps[2 * t + n][:TT, :],
                            float(F0) ** -0.5).then_inc(had_copied, 1)
            for t in range(NT):
                act.wait_ge(zt_done, t + 1)
                act.copy(zT[:, t, :, :], ps[2 * t].bitcast(BF16)[:, 0:FC0 * TT].rearrange("p (c s) -> p c s", c=FC0)
                         ).then_inc(zt_copied, 1)
            for t in range(NT):
                act.wait_ge(xnt_done, t + 1)
                act.copy(xnT[:, :, t * TT:(t + 1) * TT], ps[2 * t][:, 0:KC * TT].rearrange("p (c s) -> p c s", c=KC)
                         ).then_inc(xnt_copied, 1)

        @block.tensor
        def _(pe):
            pe.wait_ge(wo_loaded, 16)
            for t in range(NT):
                pe.wait_ge(o_loaded[t], 16)
                for h in range(NH):
                    mm = pe.matmul(ps[2 * t][:TT, 0:H], oT[:, t, h, :], wo[:, h, :],
                                   start=h == 0, stop=h == NH - 1)
                mm.then_inc(wo_done, 1)
            pe.wait_ge(ones_set, 1)
            pe.wait_ge(wabs_ready, 1)
            pe.matmul(ps[7][:, 0:3], ones[:, :], wabs[:, 0:3], start=True, stop=True).then_inc(wsum_done, 1)
            pe.wait_ge(c_loaded, 64)
            for t in range(NT):
                pe.wait_ge(xq_ready, t + 1)
                for c in range(KC):
                    mm = pe.transpose(ps[2 * t].bitcast(BF16)[:, c * TT:(c + 1) * TT], xq[:, t, c * P:(c + 1) * P],
                                      identb[:TT, :TT])
                mm.then_inc(xqt_done, 1)
            pe.wait_ge(w_ready, 2)
            for n in range(2):
                for t in range(NT):
                    if n == 0:
                        pe.wait_ge(xqt_copied, t + 1)
                    else:
                        pe.wait_ge(inter_ready, t + 1)
                    for k in range(2):
                        for c in range(KC):
                            mm = pe.matmul(ps[2 * t + k][:TT, :], xqT[:, t, c, :],
                                           w3[:, k, c * F0 + n * 512:c * F0 + (n + 1) * 512],
                                           start=c == 0, stop=c == KC - 1)
                    mm.then_inc(gu_done, 1)
            for t in range(NT):
                pe.wait_ge(inter_ready, NT + t + 1)
                for n in range(2):
                    for j in range(4):
                        c = 4 * n + j
                        mm = pe.transpose(ps[2 * t + n][:, j * TT:(j + 1) * TT], inter[:, t, c * P:(c + 1) * P],
                                          ident[:TT, :TT])
                    mm.then_inc(it_done, 1)
            for t in range(NT):
                pe.wait_ge(it_copied, 2 * t + 2)
                for n in range(2):
                    for j in range(4):
                        mm = pe.matmul(ps[2 * t + n][:TT, j * P:(j + 1) * P], iT[:, t, 4 * n + j, :], identf[:, :],
                                       start=True, stop=True)
                    mm.then_inc(had_done, 1)
            for t in range(NT):
                pe.wait_ge(zq_ready, t + 1)
                for c in range(FC0):
                    mm = pe.transpose(ps[2 * t].bitcast(BF16)[:, c * TT:(c + 1) * TT], zq[:, t, c * P:(c + 1) * P],
                                      identb[:TT, :TT])
                mm.then_inc(zt_done, 1)
            pe.wait_ge(w_ready, 3)
            for t in range(NT):
                pe.wait_ge(zt_copied, t + 1)
                for c in range(FC0):
                    mm = pe.matmul(ps[2 * t + 1][:TT, 0:H], zT[:, t, c, :], w3[:, 2, c * H:(c + 1) * H],
                                   start=c == 0, stop=c == FC0 - 1)
                mm.then_inc(down_done, 1)
            for t in range(NT):
                pe.wait_ge(xn_ready, NT + t + 1)
                for c in range(KC):
                    mm = pe.transpose(ps[2 * t][:, c * TT:(c + 1) * TT], xn[:, t, c * P:(c + 1) * P], ident[:TT, :TT])
                mm.then_inc(xnt_done, 1)
            pe.wait_ge(xnt_copied, NT)
            for o in range(KC):
                for c in range(KC):
                    mm = pe.matmul(ps[2 * o][:, 0:T], wq1[:, c, o * P:(o + 1) * P], xnT[:, c, :],
                                   start=c == 0, stop=c == KC - 1)
                mm.then_inc(q1_done, 1)

        @block.vector
        def _(dve):
            ch = Chain(dve, chain)
            dve.wait_ge(gate_ready, 1)
            for t in range(NT):
                if t == NT - 1:
                    dve.wait_ge(w_loaded, 48)
                    dve.tensor_reduce(wabs[:, 0:3], w_raw[:, :, :], AX.X, ALU.add, apply_absolute_value=True
                                      ).then_inc(wabs_ready, 1)
                dve.wait_ge(wo_done, t + 1)
                last = dve.scalar_tensor_tensor(out=x[:, t, :], in0=ps[2 * t][:TT, 0:H], scalar=gate[:TT, 0:1],
                                                in1=x[:, t, :], op0=ALU.mult, op1=ALU.add)
            ch.link(last)
            layer_norm(dve, ch, x, stats, mv, var, var_ready, rstd_ready, rstd, xn, xn_ready, 0)

            def scales(n, src):
                for t in range(NT):
                    last = dve.tensor_reduce(amax[:, n, t:t + 1], src(t), AX.X, ALU.max, apply_absolute_value=True)
                ch.link(last)
                ch.link(dve.tensor_scalar(amax[:, n, :], amax[:, n, :], 1e-5, None, ALU.max))
                ch.link(dve.reciprocal(arec[:, n, :], amax[:, n, :]))
                ch.link(dve.tensor_scalar(ascale[:, n, :], arec[:, n, :], 128.0, None, ALU.mult))

            dve.wait_ge(xn_ready, NT)
            scales(0, lambda t: xn[:, t, :])
            for t in range(NT):
                last = dve.tensor_scalar(xq_t[:, t, :], xn[:, t, :], ascale[:, 0, t:t + 1], BIG, ALU.mult, ALU.add)
            ch.link(last)
            for t in range(NT):
                dve.tensor_scalar(xq[:, t, :], xq_t[:, t, :], BIG, 127.0, ALU.subtract, ALU.min).then_inc(xq_ready, 1)
            dve.wait_ge(wsum_done, 1)
            ch.link(dve.tensor_scalar(wmean[:, 0:3], ps[7][:, 0:3], 1.0 / (F0 * H), 1e-5, ALU.mult, ALU.max))
            ch.link(dve.reciprocal(wscale[:, 0:3], wmean[:, 0:3]))
            for k in range(2):
                last = dve.tensor_scalar(deq[:, k, :], amax[:, 0, :], 1.0 / 128, wmean[:TT, k:k + 1], ALU.mult, ALU.mult)
            ch.link(last)
            for k in range(3):
                ch.link(dve.tensor_scalar(w_raw[:, k, :], w_raw[:, k, :], wscale[:, k:k + 1], BIG, ALU.mult, ALU.add))
                ch.link(dve.tensor_scalar(w_raw[:, k, :], w_raw[:, k, :], BIG, 1.0, ALU.subtract, ALU.min))
                dve.tensor_scalar(w3[:, k, :], w_raw[:, k, :], -1.0, None, ALU.max).then_inc(w_ready, 1)
            for n in range(2):
                for t in range(NT):
                    dve.wait_ge(silu_done, n * NT + t + 1)
                    dve.scalar_tensor_tensor(out=inter[:, t, n * 512:(n + 1) * 512], in0=ps[2 * t + 1][:TT, :],
                                             scalar=deq[:, 1, t:t + 1], in1=sg[:, t, n, :],
                                             op0=ALU.mult, op1=ALU.mult).then_inc(inter_ready, 1)
            for t in range(NT):
                dve.wait_ge(had_copied, 2 * t + 2)
                a, b = u[0][:, t], inter[:, t, :].rearrange("p (c d) -> p c d", d=P)
                for w in (4, 2, 1):
                    av, bv_ = (v.rearrange("p (g two w) d -> p g two (w d)", two=2, w=w) for v in (a, b))
                    dve.tensor_tensor(bv_[:, :, 0], av[:, :, 0], av[:, :, 1], ALU.add)
                    ch.link(dve.tensor_tensor(bv_[:, :, 1], av[:, :, 0], av[:, :, 1], ALU.subtract))
                    a, b = b, a
            scales(1, lambda t: inter[:, t, :])
            ch.link(dve.tensor_scalar(deq[:, 2, :], amax[:, 1, :], 1.0 / 128, wmean[:TT, 2:3], ALU.mult, ALU.mult))
            ch.link(dve.tensor_scalar(deq[:, 2, :], deq[:, 2, :], gate[:TT, 2:3], None, ALU.mult))
            for t in range(NT):
                last = dve.tensor_scalar(u[0][:, t].rearrange("p c d -> p (c d)"), inter[:, t, :],
                                         ascale[:, 1, t:t + 1], BIG, ALU.mult, ALU.add)
            ch.link(last)
            for t in range(NT):
                dve.tensor_scalar(zq[:, t, :], u[0][:, t].rearrange("p c d -> p (c d)"), BIG, 127.0,
                                  ALU.subtract, ALU.min).then_inc(zq_ready, 1)
            for t in range(NT):
                dve.wait_ge(down_done, t + 1)
                last = dve.scalar_tensor_tensor(out=x[:, t, :], in0=ps[2 * t + 1][:TT, 0:H], scalar=deq[:, 2, t:t + 1],
                                                in1=x[:, t, :], op0=ALU.mult, op1=ALU.add)
            ch.link(last)
            layer_norm(dve, ch, x, stats, mv, var, var_ready, rstd_ready, rstd, xn, xn_ready, 1)
            dve.wait_ge(c_loaded, 64)
            for o in range(KC):
                dve.wait_ge(q1_done, o + 1)
                dve.tensor_scalar(q1T[:, o, :], ps[2 * o][:, 0:T], bq1[:, o:o + 1], None, ALU.add).then_inc(q1_copied, 1)
            dve.wait_ge(q1_copied, KC)


def attention1_phase(nc, sem, keep, ctx_in, mask_in, wk_in, bk_in, wv_in, bv_in, eye8_in, eye4_in):
    with ExitStack() as ctx:
        sb = lambda name, shape, dt=F32: ctx.enter_context(nc.sbuf_tensor(name, shape, dt))
        q1T, o1T = keep["q1T"], keep["o1T"]
        PC1, CP1 = 3, 4
        W1 = CP1 * CH
        HW = 8 * S
        VW = GW + 2
        STEPS = 2 * NC
        HALF_AT = (0, 4, 8, 12, 16, 20)
        RECIPS = ((0, 2), (2, 4), (4, 6), (6, 7), (7, 8))
        AHEAD = 3
        wkv = sb("d_wkv", [P, 2, KC, H])
        whi = sb("d_whi", [P, 2, KC, H], F32R)
        wlo = sb("d_wlo", [P, 2, KC, H], F32R)
        bk = sb("d_bk", [P, KC])
        bv = sb("d_bv", [GW, NG1])
        eye8 = sb("d_eye8", [P, 8])
        eye4 = sb("d_eye4", [GW, HPG])
        mask_i = sb("d_mask_i", [CH, B, NC], I32)
        att = sb("d_attend", [CH, B, NC])
        e_scale = sb("d_exp_scale", [CH, B, NC])
        e_bias = sb("d_exp_bias", [CH, B, NC])
        esc = sb("d_exp_scale_now", [CH, 2, NC])
        ebi = sb("d_exp_bias_now", [CH, 2, NC])
        raw = sb("d_ctx", [P, 2, KC, W1])
        chi = sb("d_ctx_hi", [P, 2, KC, W1], F32R)
        clo = sb("d_ctx_lo", [P, 2, KC, W1], F32R)
        k_hi = [sb(f"d_kT_hi{i}", [P, KC, S2], F32R) for i in range(2)]
        k_lo = [sb(f"d_kT_lo{i}", [P, KC, S2], F32R) for i in range(2)]
        v_hi = [sb(f"d_v_hi{i}", [CH, NC, NG1, VW], F32R) for i in range(2)]
        v_lo = [sb(f"d_v_lo{i}", [CH, NC, NG1, VW], F32R) for i in range(2)]
        q1_hi = sb("d_q1_hi", [P, KC, T], F32R)
        q1_lo = sb("d_q1_lo", [P, KC, T])
        q_hi = [sb(f"d_q_hi{i}", [P, 2, 8, S], F32R) for i in range(2)]
        q_lo = [sb(f"d_q_lo{i}", [P, 2, 8, S], F32R) for i in range(2)]
        p = [sb(f"d_p{i}", [CH, HW]) for i in range(3)]
        p_hi = [sb(f"d_p_hi{i}", [CH, HW], F32R) for i in range(3)]
        p_lo = [sb(f"d_p_lo{i}", [CH, HW], F32R) for i in range(3)]
        ones = sb("d_ones", [P, GW])
        consts = sb("d_one_zero", [CH, 2, NC * NG1])
        den = sb("d_den", [P, NG1, HPG * S])
        o_m = sb("d_o_masked", [GW, NG1, HPG, S])
        d_m = sb("d_den_masked", [GW, NG1, HPG, S])
        dsum = sb("d_sums", [GW, NG1, T])
        bank = lambda name: ctx.enter_context(nc.psum_tensor(name, [P, 512], F32))
        ps_s = [bank(f"d_ps_s{i}") for i in range(4)]
        ps_r = [ps_s[2], ps_s[3]]
        ps_k, ps_v = bank("d_ps_k"), bank("d_ps_v")
        ps_o = [bank(f"d_ps_o{i}") for i in range(2)]
        w_loaded, m_loaded, w_hi, w_lo, prep, now_ready, q_ready, chain = (sem(n) for n in (
            "d_w_loaded", "d_misc_loaded", "d_w_hi", "d_w_lo", "d_prepared", "d_now_ready", "d_q_ready", "d_chain"))
        ctx_loaded = [sem(f"d_ctx_loaded{i}") for i in range(2)]
        (ctx_hi, ctx_lo, k_done, khi_ready, k_split, v_done, vhi_ready, v_split, s_done, exp_done, p_clipped, phi_ready,
         p_ready) = (sem(n) for n in (
            "d_ctx_hi", "d_ctx_lo", "d_k_done", "d_k_hi_ready", "d_k_split", "d_v_done", "d_v_hi_ready", "d_v_split",
            "d_s_done", "d_exp_done", "d_p_clipped", "d_p_hi_ready", "d_p_ready"))
        o_free, den_copied, r_done, r_free, o_ready, ones_set, consts_set = (sem(n) for n in (
            "d_o_masked", "d_den_copied", "d_den_spread", "d_den_masked", "d_o_ready", "d_ones_set", "d_consts_set"))
        p_used, prep0, recip_ready = sem("d_p_used"), sem("d_mask_read"), sem("d_recip_ready")
        block = ctx.enter_context(nc.Block())
        POST = 5

        def batches(eng, attend, first):
            first()
            with eng.Fori(0, B // 2 - 1) as i:
                for par in range(2):
                    attend(i * 2 + par, par, False)
            for par in range(2):
                attend(B - 2 + par, par, par == 1)

        def slot(par, pc):
            return (PC1 * par + pc) % 2

        @block.sync
        def _(sp):
            for k, w in enumerate((wk_in, wv_in)):
                sp.dma_start(wkv[:, k], w.rearrange("(c p) n -> p c n", p=P)).then_inc(w_loaded, 16)

            def load(b, par):
                for pc in range(PC1):
                    wait_for(sp, ctx_lo, PC1 * b + pc - 1)
                    sp.dma_start(raw[:, slot(par, pc)],
                                 ctx_in[b, :, pc * W1:(pc + 1) * W1].rearrange("(c p) s -> p c s", p=P)
                                 ).then_inc(ctx_loaded[slot(par, pc)], 16)
                    if isinstance(b, int) and b == 0 and pc == 0:
                        for dst, src in ((bk, bk_in), (bv, bv_in), (eye8, eye8_in), (eye4, eye4_in)):
                            sp.dma_start(dst[:, :], src).then_inc(m_loaded, 16)
                        sp.dma_start(mask_i[:, :, :], mask_in).then_inc(m_loaded, 16)

            def attend(b, par, last):
                if not last:
                    load(b + 1, 1 - par)

            batches(sp, attend, lambda: load(0, 0))

        @block.gpsimd
        def _(pool):
            pool.memset(ones[:, :], 1.0).then_inc(ones_set, 1)
            pool.memset(o_m[:, :, :, :], 0.0).then_inc(o_ready, 1)
            pool.memset(consts[:, 0, :], 1.0).then_inc(consts_set, 1)
            pool.memset(consts[:, 1, :], 0.0).then_inc(consts_set, 1)
            pool.wait_ge(consts_set, 2)
            for i in range(2):
                for k, v in enumerate((v_hi, v_lo)):
                    for j in range(VW - GW):
                        pool.tensor_copy(v[i][:, :, :, GW + j], consts[:, k, :].rearrange("p (c g) -> p c g", c=NC)
                                         ).then_inc(ones_set, 1)
            pool.wait_ge(prep, 1)

            def now(b, par):
                if not (isinstance(b, int) and b == 0):
                    pool.wait_ge(exp_done, (b - 1) * STEPS + 1)
                pool.tensor_copy(esc[:, par, :], e_scale[:, b, :])
                pool.tensor_copy(ebi[:, par, :], e_bias[:, b, :]).then_inc(now_ready, 1)

            def finish(ch, n):
                b0, b1 = RECIPS[n]
                cols = slice(b0 * S, b1 * S)
                pool.wait_ge(recip_ready, n + 1)
                ch.link(pool.tensor_tensor(o1T[:, :, cols], o1T[:, :, cols], dsum[:, :, cols], ALU.mult))
                ch.link(pool.tensor_tensor(o1T[:, :, cols], o1T[:, :, cols],
                                           bv[:, :].unsqueeze(2).broadcast_to([GW, NG1, (b1 - b0) * S]), ALU.add))

            def attend(b, par, last):
                if not last:
                    now(b + 1, 1 - par)
                ch = Chain(pool, chain, b * POST)
                if last:
                    for n in range(len(RECIPS) - 1):
                        finish(ch, n)
                for m, free in ((o_m, o_free), (d_m, r_free)):
                    pool.wait_ge(free, b * 2 + 4)
                    pool.tensor_tensor(m[:, :, 0, :], m[:, :, 0, :], m[:, :, 1, :], ALU.add)
                    ch.link(pool.tensor_tensor(m[:, :, 2, :], m[:, :, 2, :], m[:, :, 3, :], ALU.add))
                    ch.link(pool.tensor_tensor(m[:, :, 0, :], m[:, :, 0, :], m[:, :, 2, :], ALU.add))
                pool.tensor_copy(o1T[:, :, bass.ds(b * S, S)], o_m[:, :, 0, :])
                ch.link(pool.tensor_scalar(d_m[:, :, 1, :], d_m[:, :, 0, :], 1e-8, None, ALU.mult))
                pool.tensor_tensor(dsum[:, :, bass.ds(b * S, S)], d_m[:, :, 1, :], d_m[:, :, 0, :],
                                   ALU.add).then_inc(o_ready, 1)
                pool.wait_ge(o_ready, b + 2)
                if last:
                    finish(ch, len(RECIPS) - 1)

            batches(pool, attend, lambda: now(0, 0))

        @block.scalar
        def _(act):
            act.wait_ge(w_loaded, 32)
            act.copy(whi[:, :, :, :], wkv[:, :, :, :]).then_inc(w_hi, 1)

            def split(b, par, pc):
                s = slot(par, pc)
                act.wait_ge(ctx_loaded[s], (b - par) * 24 + 16 * ((PC1 * par + pc) // 2 + 1))
                wait_for(act, v_done, 2 * (PC1 * b + pc - 1))
                act.copy(chi[:, s], raw[:, s]).then_inc(ctx_hi, 1)

            def half_out(b, par, h):
                pc, half = h // 2, h % 2
                act.wait_ge(k_done, 6 * b + h + 1)
                act.activation(k_hi[par][:, half, pc * W1:(pc + 1) * W1], ps_k[:, 0:W1], ACT.Identity,
                               bias=bk[:, half:half + 1]).then_inc(khi_ready, 1)
                act.wait_ge(v_done, 6 * b + h + 1)
                act.copy(v_hi[par][:, 2 * h:2 * h + 2, :, 0:GW],
                         ps_v[:CH, :].rearrange("p (c g d) -> p c g d", c=2, g=NG1)).then_inc(vhi_ready, 1)

            def first():
                split(0, 0, 0)
                act.copy(q1_hi[:, :, :], q1T[:, :, :]).then_inc(w_hi, 1)
                act.wait_ge(m_loaded, 80)
                for pc in range(PC1):
                    if pc:
                        split(0, 0, pc)
                    half_out(0, 0, 2 * pc)
                    half_out(0, 0, 2 * pc + 1)

            def attend(b, par, last):
                if not last:
                    split(b + 1, 1 - par, 0)
                act.wait_ge(now_ready, b + 1)

                def high(v):
                    act.wait_ge(p_clipped, b * STEPS + v + 1)
                    if v >= 3:
                        act.wait_ge(p_used, b * STEPS + v - 2)
                    act.copy(p_hi[v % 3][:, :], p[v % 3][:, :]).then_inc(phi_ready, 1)

                for v in range(STEPS):
                    act.wait_ge(s_done, b * STEPS + v + 1)
                    if v >= 3:
                        act.wait_ge(p_ready, b * STEPS + v - 2)
                    act.activation(p[v % 3][:, :], ps_s[v % 4][:CH, 0:HW], ACT.Exp, bias=ebi[:, par, v // 2:v // 2 + 1],
                                   scale=esc[:, par, v // 2:v // 2 + 1]).then_inc(exp_done, 1)
                    if v >= 1:
                        high(v - 1)
                    if not last:
                        if v in (5, 13):
                            split(b + 1, 1 - par, (v + 3) // 8)
                        if v - AHEAD in HALF_AT and v < STEPS - 1:
                            half_out(b + 1, 1 - par, HALF_AT.index(v - AHEAD))
                high(STEPS - 1)
                if not last:
                    half_out(b + 1, 1 - par, 5)
                for k in range(2):
                    act.wait_ge(p_used, b * STEPS + STEPS)
                    act.copy(den[GW:GW + 1, 2 * k:2 * k + 2, :],
                             ps_o[k][GW:GW + 1, 0:HW].rearrange("p (g q) -> p g q", g=2)).then_inc(den_copied, 1)

            batches(act, attend, first)

        @block.tensor
        def _(pe):
            def project(b, par, h):
                pc, half = h // 2, h % 2
                s = slot(par, pc)
                n = 6 * b + h
                if half == 0:
                    pe.wait_ge(ctx_lo, PC1 * b + pc + 1)
                wait_for(pe, k_split, n)
                m = 0
                for c in range(KC):
                    for a, w in ((chi, whi), (chi, wlo), (clo, whi)):
                        mm = pe.matmul(ps_k[:, 0:W1], w[:, 0, c, half * P:(half + 1) * P], a[:, s, c, :],
                                       start=m == 0, stop=m == 3 * KC - 1)
                        m += 1
                mm.then_inc(k_done, 1)
                wait_for(pe, v_split, n)
                for cc in range(2):
                    ch_ = 2 * half + cc
                    m = 0
                    for c in range(KC):
                        for a, w in ((chi, whi), (chi, wlo), (clo, whi)):
                            mm = pe.matmul(ps_v[:CH, cc * H:(cc + 1) * H], a[:, s, c, ch_ * CH:(ch_ + 1) * CH],
                                           w[:, 1, c, :], start=m == 0, stop=m == 3 * KC - 1)
                            m += 1
                mm.then_inc(v_done, 1)

            def scores(b, par, v):
                c, half = v // 2, v % 2
                if v >= 4:
                    pe.wait_ge(exp_done, b * STEPS + v - 3)
                elif v >= 2:
                    pe.wait_ge(r_free, b * 2 + v - 1)
                for m, (k, q) in enumerate(((k_hi, q_hi), (k_hi, q_lo), (k_lo, q_hi))):
                    mm = pe.matmul(ps_s[v % 4][:CH, 0:HW], k[par][:, half, c * CH:(c + 1) * CH],
                                   q[par][:, half].rearrange("p h s -> p (h s)"), start=m == 0, stop=m == 2)
                mm.then_inc(s_done, 1)

            def values(b, par, v):
                c, half = v // 2, v % 2
                pe.wait_ge(p_ready, b * STEPS + v + 1)
                if c == 0:
                    pe.wait_ge(o_free, b * 2 + half + 1)
                for gg in range(2):
                    for m, (val, pr) in enumerate(((v_hi, p_hi), (v_hi, p_lo), (v_lo, p_hi))):
                        mm = pe.matmul(ps_o[half][:VW, gg * HPG * S:(gg + 1) * HPG * S], val[par][:, c, 2 * half + gg, :],
                                       pr[v % 3][:, gg * HPG * S:(gg + 1) * HPG * S],
                                       start=c == 0 and gg == 0 and m == 0, stop=c == NC - 1 and m == 2,
                                       skip_group_check=True)
                mm.then_inc(p_used, 1)

            def spread(b):
                pe.wait_ge(exp_done, b * STEPS + STEPS)
                pe.wait_ge(den_copied, b * 2 + 2)
                for k in range(2):
                    pe.matmul(ps_r[k][:GW, 0:HW], ones[GW:GW + 1, :], den[GW:GW + 1, 2 * k:2 * k + 2, :].rearrange("p g q -> p (g q)"),
                              start=True, stop=True).then_inc(r_done, 1)

            def first():
                pe.wait_ge(w_lo, 1)
                for h in range(6):
                    project(0, 0, h)
                pe.wait_ge(ones_set, 9)

            def attend(b, par, last):
                pe.wait_ge(k_split, 6 * b + 6)
                pe.wait_ge(v_split, 6 * b + 6)
                pe.wait_ge(q_ready, b + 1)
                for v in range(AHEAD):
                    scores(b, par, v)
                for v in range(STEPS):
                    if v + AHEAD < STEPS:
                        scores(b, par, v + AHEAD)
                    if v in HALF_AT and not last:
                        project(b + 1, 1 - par, HALF_AT.index(v))
                    values(b, par, v)
                spread(b)

            batches(pe, attend, first)

        @block.vector
        def _(dve):
            def split(b, par, pc):
                s = slot(par, pc)
                dve.wait_ge(ctx_hi, PC1 * b + pc + 1)
                dve.tensor_tensor(clo[:, s], raw[:, s], chi.bitcast(F32)[:, s], ALU.subtract).then_inc(ctx_lo, 1)

            def half_out(b, par, h):
                pc, half = h // 2, h % 2
                dve.wait_ge(khi_ready, 6 * b + h + 1)
                cols = slice(pc * W1, (pc + 1) * W1)
                dve.scalar_tensor_tensor(out=k_lo[par][:, half, cols], in0=ps_k[:, 0:W1], scalar=bk[:, half:half + 1],
                                         in1=k_hi[par].bitcast(F32)[:, half, cols],
                                         op0=ALU.add, op1=ALU.subtract).then_inc(k_split, 1)
                dve.wait_ge(vhi_ready, 6 * b + h + 1)
                dve.tensor_tensor(v_lo[par][:, 2 * h:2 * h + 2, :, 0:GW],
                                  ps_v[:CH, :].rearrange("p (c g d) -> p c g d", c=2, g=NG1),
                                  v_hi[par].bitcast(F32)[:, 2 * h:2 * h + 2, :, 0:GW], ALU.subtract).then_inc(v_split, 1)

            def queries(b, par):
                for q1, q in ((q1_hi.bitcast(F32), q_hi), (q1_lo, q_lo)):
                    for half in range(2):
                        last = dve.tensor_tensor(q[par][:, half],
                                                 q1[:, half, bass.ds(b * S, S)].unsqueeze(1).broadcast_to([P, 8, S]),
                                                 eye8[:, :].unsqueeze(2).broadcast_to([P, 8, S]), ALU.mult)
                last.then_inc(q_ready, 1)

            def first():
                dve.wait_ge(w_hi, 1)
                dve.tensor_tensor(wlo[:, :, :, :], wkv[:, :, :, :], whi.bitcast(F32)[:, :, :, :], ALU.subtract).then_inc(w_lo, 1)
                split(0, 0, 0)
                dve.wait_ge(m_loaded, 80)
                ch0 = Chain(dve, prep0)
                ch0.link(dve.tensor_scalar(att[:, :, :], mask_i[:, :, :], 0.5, None, ALU.is_gt))
                dve.tensor_scalar(e_scale[:, :, :], att[:, :, :], float(D1) ** -0.5, None, ALU.mult)
                dve.tensor_scalar(e_bias[:, :, :], att[:, :, :], 1.0, 50.0, ALU.subtract, ALU.mult).then_inc(prep, 1)
                dve.wait_ge(w_hi, 2)
                ch0.link(dve.tensor_tensor(q1_lo[:, :, :], q1T[:, :, :], q1_hi.bitcast(F32)[:, :, :], ALU.subtract))
                for h in range(6):
                    if h and h % 2 == 0:
                        split(0, 0, h // 2)
                    half_out(0, 0, h)
                queries(0, 0)
                dve.memset(d_m[:, 0, 0, 0:1], 0.0).then_inc(o_free, 2)
                dve.memset(d_m[:, 0, 0, 1:2], 0.0).then_inc(r_free, 2)

            def recip(n):
                cols = slice(RECIPS[n][0] * S, RECIPS[n][1] * S)
                dve.wait_ge(o_ready, RECIPS[n][1] + 1)
                dve.reciprocal(dsum[:, :, cols], dsum[:, :, cols]).then_inc(recip_ready, 1)

            def attend(b, par, last):
                if not last:
                    split(b + 1, 1 - par, 0)

                def low(v):
                    dve.wait_ge(phi_ready, b * STEPS + v + 1)
                    dve.tensor_tensor(p_lo[v % 3][:, :], p[v % 3][:, :], p_hi[v % 3].bitcast(F32)[:, :],
                                      ALU.subtract).then_inc(p_ready, 1)

                for v in range(STEPS):
                    dve.wait_ge(exp_done, b * STEPS + v + 1)
                    dve.tensor_scalar(p[v % 3][:, :], p[v % 3][:, :], E_LO, E_HI, ALU.max, ALU.min).then_inc(p_clipped, 1)
                    if v >= 1:
                        low(v - 1)
                    if last and v % 4 == 1 and v // 4 < 4:
                        recip(v // 4)
                    if not last:
                        if v in (5, 13):
                            split(b + 1, 1 - par, (v + 3) // 8)
                        if v - AHEAD in HALF_AT and v < STEPS - 1:
                            half_out(b + 1, 1 - par, HALF_AT.index(v - AHEAD))
                        if v == 9:
                            queries(b + 1, 1 - par)
                low(STEPS - 1)
                if not last:
                    half_out(b + 1, 1 - par, 5)
                dve.wait_ge(o_ready, b + 1)
                own4 = eye4[:, :].unsqueeze(2).broadcast_to([GW, HPG, S])
                for k in range(2):
                    dve.wait_ge(p_used, b * STEPS + STEPS)
                    for gg in range(2):
                        src = ps_o[k][:GW, gg * HPG * S:(gg + 1) * HPG * S].rearrange("p (j s) -> p j s", j=HPG)
                        ins = dve.tensor_tensor(o_m[:, 2 * k + gg], src, own4, ALU.mult)
                    ins.then_inc(o_free, 1)
                for k in range(2):
                    dve.wait_ge(r_done, b * 2 + k + 1)
                    for gg in range(2):
                        src = ps_r[k][:GW, gg * HPG * S:(gg + 1) * HPG * S].rearrange("p (j s) -> p j s", j=HPG)
                        ins = dve.tensor_tensor(d_m[:, 2 * k + gg], src, own4, ALU.mult)
                    ins.then_inc(r_free, 1)
                if last:
                    recip(len(RECIPS) - 1)

            batches(dve, attend, first)


def experts_phase(nc, sem, keep, wo_in, bo_in, gamma_in, beta_in, rs_in, rw_in, rb_in, w1_in, b1_in, w2_in, b2_in, out):
    NE = w1_in.shape[0]
    NR, NSH = rw_in.shape[1], w1_in.shape[0] - rw_in.shape[1]
    HH = w1_in.shape[2] // 2
    TOPK = 6
    RING = 4
    assert NE % RING == 2
    with ExitStack() as ctx:
        sb = lambda name, shape, dt=F32: ctx.enter_context(nc.sbuf_tensor(name, shape, dt))
        x, ident, mhalf, gate, o1T = (keep[n] for n in ("x", "ident", "mhalf", "gate", "o1T"))
        wo = sb("e_wo", [GW, NG1, H])
        bo = sb("e_bo", [TT, H])
        gamma = sb("e_gamma", [TT, H])
        beta = sb("e_beta", [TT, H])
        rs_raw = sb("e_rs_raw", [TT, 1])
        rs = sb("e_rs", [TT, 1])
        rw = sb("e_rw", [P, KC, NR])
        rb = sb("e_rb", [TT, NR])
        d = sb("e_delta", [TT, NT, H])
        fin = sb("e_finite", [TT, NT, H], I32)
        dn = sb("e_delta_norm", [TT, NT, H])
        stats = sb("e_stats", [TT, NT, 6])
        mv = sb("e_mv", [TT, NT, 2])
        var = sb("e_var", [TT, NT])
        rstd = sb("e_rstd", [TT, NT])
        xn = sb("e_xn", [TT, NT, H])
        xnT = sb("e_xnT", [P, KC, T])
        lg = sb("e_logits", [TT, NT, NR])
        nmx = sb("e_neg_max", [TT, NT])
        pr = sb("e_probs", [TT, NT, NR + 2])
        psum_ = sb("e_prob_sum", [TT, NT])
        prec = sb("e_prob_rec", [TT, NT])
        top = sb("e_top8", [TT, NT, 8])
        marked = sb("e_marked", [TT, NT, NR + 2])
        chosen = sb("e_chosen", [TT, NT, NR])
        gs = sb("e_gate_sum", [TT, NT])
        gr = sb("e_gate_rec", [TT, NT])
        g = sb("e_gates", [TT, NT, NE])
        gT = sb("e_gatesT", [NE, T])
        b2 = sb("e_b2", [NE, H])
        acc = sb("e_acc", [TT, NT, H])
        w1 = [sb(f"e_w1_{i}", [P, KC, 2 * HH]) for i in range(RING)]
        w2 = [sb(f"e_w2_{i}", [HH, 2, H]) for i in range(RING)]
        b1 = [sb(f"e_b1_{i}", [HH, 2]) for i in range(RING)]
        w1hi = [sb(f"e_w1hi_{i}", [P, KC, 2 * HH], F32R) for i in range(2)]
        w1lo = [sb(f"e_w1lo_{i}", [P, KC, 2 * HH], F32R) for i in range(2)]
        xhi = sb("e_xnT_hi", [P, KC, T], F32R)
        xlo = sb("e_xnT_lo", [P, KC, T], F32R)
        gcol = [sb(f"e_gcol{i}", [TT, NT]) for i in range(2)]
        hT = [sb(f"e_hT{i}", [HH, 2, T]) for i in range(2)]
        ps = [ctx.enter_context(nc.psum_tensor(f"e_ps{i}", [P, 512], F32)) for i in range(8)]
        (wo_loaded, ln_loaded, r_loaded, sent_set, var_ready, rstd_ready, xn_ready, wo_done, chain,
         xnt_done, xnt_copied, lg_done, max_ready, exp_done, gates_ready, gt_done, gt_copied, acc_done,
         x_ready, stored) = (sem("e_" + n) for n in (
            "wo_loaded", "ln_loaded", "router_loaded", "sentinels_set", "var_ready", "rstd_ready",
            "xn_ready", "wo_done", "chain", "xnT_done", "xnT_copied", "logits_done", "max_ready", "exp_done",
            "gates_ready", "gatesT_done", "gatesT_copied", "acc_done", "x_ready", "stored"))
        dn_ready = sem("e_delta_norm_ready")
        w_loaded = [sem(f"e_w_loaded{i}") for i in range(RING)]
        w_hi, w_lo, x_hi, x_lo = sem("e_w_hi"), sem("e_w_lo"), sem("e_x_hi"), sem("e_x_lo")
        gcol_ready, h_done, h_ready, y_done, y_added = (sem("e_" + n) for n in (
            "gcol_ready", "h_done", "h_ready", "y_done", "y_added"))
        block = ctx.enter_context(nc.Block())

        @block.sync
        def _(sp):
            sp.dma_start(wo[:, :, :], wo_in.rearrange("(g d) n -> d g n", d=GW)).then_inc(wo_loaded, 16)
            for dst, src in ((bo, bo_in), (gamma, gamma_in), (beta, beta_in), (rs_raw, rs_in)):
                sp.dma_start(dst[:, :], src.partition_broadcast(TT)).then_inc(ln_loaded, 16)
            sp.dma_start(rw[:, :, :], rw_in.rearrange("(c p) n -> p c n", p=P)).then_inc(r_loaded, 16)
            sp.dma_start(rb[:, :], rb_in.partition_broadcast(TT)).then_inc(r_loaded, 16)
            sp.dma_start(b2[:, :], b2_in).then_inc(r_loaded, 16)

            def load(e, slot):
                if not (isinstance(e, int) and e < RING):
                    sp.wait_ge(y_done, (e - RING) * 2 + 2)
                sp.dma_start(w1[slot][:, :, :], w1_in[e].rearrange("(c p) n -> p c n", p=P)).then_inc(w_loaded[slot], 16)
                sp.dma_start(w2[slot][:, :, :], w2_in[e].rearrange("(k d) n -> d k n", d=HH)).then_inc(w_loaded[slot], 16)
                sp.dma_start(b1[slot][:, :], b1_in[e]).then_inc(w_loaded[slot], 16)

            for e in range(RING):
                load(e, e)
            with sp.Fori(1, NE // RING) as i:
                for j in range(RING):
                    load(i * RING + j, j)
            for j in range(2):
                load(NE - 2 + j, j)
            for t in range(NT):
                sp.wait_ge(x_ready, t + 1)
                sp.dma_start(out[t * TT:(t + 1) * TT, :], x[:, t, :]).then_inc(stored, 16)
            sp.wait_ge(stored, 16 * NT)

        @block.gpsimd
        def _(pool):
            for k in range(2):
                pool.memset(pr[:, :, NR + k:NR + k + 1], -1.0 - k).then_inc(sent_set, 1)
            pool.memset(g[:, :, NR:], 1.0 / NSH).then_inc(sent_set, 1)
            for n in range(2):
                pool.wait_ge(var_ready, n + 1)
                pool.tensor_tensor(rstd[:, :], var[:, :], mhalf[:TT, 0:NT], ALU.pow).then_inc(rstd_ready, 1)
            pool.wait_ge(gates_ready, NT)

            def column(e, par):
                wait_for(pool, y_added, e * NT)
                pool.tensor_copy(gcol[par][:, :], g[:, :, bass.ds(e, 1)].rearrange("p t o -> p (t o)")).then_inc(gcol_ready, 1)

            for par in range(2):
                column(par, par)
            with pool.Fori(0, NE // 2 - 1) as i:
                for par in range(2):
                    column(i * 2 + 2 + par, par)

        @block.scalar
        def _(act):
            for t in range(NT):
                act.wait_ge(xnt_done, t + 1)
                act.copy(xnT[:, :, t * TT:(t + 1) * TT], ps[2 * t][:, 0:KC * TT].rearrange("p (c s) -> p c s", c=KC)
                         ).then_inc(xnt_copied, 1)
            act.wait_ge(xnt_copied, NT)
            act.copy(xhi[:, :, :], xnT[:, :, :]).then_inc(x_hi, 1)
            act.wait_ge(sent_set, 3)
            for t in range(NT):
                act.wait_ge(max_ready, t + 1)
                act.activation(pr[:, t, 0:NR], lg[:, t, :], ACT.Exp, bias=nmx[:, t:t + 1],
                               accum_out=psum_[:, t:t + 1]).then_inc(exp_done, 1)


            def split(e, slot):
                act.wait_ge(w_loaded[slot], (e - slot) * (48 // RING) + 48)
                act.copy(w1hi[slot % 2][:, :, :], w1[slot][:, :, :]).then_inc(w_hi, 1)

            def hidden(e, slot):
                for k in range(2):
                    act.wait_ge(h_done, e * 2 + k + 1)
                    act.activation(hT[slot % 2][:, k, :], ps[2 * (slot % 2) + k][:HH, 0:T], ACT.Relu,
                                   bias=b1[slot][:, k:k + 1]).then_inc(h_ready, 1)

            split(0, 0)
            split(1, 1)
            with act.Fori(0, NE // RING) as i:
                for j in range(RING):
                    hidden(i * RING + j, j)
                    split(i * RING + (j + 2), (j + 2) % RING)
            hidden(NE - 2, 0)
            hidden(NE - 1, 1)

        @block.tensor
        def _(pe):
            pe.wait_ge(wo_loaded, 16)
            for t in range(NT):
                for k in range(NG1):
                    mm = pe.matmul(ps[2 * t][:TT, 0:H], o1T[:, k, t * TT:(t + 1) * TT], wo[:, k, :],
                                   start=k == 0, stop=k == NG1 - 1)
                mm.then_inc(wo_done, 1)
            for t in range(NT):
                pe.wait_ge(xn_ready, t + 1)
                for c in range(KC):
                    mm = pe.transpose(ps[2 * t][:, c * TT:(c + 1) * TT], xn[:, t, c * P:(c + 1) * P], ident[:TT, :TT])
                mm.then_inc(xnt_done, 1)
            pe.wait_ge(r_loaded, 48)
            for t in range(NT):
                pe.wait_ge(xnt_copied, t + 1)
                for c in range(KC):
                    mm = pe.matmul(ps[2 * t + 1][:TT, 0:NR], xnT[:, c, t * TT:(t + 1) * TT], rw[:, c, :],
                                   start=c == 0, stop=c == KC - 1)
                mm.then_inc(lg_done, 1)
            for t in range(NT):
                pe.wait_ge(gates_ready, t + 1)
                pe.transpose(ps[2 * t][:NE, 0:TT], g[:, t, :], ident[:TT, :TT]).then_inc(gt_done, 1)
            for t in range(NT):
                pe.wait_ge(gt_copied, t + 1)
                pe.matmul(ps[2 * t + 1][:TT, 0:H], gT[:, t * TT:(t + 1) * TT], b2[:, :],
                          start=True, stop=True).then_inc(acc_done, 1)
            pe.wait_ge(y_added, NT)

            def hidden(e, slot):
                pe.wait_ge(w_lo, e + 1)
                for k in range(2):
                    m = 0
                    for c in range(KC):
                        for w, a in ((w1hi, xhi), (w1hi, xlo), (w1lo, xhi)):
                            mm = pe.matmul(ps[2 * (slot % 2) + k][:HH, 0:T], w[slot % 2][:, c, k * HH:(k + 1) * HH],
                                           a[:, c, :], start=m == 0, stop=m == 3 * KC - 1)
                            m += 1
                    mm.then_inc(h_done, 1)

            def outputs(e, slot):
                pe.wait_ge(h_ready, e * 2 + 2)
                for b in range(2):
                    wait_for(pe, y_added, e * NT)
                    for tt in range(2):
                        t = 2 * b + tt
                        for k in range(2):
                            mm = pe.matmul(ps[4 + 2 * (slot % 2) + b][:TT, tt * H:(tt + 1) * H],
                                           hT[slot % 2][:, k, t * TT:(t + 1) * TT], w2[slot][:, k, :],
                                           start=k == 0, stop=k == 1)
                    mm.then_inc(y_done, 1)

            pe.wait_ge(x_lo, 1)
            hidden(0, 0)
            hidden(1, 1)
            outputs(0, 0)
            with pe.Fori(0, NE // RING) as i:
                for j in range(RING):
                    hidden(i * RING + (j + 2), (j + 2) % RING)
                    outputs(i * RING + (j + 1), (j + 1) % RING)
            outputs(NE - 1, 1)

        @block.vector
        def _(dve):
            ch = Chain(dve, chain)
            dve.wait_ge(ln_loaded, 64)
            ch.link(dve.tensor_scalar(rs[:, :], rs_raw[:, :], 0.0, 0.3, ALU.max, ALU.min))
            for t in range(NT):
                dve.wait_ge(wo_done, t + 1)
                last = dve.tensor_tensor(d[:, t, :], ps[2 * t][:TT, 0:H], bo[:, :], ALU.add)
            ch.link(last)
            ch.link(dve.tensor_tensor(fin[:, :, :], d[:, :, :], d[:, :, :], ALU.is_equal))
            ch.link(dve.memset(dn[:, :, :], 0.0))
            ch.link(dve.copy_predicated(dn[:, :, :], fin[:, :, :], d[:, :, :]))
            for sign in (1.0, -1.0):
                ch.link(dve.tensor_scalar(fin[:, :, :], dn[:, :, :], sign * 3.4028235e38, None,
                                          ALU.is_gt if sign > 0 else ALU.is_lt))
                ch.link(dve.memset(d[:, :, :], sign * 1e4))
                ch.link(dve.copy_predicated(dn[:, :, :], fin[:, :, :], d[:, :, :]))
            ch.link(dve.tensor_scalar(d[:, :, :], dn[:, :, :], rs[:, 0:1], None, ALU.mult))
            layer_norm(dve, ch, d, stats, mv, var, var_ready, rstd_ready, rstd, dn, dn_ready, 0)
            dve.wait_ge(dn_ready, NT)
            bc = lambda v: v[:, :].unsqueeze(1).broadcast_to([TT, NT, H])
            ch.link(dve.tensor_tensor(dn[:, :, :], dn[:, :, :], bc(gamma), ALU.mult))
            ch.link(dve.tensor_tensor(dn[:, :, :], dn[:, :, :], bc(beta), ALU.add))
            ch.link(dve.scalar_tensor_tensor(out=x[:, :, :], in0=dn[:, :, :], scalar=gate[:TT, 1:2], in1=x[:, :, :],
                                             op0=ALU.mult, op1=ALU.add))
            layer_norm(dve, ch, x, stats, mv, var, var_ready, rstd_ready, rstd, xn, xn_ready, 1)
            dve.wait_ge(x_hi, 1)
            dve.tensor_tensor(xlo[:, :, :], xnT[:, :, :], xhi.bitcast(F32)[:, :, :], ALU.subtract).then_inc(x_lo, 1)
            dve.wait_ge(r_loaded, 48)
            for t in range(NT):
                dve.wait_ge(lg_done, t + 1)
                last = dve.tensor_tensor(lg[:, t, :], ps[2 * t + 1][:TT, 0:NR], rb[:, :], ALU.add)
            ch.link(last)
            for t in range(NT):
                dve.tensor_reduce(nmx[:, t:t + 1], lg[:, t, :], AX.X, ALU.max, negate=True).then_inc(max_ready, 1)
            dve.wait_ge(exp_done, NT)
            ch.link(dve.reciprocal(prec[:, :], psum_[:, :]))
            for t in range(NT):
                last = dve.tensor_scalar(pr[:, t, 0:NR], pr[:, t, 0:NR], prec[:, t:t + 1], None, ALU.mult)
            ch.link(last)
            for t in range(NT):
                last = dve.max(top[:, t, :], pr[:, t, 0:NR])
            ch.link(last)
            for k in range(8 - TOPK):
                last = dve.memset(top[:, :, TOPK + k:TOPK + k + 1], -1.0 - k)
            ch.link(last)
            for t in range(NT):
                last = dve.match_replace(marked[:, t, :], top[:, t, :], pr[:, t, :], -5.0)
            ch.link(last)
            ch.link(dve.tensor_scalar(chosen[:, :, :], marked[:, :, 0:NR], -5.0, None, ALU.is_equal))
            ch.link(dve.tensor_tensor(chosen[:, :, :], chosen[:, :, :], pr[:, :, 0:NR], ALU.mult))
            ch.link(dve.tensor_reduce(gs[:, :], chosen[:, :, :], AX.X, ALU.add))
            ch.link(dve.reciprocal(gr[:, :], gs[:, :]))
            for t in range(NT):
                dve.tensor_scalar(g[:, t, 0:NR], chosen[:, t, :], gr[:, t:t + 1], None, ALU.mult).then_inc(gates_ready, 1)
            for t in range(NT):
                dve.wait_ge(gt_done, t + 1)
                dve.tensor_copy(gT[:, t * TT:(t + 1) * TT], ps[2 * t][:NE, 0:TT]).then_inc(gt_copied, 1)
            for t in range(NT):
                dve.wait_ge(acc_done, t + 1)
                dve.tensor_copy(acc[:, t, :], ps[2 * t + 1][:TT, 0:H]).then_inc(y_added, 1)

            def split(e, slot):
                dve.wait_ge(w_hi, e + 1)
                dve.tensor_tensor(w1lo[slot % 2][:, :, :], w1[slot][:, :, :], w1hi[slot % 2].bitcast(F32)[:, :, :],
                                  ALU.subtract).then_inc(w_lo, 1)

            def add(e, slot):
                dve.wait_ge(gcol_ready, e + 1)
                dve.wait_ge(y_added, e * NT + NT)
                for t in range(NT):
                    if t % 2 == 0:
                        dve.wait_ge(y_done, e * 2 + t // 2 + 1)
                    dve.scalar_tensor_tensor(out=acc[:, t, :],
                                             in0=ps[4 + 2 * (slot % 2) + t // 2][:TT, (t % 2) * H:(t % 2 + 1) * H],
                                             scalar=gcol[slot % 2][:, t:t + 1], in1=acc[:, t, :],
                                             op0=ALU.mult, op1=ALU.add).then_inc(y_added, 1)

            split(0, 0)
            split(1, 1)
            with dve.Fori(0, NE // RING) as i:
                for j in range(RING):
                    split(i * RING + (j + 2), (j + 2) % RING)
                    add(i * RING + j, j)
            add(NE - 2, 0)
            add(NE - 1, 1)
            dve.wait_ge(y_added, NE * NT + NT)
            for t in range(NT):
                dve.scalar_tensor_tensor(out=x[:, t, :], in0=acc[:, t, :], scalar=gate[:TT, 3:4], in1=x[:, t, :],
                                         op0=ALU.mult, op1=ALU.add).then_inc(x_ready, 1)


def flamingo_program(nc, a, out):
    with ExitStack() as ctx:
        names = set()

        def sem(name):
            assert name not in names
            names.add(name)
            return ctx.enter_context(nc.semaphore(name))

        sb = lambda name, shape, dt=F32: ctx.enter_context(nc.sbuf_tensor(name, shape, dt))
        keep = {
            "x": sb("x", [TT, NT, H]),
            "ident": sb("ident", [P, P]),
            "mhalf": sb("minus_half", [P, 48]),
            "gate": sb("gate", [P, 4]),
        }
        q_scratch = nc.dram_tensor("q_scratch", [B, P, NH, S], F32).ap()
        o_scratch = nc.dram_tensor("o_scratch", [NT, P, NH * TT], F32).ap()
        query_phase(nc, sem, keep, a["x"], a["L0_xattn_Wq"], a["L0_xattn_bq"], a["L0_xattn_qn_w"],
                    a["L0_xattn_kn_w"], a["ident"], q_scratch)
        attention0_phase(nc, sem, keep, a["ctxT"], a["mask_f"], a["L0_xattn_Wk"], a["L0_xattn_bk"],
                         a["L0_xattn_Wv"], a["L0_xattn_bv"], q_scratch, o_scratch)
        keep["q1T"] = sb("q1T", [P, KC, T])
        keep["o1T"] = sb("o1T", [GW, NG1, T])
        ffn0_phase(nc, sem, keep, o_scratch, a["L0_xattn_Wo"], a["gates"], a["ident_b"], a["hadamard"],
                   a["L0_ffn_w_gateT"], a["L0_ffn_w_upT"], a["L0_ffn_w_downT"], a["L1_xattn_WqT"], a["L1_xattn_bq"])
        attention1_phase(nc, sem, keep, a["ctxT"], a["mask_i"], a["L1_xattn_WkT"], a["L1_xattn_bk"],
                         a["L1_xattn_WvT"], a["L1_xattn_bv"], a["eye8"], a["eye4"])
        experts_phase(nc, sem, keep, a["L1_xattn_WoT"], a["L1_xattn_bo"], a["L1_xattn_ln_gamma"],
                      a["L1_xattn_ln_beta"], a["L1_xattn_residual_scale"], a["L1_ffn_router_w"],
                      a["L1_ffn_router_b"], a["L1_ffn_w1"], a["L1_ffn_b1"], a["L1_ffn_w2"], a["L1_ffn_b2"], out)


def laid_out(i):
    import numpy as np

    i = {k: np.asarray(v) for k, v in i.items()}
    a = {
        "x": i["x"].reshape(T, H),
        "ctxT": i["ctx_2048"].transpose(0, 2, 1),
        "mask_f": i["mask_1xSxS2_ff0"][0],
        "mask_i": i["mask_BxS2_ik0"].reshape(B, NC, CH).transpose(2, 0, 1),
        "gates": np.concatenate([i["g_xattn"], i["g_ffn"]]),
    }
    for n in ("Wq", "bq", "Wk", "bk", "Wv", "Wo"):
        a["L0_xattn_" + n] = i["L0_xattn_" + n]
    a["L0_xattn_bv"] = i["L0_xattn_bv"].reshape(NKV, HD).T
    for n in ("qn_w", "kn_w"):
        a["L0_xattn_" + n] = i["L0_xattn_" + n].reshape(HD, 1)
    for n in ("w_gate", "w_up", "w_down"):
        a["L0_ffn_" + n + "T"] = i["L0_ffn_" + n].T
    for n in ("Wq", "Wk", "Wv", "Wo"):
        a["L1_xattn_" + n + "T"] = i["L1_xattn_" + n].T
    for n in ("bq", "bk"):
        a["L1_xattn_" + n] = i["L1_xattn_" + n].reshape(KC, P).T
    a["L1_xattn_bv"] = i["L1_xattn_bv"].reshape(NG1, GW).T
    for n in ("bo", "ln_gamma", "ln_beta"):
        a["L1_xattn_" + n] = i["L1_xattn_" + n]
    a["L1_xattn_residual_scale"] = i["L1_xattn_residual_scale"].reshape(1)
    a["L1_ffn_router_w"] = i["L1_ffn_router_w"]
    a["L1_ffn_router_b"] = i["L1_ffn_router_b"]
    for n in ("w1", "b1", "w2", "b2"):
        a["L1_ffn_" + n] = np.concatenate([i["L1_ffn_r" + n], i["L1_ffn_s" + n]])
    b1 = a["L1_ffn_b1"]
    a["L1_ffn_b1"] = b1.reshape(b1.shape[0], 2, b1.shape[1] // 2).transpose(0, 2, 1)
    a["ident"] = np.eye(P, dtype=np.float32)
    a["ident_b"] = np.eye(P, dtype=mybir.dt.np(BF16))
    a["eye8"] = np.kron(np.eye(8, dtype=np.float32), np.ones((D1, 1), np.float32))
    a["eye4"] = np.kron(np.eye(HPG, dtype=np.float32), np.ones((D1, 1), np.float32))
    had = np.ones((1, 1), np.float32)
    while had.shape[0] < P:
        had = np.block([[had, had], [had, -had]])
    a["hadamard"] = had.astype(np.float32)
    return {"in_" + k: np.ascontiguousarray(v) for k, v in a.items()}


def kernel(**inputs):
    import numpy as np
    import concourse.bacc as bacc
    from concourse.bass_utils import run_bass_kernel_spmd

    nc = bacc.Bacc("TRN2", target_bir_lowering=False, num_devices=1)
    arrays = laid_out(inputs)
    a = {k[3:]: nc.dram_tensor(k, v.shape, mybir.dt.from_np(v.dtype), kind="ExternalInput").ap()
         for k, v in arrays.items()}
    out = nc.dram_tensor("out", (T, H), F32, kind="ExternalOutput").ap()
    flamingo_program(nc, a, out)
    r = run_bass_kernel_spmd(nc, [arrays], core_ids=[0])
    return r.results[0]["out"].reshape(B, S, H)
```

```python
import math
from contextlib import ExitStack

import concourse.bass as bass
from concourse import mybir

ALU = mybir.AluOpType
ACT = mybir.ActivationFunctionType
AX = mybir.AxisListType
F32 = mybir.dt.float32
F32R = mybir.dt.float32r
BF16 = mybir.dt.bfloat16
I32 = mybir.dt.int32

B, S, H = 8, 56, 256
S2 = 1500
T = B * S
P = 128
KC = H // P
TT = 2 * S
NT = T // TT
CH = 125
NC = S2 // CH
PIECES = 4
CPP = NC // PIECES
PW = CPP * CH
NH, NKV, HD = 16, 4, 128
QG = NH // NKV * S
SB = 500
NSB = S2 // SB
F0 = 1024
FC0 = F0 // P
H1, D1 = 16, 16
HPG = 4
NG1 = H1 // HPG
GW = HPG * D1
BIG = 1.5 * 2.0 ** 23
E_LO, E_HI = math.exp(-50.0), math.exp(50.0)


def wait_for(eng, sem, value):
    if isinstance(value, int) and value <= 0:
        return
    eng.wait_ge(sem, value)


class Chain:

    def __init__(self, eng, sem, base=0):
        self.eng, self.sem, self.base, self.n = eng, sem, base, 0

    def link(self, ins):
        ins.then_inc(self.sem, 1)
        self.n += 1
        self.eng.wait_ge(self.sem, self.base + self.n)


def query_phase(nc, sem, keep, nxt, x_in, wq_in, bq_in, qw_in, kw_in, ident_in, q_scratch):
    with ExitStack() as ctx:
        sb = lambda name, shape, dt=F32: ctx.enter_context(nc.sbuf_tensor(name, shape, dt))
        x, ident, mhalf = keep["x"], keep["ident"], keep["mhalf"]
        wq = sb("wq", [P, KC, NH * HD])
        bq = sb("bq", [TT, NH * HD])
        qw = sb("qw", [P, 1])
        kw = sb("kw", [P, 1])
        qkw = sb("qkw", [P, 1])
        stats = sb("qa_stats", [TT, NT, 6])
        mv = sb("qa_mv", [TT, NT, 2])
        var = sb("qa_var", [TT, NT])
        rstd = sb("qa_rstd", [TT, NT])
        xn = sb("qa_xn", [TT, NT, H])
        xnT = sb("qa_xnT", [P, KC, T])
        q = sb("qa_q", [TT, NT, NH * HD])
        sq = sb("qa_sq", [TT, 2, 512])
        ssq = sb("qa_ssq", [TT, NT, NH])
        qvar = sb("qa_qvar", [TT, NT, NH])
        qr = sb("qa_qr", [TT, NT, NH])
        qT = sb("qa_qT", [P, 2, 2, NH, S])
        ps = [ctx.enter_context(nc.psum_tensor(f"qa_ps{i}", [P, 512], F32)) for i in range(8)]
        loaded_x, loaded_id, loaded_w, loaded_b = (sem(n) for n in (
            "a_x_loaded", "a_ident_loaded", "a_wq_loaded", "a_bias_norms_loaded"))
        dve_chain, var_ready, rstd_ready, xn_ready, xt_done, xt_copied = (sem(n) for n in (
            "a_dve_chain", "a_var_ready", "a_rstd_ready", "a_xn_ready", "a_xT_done", "a_xT_copied"))
        q_done, q_biased, q_squared, sq_reduced, qvar_ready, qr_ready, q_scaled = (sem(n) for n in (
            "a_q_done", "a_q_biased", "a_q_squared", "a_sq_reduced", "a_qvar_ready", "a_qr_ready", "a_q_scaled"))
        qt_done, qt_copied, mhalf_set = (sem(n) for n in ("a_qT_done", "a_qT_copied", "a_mhalf_set"))
        stored = [sem(f"a_qT_stored{i}") for i in range(2)]
        block = ctx.enter_context(nc.Block())

        @block.sync
        def _(sp):
            sp.dma_start(x[:, :, :], x_in.rearrange("(t p) h -> p t h", p=TT)).then_inc(loaded_x, 16)
            sp.dma_start(ident[:, :], ident_in).then_inc(loaded_id, 16)
            sp.dma_start(wq[:, :, :], wq_in.rearrange("(c p) n -> p c n", p=P)).then_inc(loaded_w, 16)
            sp.dma_start(bq[:, :], bq_in.partition_broadcast(TT)).then_inc(loaded_b, 16)
            sp.dma_start(qw[:, :], qw_in).then_inc(loaded_b, 16)
            sp.dma_start(kw[:, :], kw_in).then_inc(loaded_b, 16)
            nxt["load"](sp)
            for t in range(NT):
                sp.wait_ge(qt_copied, 4 * (t + 1))
                sp.dma_start(q_scratch[2 * t:2 * t + 2].rearrange("b p h s -> p b (h s)"),
                             qT[:, t % 2].rearrange("p b h s -> p b (h s)")).then_inc(stored[t % 2], 16)
            for i in range(2):
                sp.wait_ge(stored[i], 16 * (NT // 2))

        @block.gpsimd
        def _(pool):
            pool.memset(mhalf[:, :], -0.5).then_inc(mhalf_set, 1)
            pool.wait_ge(mhalf_set, 1)
            pool.wait_ge(var_ready, 1)
            pool.tensor_tensor(rstd[:, :], var[:, :], mhalf[:TT, 0:NT], ALU.pow).then_inc(rstd_ready, 1)
            for t in range(NT):
                pool.wait_ge(qvar_ready, t + 1)
                pool.tensor_tensor(qr[:, t, :], qvar[:, t, :], mhalf[:TT, 0:NH], ALU.pow).then_inc(qr_ready, 1)
                pool.wait_ge(qr_ready, t + 1)
                for n in range(4):
                    heads = q[:, t, n * 512:(n + 1) * 512].rearrange("p (h d) -> p h d", h=4)
                    pool.tensor_tensor(heads, heads, qr[:, t, 4 * n:4 * n + 4].unsqueeze(2).broadcast_to([TT, 4, HD]),
                                       ALU.mult).then_inc(q_scaled, 1)

        @block.scalar
        def _(act):
            for t in range(NT):
                act.wait_ge(xt_done, t + 1)
                act.copy(xnT[:, :, t * TT:(t + 1) * TT],
                         ps[t % 2][:, 0:KC * TT].rearrange("p (c s) -> p c s", c=KC)).then_inc(xt_copied, 1)
            for t in range(NT):
                for n in range(4):
                    k = 4 * t + n
                    act.wait_ge(q_biased, k + 1)
                    wait_for(act, sq_reduced, k - 1)
                    act.activation(sq[:, k % 2, :], q[:, t, n * 512:(n + 1) * 512], ACT.Square).then_inc(q_squared, 1)
            nxt["split_high"](act)

        @block.tensor
        def _(pe):
            pe.wait_ge(loaded_id, 16)
            for t in range(NT):
                pe.wait_ge(xn_ready, t + 1)
                wait_for(pe, xt_copied, t - 1)
                for c in range(KC):
                    mm = pe.transpose(ps[t % 2][:, c * TT:(c + 1) * TT], xn[:, t, c * P:(c + 1) * P],
                                      ident[:TT, :TT])
                mm.then_inc(xt_done, 1)
            pe.wait_ge(loaded_w, 16)

            def heads_to_columns(t):
                for n in range(4):
                    k = 4 * t + n
                    pe.wait_ge(q_scaled, k + 1)
                    wait_for(pe, qt_copied, k - 1)
                    for j in range(4):
                        h = 4 * n + j
                        mm = pe.transpose(ps[6 + k % 2][:, j * TT:(j + 1) * TT],
                                          q[:, t, h * HD:(h + 1) * HD], ident[:TT, :TT])
                    mm.then_inc(qt_done, 1)

            for t in range(NT):
                pe.wait_ge(xt_copied, t + 1)
                for n in range(4):
                    k = 4 * t + n
                    wait_for(pe, q_biased, k - 3)
                    for c in range(KC):
                        mm = pe.matmul(ps[2 + n][:TT, :], xnT[:, c, t * TT:(t + 1) * TT],
                                       wq[:, c, n * 512:(n + 1) * 512], start=c == 0, stop=c == KC - 1)
                    mm.then_inc(q_done, 1)
                if t:
                    heads_to_columns(t - 1)
            heads_to_columns(NT - 1)

        @block.vector
        def _(dve):
            ch = Chain(dve, dve_chain)
            dve.wait_ge(loaded_x, 16)
            for t in range(NT):
                last = dve.bn_stats(stats[:, t, :], x[:, t, :])
            ch.link(last)
            for t in range(NT):
                last = dve.bn_aggr(mv[:, t, :], stats[:, t, :])
            ch.link(last)
            dve.tensor_scalar(var[:, :], mv[:, :, 1], 1e-5, None, ALU.add).then_inc(var_ready, 1)
            dve.wait_ge(rstd_ready, 1)
            for t in range(NT):
                dve.tensor_scalar(xn[:, t, :], x[:, t, :], mv[:, t, 0:1], rstd[:, t:t + 1],
                                  ALU.subtract, ALU.mult).then_inc(xn_ready, 1)
            dve.wait_ge(loaded_b, 48)
            ch.link(dve.scalar_tensor_tensor(out=qkw[:, :], in0=qw[:, :], scalar=float(HD) ** -0.5, in1=kw[:, :],
                                             op0=ALU.mult, op1=ALU.mult))

            def columns_out(t):
                for n in range(4):
                    k = 4 * t + n
                    dve.wait_ge(qt_done, k + 1)
                    if t >= 2 and n == 0:
                        dve.wait_ge(stored[t % 2], 16 * (t // 2))
                    for bb in range(2):
                        src = ps[6 + k % 2][:, 0:4 * TT].rearrange("p (h b s) -> p b h s", h=4, b=2)[:, bb]
                        last = dve.tensor_scalar(qT[:, t % 2, bb, 4 * n:4 * n + 4, :], src, qkw[:, 0:1], None, ALU.mult)
                    last.then_inc(qt_copied, 1)

            for t in range(NT):
                for n in range(4):
                    k = 4 * t + n
                    dve.wait_ge(q_done, k + 1)
                    dve.tensor_tensor(q[:, t, n * 512:(n + 1) * 512], ps[2 + n][:TT, :],
                                      bq[:, n * 512:(n + 1) * 512], ALU.add).then_inc(q_biased, 1)
                for n in range(4):
                    k = 4 * t + n
                    dve.wait_ge(q_squared, k + 1)
                    dve.tensor_reduce(ssq[:, t, 4 * n:4 * n + 4],
                                      sq[:, k % 2, :].rearrange("p (h d) -> p h d", h=4),
                                      AX.X, ALU.add).then_inc(sq_reduced, 1)
                dve.wait_ge(sq_reduced, 4 * t + 4)
                dve.tensor_scalar(qvar[:, t, :], ssq[:, t, :], 1.0 / HD, 1e-6, ALU.mult, ALU.add).then_inc(qvar_ready, 1)
                if t:
                    columns_out(t - 1)
            columns_out(NT - 1)
            nxt["split_low"](dve)


def shared_area(nc, sb, size):
    sb("area", [P, size])
    base = nc.sbuf_base - 4 * size

    def place(name, start, shape, dt=F32):
        assert start + math.prod(shape) <= size
        return nc.alloc_sbuf_tensor_at(name, [P] + shape, dt, offset=base + 4 * start)

    return place


def attention0_inputs(sem, sb, place, ctx_in, mask_in, wk_in, bk_in, wv_in, bv_in):
    t = {"wkv": sb("b_wkv", [P, KC, NKV, 2, HD]), "bk": sb("b_bk", [CH, NKV * HD]), "bv": sb("b_bv", [P, NKV]),
         "mask": sb("b_mask", [TT, S2]), "raw": sb("b_ctx", [P, 2, KC, PW]),
         "whi": sb("b_whi", [P, KC, NKV, 2, HD], F32R), "wlo": sb("b_wlo", [P, KC, NKV, 2, HD], F32R),
         "chi": [place("b_ctx_hi0", 0, [KC, S2], F32R), sb("b_ctx_hi1", [P, KC, S2], F32R)],
         "clo": [place("b_ctx_lo0", KC * S2, [KC, S2], F32R), sb("b_ctx_lo1", [P, KC, S2], F32R)],
         "w_hi": sem("b_w_hi"), "ctx_hi": sem("b_ctx_hi"), "ctx_lo": sem("b_ctx_lo"),
         "w_loaded": sem("b_w_loaded"), "misc_loaded": sem("b_misc_loaded"),
         "ctx_loaded": [sem(f"b_ctx_loaded{i}") for i in range(2)],
         "o_writable": sem("b_o_writable")}

    def load(sp):
        for kv, w in enumerate((wk_in, wv_in)):
            for c in range(KC):
                sp.dma_start(t["wkv"][:, c, :, kv, :], w[c * P:(c + 1) * P, :].rearrange("p (g n) -> p g n", g=NKV)
                             ).then_inc(t["w_loaded"], 16)
        for pc in range(2):
            sp.dma_start(t["raw"][:, pc, :, :], ctx_in[0, :, pc * PW:(pc + 1) * PW].rearrange("(c p) s -> p c s", p=P)
                         ).then_inc(t["ctx_loaded"][pc], 16)
        sp.dma_start(t["bk"][:, :], bk_in.partition_broadcast(CH)).then_inc(t["misc_loaded"], 16)
        sp.dma_start(t["bv"][:, :], bv_in).then_inc(t["o_writable"], 16)
        for j in range(2):
            sp.dma_start(t["mask"][j * S:(j + 1) * S, :], mask_in).then_inc(t["misc_loaded"], 16)

    def split_high(act):
        act.wait_ge(t["w_loaded"], 32 * KC)
        act.copy(t["whi"][:, :, :, :, :], t["wkv"][:, :, :, :, :]).then_inc(t["w_hi"], 1)
        for pc in range(2):
            act.wait_ge(t["ctx_loaded"][pc], 16)
            act.copy(t["chi"][0][:, :, pc * PW:(pc + 1) * PW], t["raw"][:, pc, :, :]).then_inc(t["ctx_hi"], 1)

    def split_low(dve):
        dve.wait_ge(t["w_hi"], 1)
        dve.tensor_tensor(t["wlo"][:, :, :, :, :], t["wkv"][:, :, :, :, :],
                          t["whi"].bitcast(F32)[:, :, :, :, :], ALU.subtract)
        for pc in range(2):
            cols = slice(pc * PW, (pc + 1) * PW)
            dve.wait_ge(t["ctx_hi"], pc + 1)
            dve.tensor_tensor(t["clo"][0][:, :, cols], t["raw"][:, pc, :, :], t["chi"][0][:, :, cols].bitcast(F32),
                              ALU.subtract).then_inc(t["ctx_lo"], 1)

    t["load"], t["split_high"], t["split_low"] = load, split_high, split_low
    return t


def attention0_phase(nc, sem, keep, pre, load_next, ctx_in, q_scratch, o_scratch):
    with ExitStack() as ctx:
        sb = lambda name, shape, dt=F32: ctx.enter_context(nc.sbuf_tensor(name, shape, dt))
        ident, mhalf = keep["ident"], keep["mhalf"]
        PAIRS = NC // 2
        QUADS = NC // 4
        QW = 4 * CH
        whi, wlo, chi, clo, bk, bv, mask, raw = (
            pre[n] for n in ("whi", "wlo", "chi", "clo", "bk", "bv", "mask", "raw"))
        misc_loaded, ctx_loaded, ctx_hi, ctx_lo, o_writable = (
            pre[n] for n in ("misc_loaded", "ctx_loaded", "ctx_hi", "ctx_lo", "o_writable"))
        ktok = [sb(f"b_k_tok{i}", [CH, NC, HD]) for i in range(2)]
        ksq = sb("b_k_sq", [CH, 2, 4, HD])
        kss = sb("b_k_ss", [CH, 2, NC])
        kvar = sb("b_k_var", [CH, 2, NC])
        kr = sb("b_k_r", [CH, 2, NC])
        k_hi = [sb(f"b_kT_hi{i}", [P, S2], F32R) for i in range(2)]
        k_lo = [sb(f"b_kT_lo{i}", [P, S2], F32R) for i in range(2)]
        V = [sb(f"b_v{i}", [CH, NC, HD]) for i in range(4)]
        probs = [sb(f"b_probs{i}", [TT, S2]) for i in range(4)]
        pT = [sb(f"b_probsT{i}", [CH, 2, QG]) for i in range(2)]
        fence = sb("b_fence", [TT, 2 * NSB * NKV])
        mx = sb("b_max", [TT, 2, 2, NSB])
        nmx = sb("b_neg_max", [TT, 2, 2])
        rs = sb("b_row_sum", [TT, 2, 2])
        rr = sb("b_row_recip", [TT, 2, 2])
        q_raw = sb("b_q", [P, NH * S])
        q_hi = [sb(f"b_q_hi{i}", [P, NH * S], F32R) for i in range(2)]
        q_lo = [sb(f"b_q_lo{i}", [P, NH * S], F32R) for i in range(2)]
        oT = sb("b_oT", [P, NH, 2, S])
        bank = lambda name: ctx.enter_context(nc.psum_tensor(name, [P, 512], F32))
        ps_s = [bank(f"b_ps_scores{i}") for i in range(3)]
        ps_kv = [bank(f"b_ps_kv{i}") for i in range(2)]
        ps_t = [bank(f"b_ps_T{i}") for i in range(2)]
        ps_o = bank("b_ps_o")
        q_loaded, q_hi_ready, q_split, kv_done, k_biased, v_copied, k_squared, k_reduced = (
            sem(n) for n in ("b_q_loaded", "b_q_hi_ready", "b_q_split", "b_kv_done",
                             "b_k_biased", "b_v_copied", "b_k_squared", "b_k_reduced"))
        kvar_ready, kr_ready, k_scaled, kt_done, kt_hi_ready, kt_split = (sem(n) for n in (
            "b_kvar_ready", "b_kr_ready", "b_k_scaled", "b_kT_done", "b_kT_hi_ready", "b_kT_split"))
        s_done, s_masked, max_ready, exp_done, recip_ready, p_ready, pt_done, pt_copied, o_done, o_copied = (
            sem(n) for n in ("b_scores_done", "b_scores_masked", "b_max_ready", "b_exp_done", "b_recip_ready",
                             "b_probs_ready", "b_pT_done", "b_pT_copied", "b_o_done", "b_o_copied"))
        block = ctx.enter_context(nc.Block())

        def batches(eng, first, attend, tail):
            first()
            attend(0, 0, 0)
            with eng.Fori(0, B // 2 - 1) as i:
                attend(i * 2 + 1, 1, i)
                attend(i * 2 + 2, 0, i + 1)
            attend(B - 1, 1, B // 2 - 1)
            tail()

        def ahead(b, g, par, n):
            if g + n < NKV:
                return b, g + n, par
            if isinstance(b, int) and b == B - 1:
                return None
            return b + 1, g + n - NKV, 1 - par

        @block.sync
        def _(sp):
            def load(b, first_piece=0):
                for pc in range(first_piece, PIECES):
                    wait_for(sp, ctx_lo, 4 * b + pc - 1)
                    sp.dma_start(raw[:, pc % 2, :, :],
                                 ctx_in[b, :, pc * PW:(pc + 1) * PW].rearrange("(c p) s -> p c s", p=P)
                                 ).then_inc(ctx_loaded[pc % 2], 16)

            def load_queries(b):
                wait_for(sp, q_split, b)
                sp.dma_start(q_raw[:, :], q_scratch[b].rearrange("p h s -> p (h s)")).then_inc(q_loaded, 16)

            def first():
                load(0, 2)
                load_queries(0)

            def store(pair):
                sp.wait_ge(o_copied, pair * 8 + 8)
                sp.dma_start(o_scratch[pair], oT[:, :, :, :].rearrange("p h b s -> p (h b s)")).then_inc(o_writable, 16)

            def attend(b, par, pair):
                if not (isinstance(b, int) and b == B - 1):
                    load(b + 1)
                    load_queries(b + 1)
                if par == 0 and not (isinstance(b, int) and b == 0):
                    store(pair - 1)
                if isinstance(b, int) and b == B - 1:
                    sp.wait_ge(kv_done, (B - 1) * NKV * PAIRS)
                    load_next(sp)

            batches(sp, first, attend, lambda: store(NT - 1))
            sp.wait_ge(o_writable, 16 * (NT + 1))

        @block.gpsimd
        def _(pool):
            def normalise_keys(b, g, par):
                u = b * NKV + g
                pool.wait_ge(kvar_ready, u + 1)
                pool.tensor_tensor(kr[:, g % 2, :], kvar[:, g % 2, :], mhalf[:CH, 0:NC], ALU.pow).then_inc(kr_ready, 1)
                pool.wait_ge(kr_ready, u + 1)
                for i in range(QUADS):
                    k = ktok[g % 2][:, 4 * i:4 * i + 4, :]
                    pool.tensor_tensor(k, k, kr[:, g % 2, 4 * i:4 * i + 4].unsqueeze(2).broadcast_to([CH, 4, HD]),
                                       ALU.mult).then_inc(k_scaled, 1)

            def attend(b, par, pair):
                for g in range(NKV):
                    unit = ahead(b, g, par, 1)
                    if unit:
                        normalise_keys(*unit)

            batches(pool, lambda: normalise_keys(0, 0, 0), attend, lambda: None)

        @block.scalar
        def _(act):
            def split(b, pc, par):
                act.wait_ge(ctx_loaded[pc % 2], b * 32 + 16 * (pc // 2 + 1))
                wait_for(act, kv_done, (b - 1) * NKV * PAIRS)
                act.copy(chi[par][:, :, pc * PW:(pc + 1) * PW], raw[:, pc % 2, :, :]).then_inc(ctx_hi, 1)

            def split_queries(b, par):
                act.wait_ge(q_loaded, b * 16 + 16)
                wait_for(act, s_done, (b - 1) * NKV * 2 * NSB)
                act.copy(q_hi[par][:, :], q_raw[:, :]).then_inc(q_hi_ready, 1)

            def values_out(unit, i):
                b, g, _ = unit
                act.wait_ge(kv_done, (b * NKV + g) * PAIRS + i + 1)
                act.copy(V[g][:, 2 * i:2 * i + 2, :],
                         ps_kv[i % 2][:CH, :].rearrange("p (c kv d) -> p c kv d", c=2, kv=2)[:, :, 1, :]
                         ).then_inc(v_copied, 1)

            def squares(unit, j):
                b, g, _ = unit
                act.wait_ge(k_biased, (b * NKV + g) * PAIRS + 2 * j + 2)
                wait_for(act, k_reduced, (b * NKV + g) * QUADS + j - 1)
                act.activation(ksq[:, (g * QUADS + j) % 2], ktok[g % 2][:, 4 * j:4 * j + 4, :], ACT.Square
                               ).then_inc(k_squared, 1)

            def exp(u, g, j):
                act.wait_ge(max_ready, 2 * u + j + 1)
                act.activation(probs[2 * (g % 2) + j][:, :], probs[2 * (g % 2) + j][:, :], ACT.Exp,
                               bias=nmx[:, g % 2, j:j + 1], accum_out=rs[:, g % 2, j:j + 1]).then_inc(exp_done, 1)

            def probs_out(u, rs):
                for r in rs:
                    act.wait_ge(pt_done, u * PAIRS + r + 1)
                    act.copy(pT[r % 2][:, :, :], ps_t[(r + 1) % 2][:CH, 0:2 * QG].rearrange("p (c q) -> p c q", c=2)
                             ).then_inc(pt_copied, 1)

            def keys_high(unit, i):
                b, g, _ = unit
                act.wait_ge(kt_done, (b * NKV + g) * QUADS + i + 1)
                act.copy(k_hi[g % 2][:, i * QW:(i + 1) * QW], ps_t[i % 2][:, 0:QW]).then_inc(kt_hi_ready, 1)

            def first():
                for pc in range(2, PIECES):
                    split(0, pc, 0)
                for g in range(2):
                    for i in range(PAIRS):
                        values_out((0, g, 0), i)
                        if i % 2 == 1:
                            squares((0, g, 0), i // 2)
                    if g == 0:
                        split_queries(0, 0)
                for i in range(QUADS):
                    keys_high((0, 0, 0), i)

            def attend(b, par, pair):
                for g in range(NKV):
                    u = b * NKV + g
                    nxt, prj = ahead(b, g, par, 1), ahead(b, g, par, 2)
                    more = ahead(b, NKV - 1, par, 1)
                    out = lambda i: prj and values_out(prj, i)
                    square = lambda j: prj and squares(prj, j)
                    high = lambda i: nxt and keys_high(nxt, i)
                    if more and g < 2:
                        split(b + 1, 2 * g, 1 - par)
                        split(b + 1, 2 * g + 1, 1 - par)
                    if more and g == 2:
                        split_queries(b + 1, 1 - par)
                    exp(u, g, 0)
                    out(0)
                    out(1)
                    square(0)
                    out(2)
                    exp(u, g, 1)
                    out(3)
                    high(0)
                    high(1)
                    out(4)
                    high(2)
                    square(1)
                    before = not (isinstance(u, int) and u == 0)
                    if before:
                        probs_out(u - 1, range(1))
                    out(5)
                    if before:
                        probs_out(u - 1, range(1, 2))
                    square(2)
                    if before:
                        probs_out(u - 1, range(2, PAIRS))

            batches(act, first, attend, lambda: probs_out(B * NKV - 1, range(PAIRS)))

        @block.tensor
        def _(pe):
            def project(unit, i):
                b, g, par = unit
                n = (b * NKV + g) * PAIRS + i
                pe.wait_ge(ctx_lo, b * PIECES + -(-(2 * i + 2) * CH // PW))
                wait_for(pe, k_biased, n - 1)
                for cc in range(2):
                    c = 2 * i + cc
                    m = 0
                    for kc in range(KC):
                        for a, w in ((chi, whi), (chi, wlo), (clo, whi)):
                            mm = pe.matmul(ps_kv[i % 2][:CH, cc * 2 * HD:(cc + 1) * 2 * HD],
                                           a[par][:, kc, c * CH:(c + 1) * CH],
                                           w[:, kc, g].rearrange("p kv d -> p (kv d)"),
                                           start=m == 0, stop=m == 3 * KC - 1)
                            m += 1
                mm.then_inc(kv_done, 1)

            def keys_to_columns(unit, i):
                b, g, _ = unit
                u = b * NKV + g
                pe.wait_ge(k_scaled, u * QUADS + i + 1)
                if i < 2:
                    wait_for(pe, pt_copied, (u - 2) * PAIRS - i)
                else:
                    pe.wait_ge(kt_split, u * QUADS + 1)
                for cc in range(4):
                    mm = pe.transpose(ps_t[i % 2][:, cc * CH:(cc + 1) * CH], ktok[g % 2][:, 4 * i + cc, :],
                                      ident[:CH, :CH])
                mm.then_inc(kt_done, 1)

            def scores(u, g, par, m):
                j, n = m // NSB, m % NSB
                wait_for(pe, s_masked, u * 2 * NSB + m - 2)
                for k, (a, q) in enumerate(((k_hi, q_hi), (k_hi, q_lo), (k_lo, q_hi))):
                    mm = pe.matmul(ps_s[m % 3][:TT, 0:SB], q[par][:, (2 * g + j) * TT:(2 * g + j + 1) * TT],
                                   a[g % 2][:, n * SB:(n + 1) * SB], start=k == 0, stop=k == 2)
                mm.then_inc(s_done, 1)

            def transpose_probs(u, g, r):
                if not (isinstance(u, int) and u + 2 >= B * NKV) and r < 2:
                    pe.wait_ge(kt_split, (u + 2) * QUADS + 2 + r)
                for cc in range(2):
                    for j in range(2):
                        c = 2 * r + cc
                        mm = pe.transpose(ps_t[(r + 1) % 2][:CH, cc * QG + j * TT:cc * QG + (j + 1) * TT],
                                          probs[2 * (g % 2) + j][:, c * CH:(c + 1) * CH], ident[:TT, :TT])
                mm.then_inc(pt_done, 1)

            def values(u, g, between=lambda: None):
                pe.wait_ge(p_ready, u * 2 + 2)
                wait_for(pe, o_copied, u)

                def product(r):
                    pe.wait_ge(pt_copied, u * PAIRS + r + 1)
                    for cc in range(2):
                        c = 2 * r + cc
                        mm = pe.matmul(ps_o[:, 0:QG], V[g][:, c, :], pT[r % 2][:, cc, :],
                                       start=c == 0, stop=c == NC - 1)
                    return mm

                for r in range(PAIRS):
                    if r >= 2:
                        product(r - 2)
                    transpose_probs(u, g, r)
                    if r == 0:
                        between()
                product(PAIRS - 2)
                product(PAIRS - 1).then_inc(o_done, 1)

            def first():
                for g in range(2):
                    for i in range(PAIRS):
                        project((0, g, 0), i)
                for i in range(QUADS):
                    keys_to_columns((0, 0, 0), i)

            def attend(b, par, pair):
                for g in range(NKV):
                    u = b * NKV + g
                    nxt, prj = ahead(b, g, par, 1), ahead(b, g, par, 2)
                    proj = lambda i: prj and project(prj, i)
                    if g == 0:
                        pe.wait_ge(q_split, b + 1)
                    for m in range(3):
                        pe.wait_ge(kt_split, u * QUADS + m + 1)
                        scores(u, g, par, m)
                    proj(0)
                    scores(u, g, par, 3)
                    scores(u, g, par, 4)
                    proj(1)
                    scores(u, g, par, 5)
                    proj(2)
                    proj(3)
                    columns = lambda i: nxt and keys_to_columns(nxt, i)
                    columns(0)
                    columns(1)
                    proj(4)
                    columns(2)
                    if isinstance(u, int) and u == 0:
                        proj(5)
                    else:
                        values(u - 1, (g - 1) % NKV, lambda: proj(5))

            def tail():
                values(B * NKV - 1, NKV - 1)

            batches(pe, first, attend, tail)

        @block.vector
        def _(dve):
            def split(b, pc, par):
                dve.wait_ge(ctx_hi, b * PIECES + pc + 1)
                cols = slice(pc * PW, (pc + 1) * PW)
                dve.tensor_tensor(clo[par][:, :, cols], raw[:, pc % 2, :, :], chi[par][:, :, cols].bitcast(F32),
                                  ALU.subtract).then_inc(ctx_lo, 1)

            def split_queries(b, par):
                dve.wait_ge(q_hi_ready, b + 1)
                dve.tensor_tensor(q_lo[par][:, :], q_raw[:, :], q_hi[par].bitcast(F32)[:, :], ALU.subtract
                                  ).then_inc(q_split, 1)

            def keys_out(unit, i):
                b, g, _ = unit
                dve.wait_ge(v_copied, (b * NKV + g) * PAIRS + i + 1)
                dve.tensor_tensor(ktok[g % 2][:, 2 * i:2 * i + 2, :],
                                  ps_kv[i % 2][:CH, :].rearrange("p (c kv d) -> p c kv d", c=2, kv=2)[:, :, 0, :],
                                  bk[:, g * HD:(g + 1) * HD].unsqueeze(1).broadcast_to([CH, 2, HD]),
                                  ALU.add).then_inc(k_biased, 1)

            def reduce_squares(unit, j):
                b, g, _ = unit
                dve.wait_ge(k_squared, (b * NKV + g) * QUADS + j + 1)
                dve.tensor_reduce(kss[:, g % 2, 4 * j:4 * j + 4], ksq[:, (g * QUADS + j) % 2], AX.X, ALU.add
                                  ).then_inc(k_reduced, 1)
                if j == QUADS - 1:
                    dve.wait_ge(k_reduced, (b * NKV + g + 1) * QUADS)
                    dve.tensor_scalar(kvar[:, g % 2, :], kss[:, g % 2, :], 1.0 / HD, 1e-6, ALU.mult, ALU.add
                                      ).then_inc(kvar_ready, 1)

            def keys_low(unit, i):
                b, g, _ = unit
                dve.wait_ge(kt_hi_ready, (b * NKV + g) * QUADS + i + 1)
                cols = slice(i * QW, (i + 1) * QW)
                dve.tensor_tensor(k_lo[g % 2][:, cols], ps_t[i % 2][:, 0:QW], k_hi[g % 2].bitcast(F32)[:, cols],
                                  ALU.subtract).then_inc(kt_split, 1)

            def mask_scores(u, g, m):
                j, n = m // NSB, m % NSB
                dve.wait_ge(s_done, u * 2 * NSB + m + 1)
                dve.memset(fence[:, 6 * g + m:6 * g + m + 1], 0.0)
                dve.tensor_tensor_reduce(out=probs[2 * (g % 2) + j][:, n * SB:(n + 1) * SB],
                                         in0=ps_s[m % 3][:TT, 0:SB], in1=mask[:, n * SB:(n + 1) * SB],
                                         scale=1.0, scalar=-3.0e38, op0=ALU.add, op1=ALU.max,
                                         accum_out=mx[:, g % 2, j, n:n + 1]).then_inc(s_masked, 1)
                if n == NSB - 1:
                    dve.wait_ge(s_masked, u * 2 * NSB + m + 1)
                    dve.tensor_reduce(nmx[:, g % 2, j:j + 1], mx[:, g % 2, j, :], AX.X, ALU.max,
                                      negate=True).then_inc(max_ready, 1)

            def normalise(u, g, j):
                n = 2 * u + j
                dve.wait_ge(exp_done, n + 1)
                dve.reciprocal(rr[:, g % 2, j:j + 1], rs[:, g % 2, j:j + 1]).then_inc(recip_ready, 1)
                dve.wait_ge(recip_ready, n + 1)
                p = probs[2 * (g % 2) + j]
                dve.tensor_scalar(p[:, :], p[:, :], rr[:, g % 2, j:j + 1], None, ALU.mult).then_inc(p_ready, 1)

            def outputs(u, g, par, pair):
                dve.wait_ge(o_done, u + 1)
                if g == 0 and par == 0:
                    dve.wait_ge(o_writable, pair * 16 + 16)
                dve.tensor_scalar(oT[:, g * NH // NKV:(g + 1) * NH // NKV, par, :],
                                  ps_o[:, 0:QG].rearrange("p (h s) -> p h s", s=S), bv[:, g:g + 1], None,
                                  ALU.add).then_inc(o_copied, 1)

            def first():
                for pc in range(2, PIECES):
                    split(0, pc, 0)
                dve.wait_ge(misc_loaded, 48)
                for g in range(2):
                    for i in range(PAIRS):
                        keys_out((0, g, 0), i)
                        if i in (3, 5):
                            reduce_squares((0, g, 0), i // 2 - 1)
                    reduce_squares((0, g, 0), 2)
                    if g == 0:
                        split_queries(0, 0)
                for i in range(QUADS):
                    keys_low((0, 0, 0), i)

            def attend(b, par, pair):
                for g in range(NKV):
                    u = b * NKV + g
                    nxt, prj = ahead(b, g, par, 1), ahead(b, g, par, 2)
                    more = ahead(b, NKV - 1, par, 1)
                    out = lambda i: prj and keys_out(prj, i)
                    squares = lambda j: prj and reduce_squares(prj, j)
                    low = lambda i: nxt and keys_low(nxt, i)
                    for m in range(5):
                        mask_scores(u, g, m)
                    out(0)
                    out(1)
                    mask_scores(u, g, 5)
                    squares(0)
                    out(2)
                    out(3)
                    low(0)
                    low(1)
                    out(4)
                    low(2)
                    out(5)
                    squares(1)
                    normalise(u, g, 0)
                    squares(2)
                    normalise(u, g, 1)
                    if more and g < 2:
                        split(b + 1, 2 * g, 1 - par)
                        split(b + 1, 2 * g + 1, 1 - par)
                    if more and g == 2:
                        split_queries(b + 1, 1 - par)
                    if not (isinstance(u, int) and u == 0):
                        if g == 0:
                            outputs(u - 1, NKV - 1, 1 - par, pair)
                        else:
                            outputs(u - 1, g - 1, par, pair)

            batches(dve, first, attend, lambda: outputs(B * NKV - 1, NKV - 1, 1, B // 2 - 1))


def layer_norm(dve, ch, x, stats, mv, var, var_ready, rstd_ready, rstd, out, out_ready, base, tiles=range(NT)):
    ts = slice(tiles[0], tiles[-1] + 1)
    for t in tiles:
        last = dve.bn_stats(stats[:, t, :], x[:, t, :])
    ch.link(last)
    for t in tiles:
        last = dve.bn_aggr(mv[:, t, :], stats[:, t, :])
    ch.link(last)
    dve.tensor_scalar(var[:, ts], mv[:, ts, 1], 1e-5, None, ALU.add).then_inc(var_ready, 1)
    dve.wait_ge(rstd_ready, base + 1)
    for t in tiles:
        dve.tensor_scalar(out[:, t, :], x[:, t, :], mv[:, t, 0:1], rstd[:, t:t + 1],
                          ALU.subtract, ALU.mult).then_inc(out_ready, 1)


def ffn0_phase(nc, sem, keep, wo_loaded, nxt, o_scratch, gates_in, identb_in, had_in, wg_in, wu_in, wd_in, wq1_in, bq1_in):
    with ExitStack() as ctx:
        sb = lambda name, shape, dt=F32: ctx.enter_context(nc.sbuf_tensor(name, shape, dt))
        x, ident, mhalf, gate = keep["x"], keep["ident"], keep["mhalf"], keep["gate"]
        q1T = keep["q1T"]
        oT = sb("c_oT", [P, NT, NH, TT])
        wo = keep["wo"]
        w_raw = sb("c_w_raw", [P, 3, 2048])
        w3 = sb("c_w_ternary", [P, 3, 2048], BF16)
        wabs = sb("c_w_abs", [P, 4])
        wmean = sb("c_w_mean", [P, 4])
        wscale = sb("c_w_scale", [P, 4])
        ones = sb("c_ones", [P, P])
        gate_raw = sb("c_gate_raw", [P, 4])
        identb = sb("c_identb", [P, P], BF16)
        identf = sb("c_had", [P, P])
        stats = sb("c_stats", [TT, NT, 6])
        mv = sb("c_mv", [TT, NT, 2])
        var = sb("c_var", [TT, NT])
        rstd = sb("c_rstd", [TT, NT])
        xn = sb("c_xn", [TT, NT, H])
        amax = sb("c_amax", [TT, 2, NT])
        arec = sb("c_arec", [TT, 2, NT])
        ascale = sb("c_ascale", [TT, 2, NT])
        deq = sb("c_deq", [TT, 3, NT])
        xq = sb("c_xq", [TT, NT, H], BF16)
        xqT = sb("c_xqT", [P, NT, KC, TT], BF16)
        sg = sb("c_silu", [TT, NT, 2, 512])
        inter = sb("c_inter", [TT, NT, F0])
        iT = sb("c_interT", [P, NT, FC0, TT])
        u = [sb(f"c_had{i}", [TT, NT, FC0, P]) for i in range(1)]
        xq_t = u[0][:, :, 0:KC, :].rearrange("p t c d -> p t (c d)")
        zq = sb("c_zq", [TT, NT, F0], BF16)
        zT = sb("c_zT", [P, NT, FC0, TT], BF16)
        xnT = sb("c_xnT", [P, KC, T])
        wq1 = sb("c_wq1", [P, KC, H])
        bq1 = sb("c_bq1", [P, KC])
        ps = [ctx.enter_context(nc.psum_tensor(f"c_ps{i}", [P, 512], F32)) for i in range(8)]
        o_loaded = [sem(f"c_o_loaded{t}") for t in range(NT)]
        (w_loaded, c_loaded, gates_loaded) = (sem(n) for n in (
            "c_w_loaded", "c_others_loaded", "c_gates_loaded"))
        (chain, gate_ready, wabs_ready, wsum_done, w_ready, wo_done) = (sem(n) for n in (
            "c_chain", "c_gate_ready", "c_wabs_ready", "c_wsum_done", "c_w_ready", "c_wo_done"))
        had_summed = sem("c_had_summed")
        (var_ready, rstd_ready, xn_ready, xq_ready, xqt_done, xqt_copied, gu_done, silu_done, inter_ready) = (
            sem(n) for n in ("c_var_ready", "c_rstd_ready", "c_xn_ready", "c_xq_ready", "c_xqT_done", "c_xqT_copied",
                             "c_gate_up_done", "c_silu_done", "c_inter_ready"))
        (it_done, it_copied, had_done, had_copied, zq_ready, zt_done, zt_copied, down_done, xnt_done, xnt_copied,
         q1_done, q1_copied) = (sem(n) for n in (
            "c_interT_done", "c_interT_copied", "c_had_done", "c_had_copied", "c_zq_ready", "c_zT_done",
            "c_zT_copied", "c_down_done", "c_xnT_done", "c_xnT_copied", "c_q1_done", "c_q1_copied"))
        block = ctx.enter_context(nc.Block())

        @block.sync
        def _(sp):
            for t in range(NT):
                sp.dma_start(oT[:, t], o_scratch[t].rearrange("p (h s) -> p h s", h=NH)).then_inc(o_loaded[t], 16)
                if t == 0:
                    sp.dma_start(gate_raw[:, :], gates_in.partition_broadcast(P)).then_inc(gates_loaded, 16)
                if t == 1:
                    for n, w in enumerate((wg_in, wu_in, wd_in)):
                        sp.dma_start(w_raw[:, n, :].rearrange("p (c n) -> p c n", n=w.shape[1]),
                                     w.rearrange("(c p) n -> p c n", p=P)).then_inc(w_loaded, 16)
            sp.dma_start(identb[:, :], identb_in).then_inc(c_loaded, 16)
            sp.dma_start(identf[:, :], had_in).then_inc(c_loaded, 16)
            sp.dma_start(wq1[:, :, :], wq1_in.rearrange("(c p) n -> p c n", p=P)).then_inc(c_loaded, 16)
            sp.dma_start(bq1[:, :], bq1_in).then_inc(c_loaded, 16)
            nxt["load"](sp)

        def butterflies(eng, ch, t):
            eng.wait_ge(had_copied, 2 * t + 2)
            a, b = u[0][:, t], inter[:, t, :].rearrange("p (c d) -> p c d", d=P)
            for w in (4, 2, 1):
                av, bv_ = (v.rearrange("p (g two w) d -> p g two (w d)", two=2, w=w) for v in (a, b))
                eng.tensor_tensor(bv_[:, :, 0], av[:, :, 0], av[:, :, 1], ALU.add)
                ch.link(eng.tensor_tensor(bv_[:, :, 1], av[:, :, 0], av[:, :, 1], ALU.subtract))
                a, b = b, a

        @block.gpsimd
        def _(pool):
            for n in range(3):
                pool.wait_ge(var_ready, n + 1)
                ts = (slice(0, NT - 1), slice(NT - 1, NT), slice(0, NT))[n]
                pool.tensor_tensor(rstd[:, ts], var[:, ts], mhalf[:TT, ts], ALU.pow).then_inc(rstd_ready, 1)
                if n == 1:
                    butterflies(pool, Chain(pool, had_summed), NT - 1)

        @block.scalar
        def _(act):
            act.wait_ge(gates_loaded, 16)
            act.activation(gate[:, :], gate_raw[:, :], ACT.Tanh).then_inc(gate_ready, 1)

            def tokens_to_columns(tiles):
                for t in tiles:
                    act.wait_ge(xqt_done, t + 1)
                    act.copy(xqT[:, t, :, :], ps[2 * t].bitcast(BF16)[:, 0:KC * TT].rearrange("p (c s) -> p c s", c=KC)
                             ).then_inc(xqt_copied, 1)

            tokens_to_columns(range(NT - 1))
            for n in range(2):
                for t in range(NT):
                    if n == 0 and t == NT - 1:
                        tokens_to_columns(range(t, NT))
                    act.wait_ge(gu_done, n * NT + t + 1)
                    act.activation(sg[:, t, n, :], ps[2 * t][:TT, :], ACT.Silu,
                                   scale=deq[:, 0, t:t + 1]).then_inc(silu_done, 1)
            for t in range(NT):
                for n in range(2):
                    act.wait_ge(it_done, 2 * t + n + 1)
                    act.copy(iT[:, t, 4 * n:4 * n + 4, :],
                             ps[2 * t + n][:, 0:4 * TT].rearrange("p (c s) -> p c s", c=4)).then_inc(it_copied, 1)
            for t in range(NT):
                for n in range(2):
                    act.wait_ge(had_done, 2 * t + n + 1)
                    act.mul(u[0][:, t, 4 * n:4 * n + 4, :].rearrange("p c d -> p (c d)"), ps[2 * t + n][:TT, :],
                            float(F0) ** -0.5).then_inc(had_copied, 1)
            for t in range(NT):
                act.wait_ge(zt_done, t + 1)
                act.copy(zT[:, t, :, :], ps[2 * t].bitcast(BF16)[:, 0:FC0 * TT].rearrange("p (c s) -> p c s", c=FC0)
                         ).then_inc(zt_copied, 1)
            act.wait_ge(wo_done, NT)
            nxt["split_high"](act)
            for t in range(NT):
                act.wait_ge(xnt_done, t + 1)
                act.copy(xnT[:, :, t * TT:(t + 1) * TT], ps[2 * t][:, 0:KC * TT].rearrange("p (c s) -> p c s", c=KC)
                         ).then_inc(xnt_copied, 1)

        @block.tensor
        def _(pe):
            pe.wait_ge(wo_loaded, 16)
            for t in range(NT):
                if t == NT - 2:
                    pe.wait_ge(wabs_ready, 1)
                    pe.matmul(ps[7][:, 0:3], ones[:, :], wabs[:, 0:3], start=True, stop=True).then_inc(wsum_done, 1)
                pe.wait_ge(o_loaded[t], 16)
                for h in range(NH):
                    mm = pe.matmul(ps[2 * t][:TT, 0:H], oT[:, t, h, :], wo[:, h, :],
                                   start=h == 0, stop=h == NH - 1)
                mm.then_inc(wo_done, 1)
            pe.wait_ge(c_loaded, 64)

            def tokens_to_columns(tiles):
                for t in tiles:
                    pe.wait_ge(xq_ready, t + 1)
                    for c in range(KC):
                        mm = pe.transpose(ps[2 * t].bitcast(BF16)[:, c * TT:(c + 1) * TT], xq[:, t, c * P:(c + 1) * P],
                                          identb[:TT, :TT])
                    mm.then_inc(xqt_done, 1)

            tokens_to_columns(range(NT - 1))
            pe.wait_ge(w_ready, 2)
            for n in range(2):
                for t in range(NT):
                    if n == 0 and t == NT - 1:
                        tokens_to_columns(range(t, NT))
                    if n == 0:
                        pe.wait_ge(xqt_copied, t + 1)
                    else:
                        pe.wait_ge(inter_ready, t + 1)
                    for k in range(2):
                        for c in range(KC):
                            mm = pe.matmul(ps[2 * t + k][:TT, :], xqT[:, t, c, :],
                                           w3[:, k, c * F0 + n * 512:c * F0 + (n + 1) * 512],
                                           start=c == 0, stop=c == KC - 1)
                    mm.then_inc(gu_done, 1)
            for t in range(NT):
                pe.wait_ge(inter_ready, NT + t + 1)
                for n in range(2):
                    for j in range(4):
                        c = 4 * n + j
                        mm = pe.transpose(ps[2 * t + n][:, j * TT:(j + 1) * TT], inter[:, t, c * P:(c + 1) * P],
                                          ident[:TT, :TT])
                    mm.then_inc(it_done, 1)
            for t in range(NT):
                pe.wait_ge(it_copied, 2 * t + 2)
                for n in range(2):
                    for j in range(4):
                        mm = pe.matmul(ps[2 * t + n][:TT, j * P:(j + 1) * P], iT[:, t, 4 * n + j, :], identf[:, :],
                                       start=True, stop=True)
                    mm.then_inc(had_done, 1)
            pe.wait_ge(w_ready, 3)
            for t in range(NT):
                pe.wait_ge(zq_ready, t + 1)
                for c in range(FC0):
                    mm = pe.transpose(ps[2 * t].bitcast(BF16)[:, c * TT:(c + 1) * TT], zq[:, t, c * P:(c + 1) * P],
                                      identb[:TT, :TT])
                mm.then_inc(zt_done, 1)
                pe.wait_ge(zt_copied, t + 1)
                for c in range(FC0):
                    mm = pe.matmul(ps[2 * t + 1][:TT, 0:H], zT[:, t, c, :], w3[:, 2, c * H:(c + 1) * H],
                                   start=c == 0, stop=c == FC0 - 1)
                mm.then_inc(down_done, 1)
            for t in range(NT):
                pe.wait_ge(xn_ready, NT + t + 1)
                for c in range(KC):
                    mm = pe.transpose(ps[2 * t][:, c * TT:(c + 1) * TT], xn[:, t, c * P:(c + 1) * P], ident[:TT, :TT])
                mm.then_inc(xnt_done, 1)
            pe.wait_ge(xnt_copied, NT)
            for o in range(KC):
                for c in range(KC):
                    mm = pe.matmul(ps[2 * o][:, 0:T], wq1[:, c, o * P:(o + 1) * P], xnT[:, c, :],
                                   start=c == 0, stop=c == KC - 1)
                mm.then_inc(q1_done, 1)

        @block.vector
        def _(dve):
            ch = Chain(dve, chain)

            def ternary(k):
                ch.link(dve.tensor_scalar(w_raw[:, k, :], w_raw[:, k, :], wscale[:, k:k + 1], BIG, ALU.mult, ALU.add))
                ch.link(dve.tensor_scalar(w_raw[:, k, :], w_raw[:, k, :], BIG, 1.0, ALU.subtract, ALU.min))
                dve.tensor_scalar(w3[:, k, :], w_raw[:, k, :], -1.0, None, ALU.max).then_inc(w_ready, 1)

            dve.memset(ones[:, :], 1.0)
            dve.wait_ge(gate_ready, 1)
            def scales(n, src, tiles):
                ts = slice(tiles[0], tiles[-1] + 1)
                for t in tiles:
                    last = dve.tensor_reduce(amax[:, n, t:t + 1], src(t), AX.X, ALU.max, apply_absolute_value=True)
                ch.link(last)
                ch.link(dve.tensor_scalar(amax[:, n, ts], amax[:, n, ts], 1e-5, None, ALU.max))
                ch.link(dve.reciprocal(arec[:, n, ts], amax[:, n, ts]))
                ch.link(dve.tensor_scalar(ascale[:, n, ts], arec[:, n, ts], 128.0, None, ALU.mult))

            def residual(t):
                dve.wait_ge(wo_done, t + 1)
                return dve.scalar_tensor_tensor(out=x[:, t, :], in0=ps[2 * t][:TT, 0:H], scalar=gate[:TT, 0:1],
                                                in1=x[:, t, :], op0=ALU.mult, op1=ALU.add)

            def quantised(n, tiles):
                ts = slice(tiles[0], tiles[-1] + 1)
                layer_norm(dve, ch, x, stats, mv, var, var_ready, rstd_ready, rstd, xn, xn_ready, n, tiles)
                dve.wait_ge(xn_ready, tiles[-1] + 1)
                scales(0, lambda t: xn[:, t, :], tiles)
                for k in range(2):
                    last = dve.tensor_scalar(deq[:, k, ts], amax[:, 0, ts], 1.0 / 128, wmean[:TT, k:k + 1],
                                             ALU.mult, ALU.mult)
                ch.link(last)
                for t in tiles:
                    last = dve.tensor_scalar(xq_t[:, t, :], xn[:, t, :], ascale[:, 0, t:t + 1], BIG, ALU.mult, ALU.add)
                ch.link(last)
                for t in tiles:
                    dve.tensor_scalar(xq[:, t, :], xq_t[:, t, :], BIG, 127.0, ALU.subtract, ALU.min).then_inc(xq_ready, 1)

            residual(0)
            dve.wait_ge(w_loaded, 48)
            dve.tensor_reduce(wabs[:, 0:3], w_raw[:, :, :], AX.X, ALU.add, apply_absolute_value=True
                              ).then_inc(wabs_ready, 1)
            residual(1)
            dve.wait_ge(wsum_done, 1)
            ch.link(dve.tensor_scalar(wmean[:, 0:3], ps[7][:, 0:3], 1.0 / (F0 * H), 1e-5, ALU.mult, ALU.max))
            ch.link(dve.reciprocal(wscale[:, 0:3], wmean[:, 0:3]))
            ternary(0)
            ternary(1)
            ch.link(residual(2))
            quantised(0, range(NT - 1))
            ch.link(residual(NT - 1))
            quantised(1, range(NT - 1, NT))
            for n in range(2):
                for t in range(NT):
                    dve.wait_ge(silu_done, n * NT + t + 1)
                    dve.scalar_tensor_tensor(out=inter[:, t, n * 512:(n + 1) * 512], in0=ps[2 * t + 1][:TT, :],
                                             scalar=deq[:, 1, t:t + 1], in1=sg[:, t, n, :],
                                             op0=ALU.mult, op1=ALU.mult).then_inc(inter_ready, 1)
            ternary(2)
            ch.link(dve.tensor_scalar(wmean[:, 3:4], wmean[:, 2:3], gate[:, 2:3], 1.0 / 128, ALU.mult, ALU.mult))
            for t in range(NT):
                if t < NT - 1:
                    butterflies(dve, ch, t)
                else:
                    dve.wait_ge(had_summed, 3)
                scales(1, lambda t: inter[:, t, :], range(t, t + 1))
                dve.tensor_scalar(deq[:, 2, t:t + 1], amax[:, 1, t:t + 1], wmean[:TT, 3:4], None, ALU.mult)
                ch.link(dve.tensor_scalar(u[0][:, t].rearrange("p c d -> p (c d)"), inter[:, t, :],
                                          ascale[:, 1, t:t + 1], BIG, ALU.mult, ALU.add))
                dve.tensor_scalar(zq[:, t, :], u[0][:, t].rearrange("p c d -> p (c d)"), BIG, 127.0,
                                  ALU.subtract, ALU.min).then_inc(zq_ready, 1)
            for t in range(NT):
                dve.wait_ge(down_done, t + 1)
                last = dve.scalar_tensor_tensor(out=x[:, t, :], in0=ps[2 * t + 1][:TT, 0:H], scalar=deq[:, 2, t:t + 1],
                                                in1=x[:, t, :], op0=ALU.mult, op1=ALU.add)
            ch.link(last)
            layer_norm(dve, ch, x, stats, mv, var, var_ready, rstd_ready, rstd, xn, xn_ready, 2)
            dve.wait_ge(c_loaded, 64)
            nxt["split_low"](dve)
            for o in range(KC):
                dve.wait_ge(q1_done, o + 1)
                dve.tensor_scalar(q1T[:, o, :], ps[2 * o][:, 0:T], bq1[:, o:o + 1], None, ALU.add).then_inc(q1_copied, 1)
            dve.wait_ge(q1_copied, KC)


PC1, CP1 = 3, 4
W1 = CP1 * CH


def attention1_inputs(sem, sb, place, ctx_in, mask_in, wk_in, bk_in, wv_in, bv_in, eye8_in, eye4_in):
    t = {"wkv": sb("d_wkv", [P, 2, KC, H]), "raw": place("d_ctx", NH * H, [2, KC, W1]), "w_loaded": sem("d_w_loaded"),
         "whi": sb("d_whi", [P, 2, KC, H], F32R), "wlo": sb("d_wlo", [P, 2, KC, H], F32R),
         "chi": place("d_ctx_hi", 0, [2, KC, W1], F32R), "clo": place("d_ctx_lo", 2 * KC * W1, [2, KC, W1], F32R),
         "bk": sb("d_bk", [P, KC]), "bv": sb("d_bv", [GW, NG1]), "eye8": sb("d_eye8", [P, 8]),
         "eye4": sb("d_eye4", [GW, HPG]), "mask_i": sb("d_mask_i", [CH, B, NC], I32), "m_loaded": sem("d_misc_loaded"),
         "w_hi": sem("d_w_hi"), "ctx_hi": sem("d_ctx_hi"), "ctx_lo": sem("d_ctx_lo"),
         "ctx_loaded": [sem(f"d_ctx_loaded{i}") for i in range(2)]}

    def load(sp):
        for k, w in enumerate((wk_in, wv_in)):
            sp.dma_start(t["wkv"][:, k], w.rearrange("(c p) n -> p c n", p=P)).then_inc(t["w_loaded"], 16)
        for pc in range(2):
            sp.dma_start(t["raw"][:, pc], ctx_in[0, :, pc * W1:(pc + 1) * W1].rearrange("(c p) s -> p c s", p=P)
                         ).then_inc(t["ctx_loaded"][pc], 16)
        for name, src in (("bk", bk_in), ("bv", bv_in), ("eye8", eye8_in), ("eye4", eye4_in)):
            sp.dma_start(t[name][:, :], src).then_inc(t["m_loaded"], 16)
        sp.dma_start(t["mask_i"][:, :, :], mask_in).then_inc(t["m_loaded"], 16)

    def split_high(act):
        act.wait_ge(t["w_loaded"], 32)
        act.copy(t["whi"][:, :, :, :], t["wkv"][:, :, :, :]).then_inc(t["w_hi"], 1)
        for pc in range(2):
            act.wait_ge(t["ctx_loaded"][pc], 16)
            act.copy(t["chi"][:, pc], t["raw"][:, pc]).then_inc(t["ctx_hi"], 1)

    def split_low(dve):
        dve.wait_ge(t["w_hi"], 1)
        dve.tensor_tensor(t["wlo"][:, :, :, :], t["wkv"][:, :, :, :], t["whi"].bitcast(F32)[:, :, :, :], ALU.subtract)
        for pc in range(2):
            dve.wait_ge(t["ctx_hi"], pc + 1)
            dve.tensor_tensor(t["clo"][:, pc], t["raw"][:, pc], t["chi"][:, pc].bitcast(F32), ALU.subtract
                              ).then_inc(t["ctx_lo"], 1)

    t["load"], t["split_high"], t["split_low"] = load, split_high, split_low
    return t


def attention1_phase(nc, sem, keep, pre, load_next, ctx_in):
    with ExitStack() as ctx:
        sb = lambda name, shape, dt=F32: ctx.enter_context(nc.sbuf_tensor(name, shape, dt))
        q1T, o1T = keep["q1T"], keep["o1T"]
        HW = 8 * S
        VW = GW + 2
        STEPS = 2 * NC
        HALF_AT = (0, 4, 8, 12, 16, 20)
        RECIPS = ((0, 2), (2, 4), (4, 6), (6, 7), (7, 8))
        AHEAD = 3
        whi, wlo, raw, chi, clo, ctx_loaded, w_hi, ctx_hi, ctx_lo = (
            pre[n] for n in ("whi", "wlo", "raw", "chi", "clo", "ctx_loaded", "w_hi", "ctx_hi", "ctx_lo"))
        bk, bv, eye8, eye4, mask_i, m_loaded = (pre[n] for n in ("bk", "bv", "eye8", "eye4", "mask_i", "m_loaded"))
        att = sb("d_attend", [CH, B, NC])
        e_scale = sb("d_exp_scale", [CH, B, NC])
        e_bias = sb("d_exp_bias", [CH, B, NC])
        esc = sb("d_exp_scale_now", [CH, 2, NC])
        ebi = sb("d_exp_bias_now", [CH, 2, NC])
        k_hi = [sb(f"d_kT_hi{i}", [P, KC, S2], F32R) for i in range(2)]
        k_lo = [sb(f"d_kT_lo{i}", [P, KC, S2], F32R) for i in range(2)]
        v_hi = [sb(f"d_v_hi{i}", [CH, NC, NG1, VW], F32R) for i in range(2)]
        v_lo = [sb(f"d_v_lo{i}", [CH, NC, NG1, VW], F32R) for i in range(2)]
        q1_hi = sb("d_q1_hi", [P, KC, T], F32R)
        q1_lo = q1T
        q_hi = [sb(f"d_q_hi{i}", [P, 2, 8, S], F32R) for i in range(2)]
        q_lo = [sb(f"d_q_lo{i}", [P, 2, 8, S], F32R) for i in range(2)]
        p = [sb(f"d_p{i}", [CH, HW]) for i in range(3)]
        p_hi = [sb(f"d_p_hi{i}", [CH, HW], F32R) for i in range(3)]
        p_lo = [sb(f"d_p_lo{i}", [CH, HW], F32R) for i in range(3)]
        ones = sb("d_ones", [P, GW])
        consts = sb("d_one_zero", [CH, 2, NC * NG1])
        den = sb("d_den", [P, NG1, HPG * S])
        o_m = sb("d_o_masked", [GW, NG1, HPG, S])
        d_m = sb("d_den_masked", [GW, NG1, HPG, S])
        dsum = sb("d_sums", [GW, NG1, T])
        bank = lambda name: ctx.enter_context(nc.psum_tensor(name, [P, 512], F32))
        ps_s = [bank(f"d_ps_s{i}") for i in range(4)]
        ps_r = [ps_s[2], ps_s[3]]
        ps_k, ps_v = bank("d_ps_k"), bank("d_ps_v")
        ps_o = [bank(f"d_ps_o{i}") for i in range(2)]
        prep, now_ready, q_ready, chain = (sem(n) for n in (
            "d_prepared", "d_now_ready", "d_q_ready", "d_chain"))
        (k_done, khi_ready, k_split, v_done, vhi_ready, v_split, s_done, exp_done, p_clipped, phi_ready,
         p_ready) = (sem(n) for n in (
            "d_k_done", "d_k_hi_ready", "d_k_split", "d_v_done", "d_v_hi_ready", "d_v_split",
            "d_s_done", "d_exp_done", "d_p_clipped", "d_p_hi_ready", "d_p_ready"))
        o_free, den_copied, r_done, r_free, o_ready, ones_set, consts_set = (sem(n) for n in (
            "d_o_masked", "d_den_copied", "d_den_spread", "d_den_masked", "d_o_ready", "d_ones_set", "d_consts_set"))
        p_used, prep0, recip_ready = sem("d_p_used"), sem("d_mask_read"), sem("d_recip_ready")
        block = ctx.enter_context(nc.Block())
        POST = 5

        def batches(eng, attend, first):
            first()
            with eng.Fori(0, B // 2 - 1) as i:
                for par in range(2):
                    attend(i * 2 + par, par, False)
            for par in range(2):
                attend(B - 2 + par, par, par == 1)

        def slot(par, pc):
            return (PC1 * par + pc) % 2

        @block.sync
        def _(sp):
            def load(b, par, first_piece=0):
                for pc in range(first_piece, PC1):
                    wait_for(sp, ctx_lo, PC1 * b + pc - 1)
                    sp.dma_start(raw[:, slot(par, pc)],
                                 ctx_in[b, :, pc * W1:(pc + 1) * W1].rearrange("(c p) s -> p c s", p=P)
                                 ).then_inc(ctx_loaded[slot(par, pc)], 16)

            def attend(b, par, last):
                if not last:
                    load(b + 1, 1 - par)

            def first():
                load(0, 0, 2)
                load_next(sp)

            batches(sp, attend, first)

        @block.gpsimd
        def _(pool):
            pool.memset(ones[:, :], 1.0).then_inc(ones_set, 1)
            pool.memset(o_m[:, :, :, :], 0.0).then_inc(o_ready, 1)
            pool.memset(consts[:, 0, :], 1.0).then_inc(consts_set, 1)
            pool.memset(consts[:, 1, :], 0.0).then_inc(consts_set, 1)
            pool.wait_ge(consts_set, 2)
            for i in range(2):
                for k, v in enumerate((v_hi, v_lo)):
                    for j in range(VW - GW):
                        pool.tensor_copy(v[i][:, :, :, GW + j], consts[:, k, :].rearrange("p (c g) -> p c g", c=NC)
                                         ).then_inc(ones_set, 1)
            pool.wait_ge(prep, 1)

            def now(b, par):
                if not (isinstance(b, int) and b == 0):
                    pool.wait_ge(exp_done, (b - 1) * STEPS + 1)
                pool.tensor_copy(esc[:, par, :], e_scale[:, b, :])
                pool.tensor_copy(ebi[:, par, :], e_bias[:, b, :]).then_inc(now_ready, 1)

            def finish(ch, n):
                b0, b1 = RECIPS[n]
                cols = slice(b0 * S, b1 * S)
                pool.wait_ge(recip_ready, n + 1)
                ch.link(pool.tensor_tensor(o1T[:, :, cols], o1T[:, :, cols], dsum[:, :, cols], ALU.mult))
                ch.link(pool.tensor_tensor(o1T[:, :, cols], o1T[:, :, cols],
                                           bv[:, :].unsqueeze(2).broadcast_to([GW, NG1, (b1 - b0) * S]), ALU.add))

            def attend(b, par, last):
                if not last:
                    now(b + 1, 1 - par)
                ch = Chain(pool, chain, b * POST)
                if last:
                    for n in range(len(RECIPS) - 1):
                        finish(ch, n)
                for m, free in ((o_m, o_free), (d_m, r_free))[:1 if last else 2]:
                    pool.wait_ge(free, b * 2 + 4)
                    pool.tensor_tensor(m[:, :, 0, :], m[:, :, 0, :], m[:, :, 1, :], ALU.add)
                    ch.link(pool.tensor_tensor(m[:, :, 2, :], m[:, :, 2, :], m[:, :, 3, :], ALU.add))
                    ch.link(pool.tensor_tensor(m[:, :, 0, :], m[:, :, 0, :], m[:, :, 2, :], ALU.add))
                if last:
                    pool.tensor_copy(o1T[:, :, bass.ds(b * S, S)], o_m[:, :, 0, :]).then_inc(o_ready, 1)
                    pool.wait_ge(o_ready, b + 2)
                    finish(ch, len(RECIPS) - 1)
                    return
                pool.tensor_copy(o1T[:, :, bass.ds(b * S, S)], o_m[:, :, 0, :])
                ch.link(pool.tensor_scalar(d_m[:, :, 1, :], d_m[:, :, 0, :], 1e-8, None, ALU.mult))
                pool.tensor_tensor(dsum[:, :, bass.ds(b * S, S)], d_m[:, :, 1, :], d_m[:, :, 0, :],
                                   ALU.add).then_inc(o_ready, 1)
                pool.wait_ge(o_ready, b + 2)

            batches(pool, attend, lambda: now(0, 0))

        @block.scalar
        def _(act):
            def split(b, par, pc):
                s = slot(par, pc)
                act.wait_ge(ctx_loaded[s], (b - par) * 24 + 16 * ((PC1 * par + pc) // 2 + 1))
                wait_for(act, v_done, 2 * (PC1 * b + pc - 1))
                act.copy(chi[:, s], raw[:, s]).then_inc(ctx_hi, 1)

            def half_out(b, par, h):
                pc, half = h // 2, h % 2
                act.wait_ge(k_done, 6 * b + h + 1)
                act.activation(k_hi[par][:, half, pc * W1:(pc + 1) * W1], ps_k[:, 0:W1], ACT.Identity,
                               bias=bk[:, half:half + 1]).then_inc(khi_ready, 1)
                act.wait_ge(v_done, 6 * b + h + 1)
                act.copy(v_hi[par][:, 2 * h:2 * h + 2, :, 0:GW],
                         ps_v[:CH, :].rearrange("p (c g d) -> p c g d", c=2, g=NG1)).then_inc(vhi_ready, 1)

            def first():
                act.copy(q1_hi[:, :, :], q1T[:, :, :]).then_inc(w_hi, 1)
                act.wait_ge(m_loaded, 80)
                for h in range(2 * PC1):
                    if h == 2:
                        split(0, 0, 2)
                    half_out(0, 0, h)

            def attend(b, par, last):
                if not last:
                    split(b + 1, 1 - par, 0)
                act.wait_ge(now_ready, b + 1)

                def high(v):
                    act.wait_ge(p_clipped, b * STEPS + v + 1)
                    if v >= 3:
                        act.wait_ge(p_used, b * STEPS + v - 2)
                    act.copy(p_hi[v % 3][:, :], p[v % 3][:, :]).then_inc(phi_ready, 1)

                for v in range(STEPS):
                    act.wait_ge(s_done, b * STEPS + v + 1)
                    if v >= 3:
                        act.wait_ge(p_ready, b * STEPS + v - 2)
                    act.activation(p[v % 3][:, :], ps_s[v % 4][:CH, 0:HW], ACT.Exp, bias=ebi[:, par, v // 2:v // 2 + 1],
                                   scale=esc[:, par, v // 2:v // 2 + 1]).then_inc(exp_done, 1)
                    if v >= 1:
                        high(v - 1)
                    if not last:
                        if v in (5, 13):
                            split(b + 1, 1 - par, (v + 3) // 8)
                        if v - AHEAD in HALF_AT and v < STEPS - 1:
                            half_out(b + 1, 1 - par, HALF_AT.index(v - AHEAD))
                high(STEPS - 1)
                if not last:
                    half_out(b + 1, 1 - par, 5)
                for k in range(2):
                    act.wait_ge(p_used, b * STEPS + STEPS)
                    act.copy(den[GW:GW + 1, 2 * k:2 * k + 2, :],
                             ps_o[k][GW:GW + 1, 0:HW].rearrange("p (g q) -> p g q", g=2)).then_inc(den_copied, 1)

            batches(act, attend, first)

        @block.tensor
        def _(pe):
            def project(b, par, h):
                pc, half = h // 2, h % 2
                s = slot(par, pc)
                n = 6 * b + h
                if half == 0:
                    pe.wait_ge(ctx_lo, PC1 * b + pc + 1)
                wait_for(pe, k_split, n)
                m = 0
                for c in range(KC):
                    for a, w in ((chi, whi), (chi, wlo), (clo, whi)):
                        mm = pe.matmul(ps_k[:, 0:W1], w[:, 0, c, half * P:(half + 1) * P], a[:, s, c, :],
                                       start=m == 0, stop=m == 3 * KC - 1)
                        m += 1
                mm.then_inc(k_done, 1)
                wait_for(pe, v_split, n)
                for cc in range(2):
                    ch_ = 2 * half + cc
                    m = 0
                    for c in range(KC):
                        for a, w in ((chi, whi), (chi, wlo), (clo, whi)):
                            mm = pe.matmul(ps_v[:CH, cc * H:(cc + 1) * H], a[:, s, c, ch_ * CH:(ch_ + 1) * CH],
                                           w[:, 1, c, :], start=m == 0, stop=m == 3 * KC - 1)
                            m += 1
                mm.then_inc(v_done, 1)

            def scores(b, par, v):
                c, half = v // 2, v % 2
                if v >= 4:
                    pe.wait_ge(exp_done, b * STEPS + v - 3)
                elif v >= 2:
                    pe.wait_ge(r_free, b * 2 + v - 1)
                for m, (k, q) in enumerate(((k_hi, q_hi), (k_hi, q_lo), (k_lo, q_hi))):
                    mm = pe.matmul(ps_s[v % 4][:CH, 0:HW], k[par][:, half, c * CH:(c + 1) * CH],
                                   q[par][:, half].rearrange("p h s -> p (h s)"), start=m == 0, stop=m == 2)
                mm.then_inc(s_done, 1)

            def values(b, par, v):
                c, half = v // 2, v % 2
                pe.wait_ge(p_ready, b * STEPS + v + 1)
                if c == 0:
                    pe.wait_ge(o_free, b * 2 + half + 1)
                for gg in range(2):
                    for m, (val, pr) in enumerate(((v_hi, p_hi), (v_hi, p_lo), (v_lo, p_hi))):
                        mm = pe.matmul(ps_o[half][:VW, gg * HPG * S:(gg + 1) * HPG * S], val[par][:, c, 2 * half + gg, :],
                                       pr[v % 3][:, gg * HPG * S:(gg + 1) * HPG * S],
                                       start=c == 0 and gg == 0 and m == 0, stop=c == NC - 1 and m == 2,
                                       skip_group_check=True)
                mm.then_inc(p_used, 1)

            def spread(b):
                pe.wait_ge(exp_done, b * STEPS + STEPS)
                pe.wait_ge(den_copied, b * 2 + 2)
                for k in range(2):
                    pe.matmul(ps_r[k][:GW, 0:HW], ones[GW:GW + 1, :], den[GW:GW + 1, 2 * k:2 * k + 2, :].rearrange("p g q -> p (g q)"),
                              start=True, stop=True).then_inc(r_done, 1)

            def first():
                for h in range(6):
                    project(0, 0, h)
                pe.wait_ge(ones_set, 9)

            def attend(b, par, last):
                pe.wait_ge(k_split, 6 * b + 6)
                pe.wait_ge(v_split, 6 * b + 6)
                pe.wait_ge(q_ready, b + 1)
                for v in range(AHEAD):
                    scores(b, par, v)
                for v in range(STEPS):
                    if v + AHEAD < STEPS:
                        scores(b, par, v + AHEAD)
                    if v in HALF_AT and not last:
                        project(b + 1, 1 - par, HALF_AT.index(v))
                    values(b, par, v)
                spread(b)

            batches(pe, attend, first)

        @block.vector
        def _(dve):
            def split(b, par, pc):
                s = slot(par, pc)
                dve.wait_ge(ctx_hi, PC1 * b + pc + 1)
                dve.tensor_tensor(clo[:, s], raw[:, s], chi[:, s].bitcast(F32), ALU.subtract).then_inc(ctx_lo, 1)

            def half_out(b, par, h):
                pc, half = h // 2, h % 2
                dve.wait_ge(khi_ready, 6 * b + h + 1)
                cols = slice(pc * W1, (pc + 1) * W1)
                dve.scalar_tensor_tensor(out=k_lo[par][:, half, cols], in0=ps_k[:, 0:W1], scalar=bk[:, half:half + 1],
                                         in1=k_hi[par].bitcast(F32)[:, half, cols],
                                         op0=ALU.add, op1=ALU.subtract).then_inc(k_split, 1)
                dve.wait_ge(vhi_ready, 6 * b + h + 1)
                dve.tensor_tensor(v_lo[par][:, 2 * h:2 * h + 2, :, 0:GW],
                                  ps_v[:CH, :].rearrange("p (c g d) -> p c g d", c=2, g=NG1),
                                  v_hi[par].bitcast(F32)[:, 2 * h:2 * h + 2, :, 0:GW], ALU.subtract).then_inc(v_split, 1)

            def queries(b, par):
                for q1, q in ((q1_hi.bitcast(F32), q_hi), (q1_lo, q_lo)):
                    for half in range(2):
                        last = dve.tensor_tensor(q[par][:, half],
                                                 q1[:, half, bass.ds(b * S, S)].unsqueeze(1).broadcast_to([P, 8, S]),
                                                 eye8[:, :].unsqueeze(2).broadcast_to([P, 8, S]), ALU.mult)
                last.then_inc(q_ready, 1)

            def first():
                dve.wait_ge(m_loaded, 80)
                ch0 = Chain(dve, prep0)
                ch0.link(dve.tensor_scalar(att[:, :, :], mask_i[:, :, :], 0.5, None, ALU.is_gt))
                dve.tensor_scalar(e_scale[:, :, :], att[:, :, :], float(D1) ** -0.5, None, ALU.mult)
                dve.tensor_scalar(e_bias[:, :, :], att[:, :, :], 1.0, 50.0, ALU.subtract, ALU.mult).then_inc(prep, 1)
                dve.wait_ge(w_hi, 2)
                ch0.link(dve.tensor_tensor(q1_lo[:, :, :], q1T[:, :, :], q1_hi.bitcast(F32)[:, :, :], ALU.subtract))
                for h in range(2 * PC1):
                    if h == 2:
                        split(0, 0, 2)
                    half_out(0, 0, h)
                    if h == 3:
                        queries(0, 0)
                dve.memset(d_m[:, 0, 0, 0:1], 0.0).then_inc(o_free, 2)
                dve.memset(d_m[:, 0, 0, 1:2], 0.0).then_inc(r_free, 2)

            def recip(n):
                cols = slice(RECIPS[n][0] * S, RECIPS[n][1] * S)
                dve.wait_ge(o_ready, RECIPS[n][1] + 1)
                dve.reciprocal(dsum[:, :, cols], dsum[:, :, cols]).then_inc(recip_ready, 1)

            def attend(b, par, last):
                if not last:
                    split(b + 1, 1 - par, 0)

                def low(v):
                    dve.wait_ge(phi_ready, b * STEPS + v + 1)
                    dve.tensor_tensor(p_lo[v % 3][:, :], p[v % 3][:, :], p_hi[v % 3].bitcast(F32)[:, :],
                                      ALU.subtract).then_inc(p_ready, 1)

                for v in range(STEPS):
                    dve.wait_ge(exp_done, b * STEPS + v + 1)
                    dve.tensor_scalar(p[v % 3][:, :], p[v % 3][:, :], E_LO, E_HI, ALU.max, ALU.min).then_inc(p_clipped, 1)
                    if v >= 1:
                        low(v - 1)
                    if isinstance(b, int) and b == B - 2 and v in (1, 5, 9):
                        recip(v // 4)
                    if last and v == 1:
                        recip(len(RECIPS) - 2)
                    if not last:
                        if v in (5, 13):
                            split(b + 1, 1 - par, (v + 3) // 8)
                        if v - AHEAD in HALF_AT and v < STEPS - 1:
                            half_out(b + 1, 1 - par, HALF_AT.index(v - AHEAD))
                        if v == 9:
                            queries(b + 1, 1 - par)
                low(STEPS - 1)
                if not last:
                    half_out(b + 1, 1 - par, 5)
                dve.wait_ge(o_ready, b + 1)
                own4 = eye4[:, :].unsqueeze(2).broadcast_to([GW, HPG, S])
                for k in range(2):
                    dve.wait_ge(p_used, b * STEPS + STEPS)
                    for gg in range(2):
                        src = ps_o[k][:GW, gg * HPG * S:(gg + 1) * HPG * S].rearrange("p (j s) -> p j s", j=HPG)
                        ins = dve.tensor_tensor(o_m[:, 2 * k + gg], src, own4, ALU.mult)
                    ins.then_inc(o_free, 1)
                for k in range(2):
                    dve.wait_ge(r_done, b * 2 + k + 1)
                    for gg in range(2):
                        src = ps_r[k][:GW, gg * HPG * S:(gg + 1) * HPG * S].rearrange("p (j s) -> p j s", j=HPG)
                        ins = dve.tensor_tensor(d_m[:, 2 * k + gg], src, own4, ALU.mult)
                    ins.then_inc(r_free, 1)
                if last:
                    ch1 = Chain(dve, prep0, 2)
                    dve.wait_ge(r_free, b * 2 + 4)
                    dve.tensor_tensor(d_m[:, :, 0, :], d_m[:, :, 0, :], d_m[:, :, 1, :], ALU.add)
                    ch1.link(dve.tensor_tensor(d_m[:, :, 2, :], d_m[:, :, 2, :], d_m[:, :, 3, :], ALU.add))
                    ch1.link(dve.tensor_tensor(d_m[:, :, 0, :], d_m[:, :, 0, :], d_m[:, :, 2, :], ALU.add))
                    ch1.link(dve.scalar_tensor_tensor(out=dsum[:, :, b * S:(b + 1) * S], in0=d_m[:, :, 0, :], scalar=1e-8,
                                                      in1=d_m[:, :, 0, :], op0=ALU.mult, op1=ALU.add))
                    dve.reciprocal(dsum[:, :, RECIPS[-1][0] * S:RECIPS[-1][1] * S],
                                   dsum[:, :, RECIPS[-1][0] * S:RECIPS[-1][1] * S]).then_inc(recip_ready, 1)

            batches(dve, attend, first)


def experts_inputs(sem, sb, wo_in, bo_in, gamma_in, beta_in, rs_in):
    t = {"wo": sb("e_wo", [GW, NG1, H]), "bo": sb("e_bo", [TT, H]), "gamma": sb("e_gamma", [TT, H]),
         "beta": sb("e_beta", [TT, H]), "rs_raw": sb("e_rs_raw", [TT, 1]),
         "wo_loaded": sem("e_wo_loaded"), "ln_loaded": sem("e_ln_loaded")}

    def load(sp):
        sp.dma_start(t["wo"][:, :, :], wo_in.rearrange("(g d) n -> d g n", d=GW)).then_inc(t["wo_loaded"], 16)
        for name, src in (("bo", bo_in), ("gamma", gamma_in), ("beta", beta_in), ("rs_raw", rs_in)):
            sp.dma_start(t[name][:, :], src.partition_broadcast(TT)).then_inc(t["ln_loaded"], 16)

    t["load"] = load
    return t


def experts_phase(nc, sem, keep, pre, rw_in, rb_in, w1_in, b1_in, w2_in, b2_in, out):
    NE = w1_in.shape[0]
    NR, NSH = rw_in.shape[1], w1_in.shape[0] - rw_in.shape[1]
    HH = w1_in.shape[2] // 2
    TOPK = 6
    RING = 4
    assert NE % RING == 2
    with ExitStack() as ctx:
        sb = lambda name, shape, dt=F32: ctx.enter_context(nc.sbuf_tensor(name, shape, dt))
        x, ident, mhalf, gate, o1T = (keep[n] for n in ("x", "ident", "mhalf", "gate", "o1T"))
        wo, bo, gamma, beta, rs_raw, wo_loaded, ln_loaded = (
            pre[n] for n in ("wo", "bo", "gamma", "beta", "rs_raw", "wo_loaded", "ln_loaded"))
        rs = sb("e_rs", [TT, 1])
        rw = sb("e_rw", [P, KC, NR])
        rb = sb("e_rb", [TT, NR])
        d = sb("e_delta", [TT, NT, H])
        fin = sb("e_finite", [TT, 3, H], I32)
        limits = sb("e_limits", [TT, 2, H])
        dn = sb("e_delta_norm", [TT, NT, H])
        stats = sb("e_stats", [TT, NT, 6])
        mv = sb("e_mv", [TT, NT, 2])
        var = sb("e_var", [TT, NT])
        rstd = sb("e_rstd", [TT, NT])
        xn = sb("e_xn", [TT, NT, H])
        xnT = sb("e_xnT", [P, KC, T])
        lg = sb("e_logits", [TT, NT, NR])
        nmx = sb("e_neg_max", [TT, NT])
        pr = sb("e_probs", [TT, NT, NR + 2])
        psum_ = sb("e_prob_sum", [TT, NT])
        prec = sb("e_prob_rec", [TT, NT])
        top = sb("e_top8", [TT, NT, 8])
        marked = sb("e_marked", [TT, NT, NR + 2])
        chosen = sb("e_chosen", [TT, NT, NR])
        gs = sb("e_gate_sum", [TT, NT])
        gr = sb("e_gate_rec", [TT, NT])
        g = sb("e_gates", [TT, NT, NE])
        gT = sb("e_gatesT", [NE, T])
        b2 = sb("e_b2", [NE, H])
        acc = sb("e_acc", [TT, NT, H])
        w1 = [sb(f"e_w1_{i}", [P, KC, 2 * HH]) for i in range(RING)]
        w2 = [sb(f"e_w2_{i}", [HH, 2, H]) for i in range(RING)]
        b1 = [sb(f"e_b1_{i}", [HH, 2]) for i in range(RING)]
        w1hi = [sb(f"e_w1hi_{i}", [P, KC, 2 * HH], F32R) for i in range(2)]
        w1lo = [sb(f"e_w1lo_{i}", [P, KC, 2 * HH], F32R) for i in range(2)]
        xhi = sb("e_xnT_hi", [P, KC, T], F32R)
        xlo = sb("e_xnT_lo", [P, KC, T], F32R)
        gcol = [sb(f"e_gcol{i}", [TT, NT]) for i in range(2)]
        w2hi = [sb(f"e_w2hi_{i}", [HH, 2, H], F32R) for i in range(2)]
        w2lo = [sb(f"e_w2lo_{i}", [HH, 2, H], F32R) for i in range(2)]
        hT = [sb(f"e_hT{i}", [HH, 2, T]) for i in range(2)]
        hhi = [sb(f"e_hT_hi{i}", [HH, 2, T], F32R) for i in range(2)]
        hlo = [sb(f"e_hT_lo{i}", [HH, 2, T], F32R) for i in range(2)]
        ps = [ctx.enter_context(nc.psum_tensor(f"e_ps{i}", [P, 512], F32)) for i in range(8)]
        (r_loaded, sent_set, var_ready, rstd_ready, xn_ready, wo_done, chain,
         xnt_done, xnt_copied, lg_done, max_ready, exp_done, gates_ready, gates_used, gt_copied,
         x_ready, stored) = (sem("e_" + n) for n in (
            "router_loaded", "sentinels_set", "var_ready", "rstd_ready",
            "xn_ready", "wo_done", "chain", "xnT_done", "xnT_copied", "logits_done", "max_ready", "exp_done",
            "gates_ready", "gates_used", "gatesT_copied", "x_ready", "stored"))
        w_loaded = [sem(f"e_w_loaded{i}") for i in range(RING)]
        w_hi, w_lo, w2_hi, w2_lo = (sem(n) for n in ("e_w_hi", "e_w_lo", "e_w2_hi", "e_w2_lo"))
        gcol_ready, h_done, h_ready, low_ready, y_done, y_added = (sem("e_" + n) for n in (
            "gcol_ready", "h_done", "h_ready", "low_ready", "y_done", "y_added"))
        block = ctx.enter_context(nc.Block())

        @block.sync
        def _(sp):
            def load(e, slot):
                if not (isinstance(e, int) and e < RING):
                    sp.wait_ge(y_done, (e - RING) * 2 + 2)
                sp.dma_start(w1[slot][:, :, :], w1_in[e].rearrange("(c p) n -> p c n", p=P)).then_inc(w_loaded[slot], 16)
                sp.dma_start(w2[slot][:, :, :], w2_in[e].rearrange("(k d) n -> d k n", d=HH)).then_inc(w_loaded[slot], 16)
                sp.dma_start(b1[slot][:, :], b1_in[e]).then_inc(w_loaded[slot], 16)

            for e in range(RING):
                load(e, e)
                if e == 1:
                    sp.dma_start(rw[:, :, :], rw_in.rearrange("(c p) n -> p c n", p=P)).then_inc(r_loaded, 16)
                    sp.dma_start(rb[:, :], rb_in.partition_broadcast(TT)).then_inc(r_loaded, 16)
                    sp.dma_start(b2[:, :], b2_in).then_inc(r_loaded, 16)
            with sp.Fori(1, NE // RING) as i:
                for j in range(RING):
                    load(i * RING + j, j)
            for j in range(2):
                load(NE - 2 + j, j)
            for t in range(NT):
                sp.wait_ge(x_ready, t + 1)
                sp.dma_start(out[t * TT:(t + 1) * TT, :], x[:, t, :]).then_inc(stored, 16)
            sp.wait_ge(stored, 16 * NT)

        @block.gpsimd
        def _(pool):
            for k in range(2):
                pool.memset(pr[:, :, NR + k:NR + k + 1], -1.0 - k).then_inc(sent_set, 1)
            pool.memset(g[:, :, NR:], 1.0 / NSH).then_inc(sent_set, 1)
            for n in range(2):
                pool.wait_ge(var_ready, n + 1)
                pool.tensor_tensor(rstd[:, :], var[:, :], mhalf[:TT, 0:NT], ALU.pow).then_inc(rstd_ready, 1)
            pool.wait_ge(gates_ready, NT)

            def column(e, par):
                wait_for(pool, y_added, e * NT)
                pool.tensor_copy(gcol[par][:, :], g[:, :, bass.ds(e, 1)].rearrange("p t o -> p (t o)")).then_inc(gcol_ready, 1)

            for par in range(2):
                column(par, par)
            with pool.Fori(0, NE // 2 - 1) as i:
                for par in range(2):
                    column(i * 2 + 2 + par, par)

        @block.scalar
        def _(act):
            def split(e, slot):
                act.wait_ge(w_loaded[slot], (e - slot) * (48 // RING) + 48)
                act.copy(w1hi[slot % 2][:, :, :], w1[slot][:, :, :]).then_inc(w_hi, 1)

            split(0, 0)
            split(1, 1)
            for t in range(NT):
                act.wait_ge(xnt_done, t + 1)
                act.copy(xnT[:, :, t * TT:(t + 1) * TT], ps[t][:, 0:KC * TT].rearrange("p (c s) -> p c s", c=KC)
                         ).then_inc(xnt_copied, 1)
            act.wait_ge(xnt_copied, NT)
            act.copy(xhi[:, :, :], xnT[:, :, :]).then_inc(xnt_copied, 1)
            act.wait_ge(sent_set, 3)
            for t in range(NT):
                act.wait_ge(max_ready, t + 1)
                act.activation(pr[:, t, 0:NR], lg[:, t, :], ACT.Exp, bias=nmx[:, t:t + 1],
                               accum_out=psum_[:, t:t + 1]).then_inc(exp_done, 1)


            def split_second(e, slot):
                if not (isinstance(e, int) and e < 2):
                    act.wait_ge(y_done, (e - 2) * 2 + 2)
                act.copy(w2hi[slot % 2][:, :, :], w2[slot][:, :, :]).then_inc(w2_hi, 1)

            def hidden(e, slot):
                for k in range(2):
                    act.wait_ge(h_done, e * 2 + k + 1)
                    act.activation(hT[slot % 2][:, k, :], ps[2 * (slot % 2) + k][:HH, 0:T], ACT.Relu,
                                   bias=b1[slot][:, k:k + 1]).then_inc(h_ready, 1)
                act.wait_ge(h_ready, e * 3 + 2)
                act.copy(hhi[slot % 2][:, :, :], hT[slot % 2][:, :, :]).then_inc(h_ready, 1)

            split_second(0, 0)
            split_second(1, 1)
            hidden(0, 0)
            with act.Fori(0, NE // RING) as i:
                for j in range(RING):
                    split(i * RING + (j + 2), (j + 2) % RING)
                    hidden(i * RING + (j + 1), (j + 1) % RING)
                    split_second(i * RING + (j + 2), (j + 2) % RING)
            hidden(NE - 1, 1)

        @block.tensor
        def _(pe):
            pe.wait_ge(wo_loaded, 16)
            for t in range(NT):
                for k in range(NG1):
                    mm = pe.matmul(ps[t][:TT, 0:H], o1T[:, k, t * TT:(t + 1) * TT], wo[:, k, :],
                                   start=k == 0, stop=k == NG1 - 1)
                mm.then_inc(wo_done, 1)
            for t in range(NT):
                pe.wait_ge(xn_ready, t + 1)
                for c in range(KC):
                    mm = pe.transpose(ps[t][:, c * TT:(c + 1) * TT], xn[:, t, c * P:(c + 1) * P], ident[:TT, :TT])
                mm.then_inc(xnt_done, 1)
            pe.wait_ge(r_loaded, 48)
            for t in range(NT):
                pe.wait_ge(xnt_copied, t + 1)
                for c in range(KC):
                    mm = pe.matmul(ps[4 + t][:TT, 0:NR], xnT[:, c, t * TT:(t + 1) * TT], rw[:, c, :],
                                   start=c == 0, stop=c == KC - 1)
                mm.then_inc(lg_done, 1)

            def hidden(e, slot):
                pe.wait_ge(w_lo, e + 1)
                for k in range(2):
                    m = 0
                    for c in range(KC):
                        for w, a in ((w1hi, xhi), (w1hi, xlo), (w1lo, xhi)):
                            mm = pe.matmul(ps[2 * (slot % 2) + k][:HH, 0:T], w[slot % 2][:, c, k * HH:(k + 1) * HH],
                                           a[:, c, :], start=m == 0, stop=m == 3 * KC - 1)
                            m += 1
                    mm.then_inc(h_done, 1)

            def outputs(e, slot):
                pe.wait_ge(low_ready, e + 2)
                pe.wait_ge(w2_lo, e + 1)
                for b in range(2):
                    wait_for(pe, y_added, e * NT)
                    for tt in range(2):
                        t = 2 * b + tt
                        m = 0
                        for k in range(2):
                            for h, w in ((hhi, w2hi), (hhi, w2lo), (hlo, w2hi)):
                                mm = pe.matmul(ps[4 + 2 * (slot % 2) + b][:TT, tt * H:(tt + 1) * H],
                                               h[slot % 2][:, k, t * TT:(t + 1) * TT], w[slot % 2][:, k, :],
                                               start=m == 0, stop=m == 5)
                                m += 1
                    mm.then_inc(y_done, 1)

            pe.wait_ge(low_ready, 1)
            hidden(0, 0)
            hidden(1, 1)
            for t in range(NT):
                pe.wait_ge(gates_ready, t + 1)
                pe.transpose(ps[4 + t][:NE, 0:TT], g[:, t, :], ident[:TT, :TT]).then_inc(gates_used, 1)
            for t in range(NT):
                pe.wait_ge(gt_copied, t + 1)
                pe.matmul(ps[4 + t][:TT, 0:H], gT[:, t * TT:(t + 1) * TT], b2[:, :],
                          start=True, stop=True).then_inc(gates_used, 1)
            pe.wait_ge(y_added, NT)
            outputs(0, 0)
            with pe.Fori(0, NE // RING) as i:
                for j in range(RING):
                    hidden(i * RING + (j + 2), (j + 2) % RING)
                    outputs(i * RING + (j + 1), (j + 1) % RING)
            outputs(NE - 1, 1)

        @block.vector
        def _(dve):
            def split(e, slot):
                dve.wait_ge(w_hi, e + 1)
                dve.tensor_tensor(w1lo[slot % 2][:, :, :], w1[slot][:, :, :], w1hi[slot % 2].bitcast(F32)[:, :, :],
                                  ALU.subtract).then_inc(w_lo, 1)

            def split_second(e, slot):
                dve.wait_ge(w2_hi, e + 1)
                dve.tensor_tensor(w2lo[slot % 2][:, :, :], w2[slot][:, :, :], w2hi[slot % 2].bitcast(F32)[:, :, :],
                                  ALU.subtract).then_inc(w2_lo, 1)

            def hidden_low(e, slot):
                dve.wait_ge(h_ready, e * 3 + 3)
                dve.tensor_tensor(hlo[slot % 2][:, :, :], hT[slot % 2][:, :, :], hhi[slot % 2].bitcast(F32)[:, :, :],
                                  ALU.subtract).then_inc(low_ready, 1)

            ch = Chain(dve, chain)
            dve.wait_ge(ln_loaded, 64)
            ch.link(dve.tensor_scalar(rs[:, :], rs_raw[:, :], 0.0, 0.3, ALU.max, ALU.min))
            dve.memset(limits[:, 0, :], 1e4)
            dve.memset(limits[:, 1, :], -1e4)
            ch.link(dve.memset(dn[:, :, :], 0.0))
            for t in range(NT):
                dt, dnt = d[:, t, :], dn[:, t, :]
                dve.wait_ge(wo_done, t + 1)
                ch.link(dve.tensor_tensor(dt, ps[t][:TT, 0:H], bo[:, :], ALU.add))
                ch.link(dve.tensor_tensor(fin[:, 0, :], dt, dt, ALU.is_equal))
                ch.link(dve.copy_predicated(dnt, fin[:, 0, :], dt))
                dve.tensor_scalar(fin[:, 1, :], dnt, 3.4028235e38, None, ALU.is_gt)
                ch.link(dve.tensor_scalar(fin[:, 2, :], dnt, -3.4028235e38, None, ALU.is_lt))
                ch.link(dve.copy_predicated(dnt, fin[:, 1, :], limits[:, 0, :]))
                ch.link(dve.copy_predicated(dnt, fin[:, 2, :], limits[:, 1, :]))
                ch.link(dve.tensor_scalar(dt, dnt, rs[:, 0:1], None, ALU.mult))
                last = dve.bn_stats(stats[:, t, :], dt)
            ch.link(last)
            for t in range(NT):
                last = dve.bn_aggr(mv[:, t, :], stats[:, t, :])
            ch.link(last)
            dve.tensor_scalar(var[:, :], mv[:, :, 1], 1e-5, None, ALU.add).then_inc(var_ready, 1)
            for t in range(NT):
                last = dve.scalar_tensor_tensor(out=dn[:, t, :], in0=d[:, t, :], scalar=mv[:, t, 0:1], in1=gamma[:, :],
                                                op0=ALU.subtract, op1=ALU.mult)
            ch.link(last)
            dve.wait_ge(rstd_ready, 1)
            for t in range(NT):
                last = dve.scalar_tensor_tensor(out=dn[:, t, :], in0=dn[:, t, :], scalar=rstd[:, t:t + 1], in1=beta[:, :],
                                                op0=ALU.mult, op1=ALU.add)
            ch.link(last)
            ch.link(dve.scalar_tensor_tensor(out=x[:, :, :], in0=dn[:, :, :], scalar=gate[:TT, 1:2], in1=x[:, :, :],
                                             op0=ALU.mult, op1=ALU.add))
            layer_norm(dve, ch, x, stats, mv, var, var_ready, rstd_ready, rstd, xn, xn_ready, 1)
            split(0, 0)
            split(1, 1)
            dve.wait_ge(xnt_copied, NT + 1)
            dve.tensor_tensor(xlo[:, :, :], xnT[:, :, :], xhi.bitcast(F32)[:, :, :], ALU.subtract).then_inc(low_ready, 1)
            dve.wait_ge(r_loaded, 48)
            for t in range(NT):
                dve.wait_ge(lg_done, t + 1)
                last = dve.tensor_tensor(lg[:, t, :], ps[4 + t][:TT, 0:NR], rb[:, :], ALU.add)
            ch.link(last)
            for t in range(NT):
                dve.tensor_reduce(nmx[:, t:t + 1], lg[:, t, :], AX.X, ALU.max, negate=True).then_inc(max_ready, 1)
            dve.wait_ge(exp_done, NT)
            ch.link(dve.reciprocal(prec[:, :], psum_[:, :]))
            for t in range(NT):
                last = dve.tensor_scalar(pr[:, t, 0:NR], pr[:, t, 0:NR], prec[:, t:t + 1], None, ALU.mult)
            ch.link(last)
            for t in range(NT):
                last = dve.max(top[:, t, :], pr[:, t, 0:NR])
            ch.link(last)
            for k in range(8 - TOPK):
                last = dve.memset(top[:, :, TOPK + k:TOPK + k + 1], -1.0 - k)
            ch.link(last)
            for t in range(NT):
                last = dve.match_replace(marked[:, t, :], top[:, t, :], pr[:, t, :], -5.0)
            ch.link(last)
            ch.link(dve.tensor_scalar(chosen[:, :, :], marked[:, :, 0:NR], -5.0, None, ALU.is_equal))
            ch.link(dve.tensor_tensor(chosen[:, :, :], chosen[:, :, :], pr[:, :, 0:NR], ALU.mult))
            ch.link(dve.tensor_reduce(gs[:, :], chosen[:, :, :], AX.X, ALU.add))
            ch.link(dve.reciprocal(gr[:, :], gs[:, :]))
            for t in range(NT):
                dve.tensor_scalar(g[:, t, 0:NR], chosen[:, t, :], gr[:, t:t + 1], None, ALU.mult).then_inc(gates_ready, 1)
            for t in range(NT):
                dve.wait_ge(gates_used, t + 1)
                dve.tensor_copy(gT[:, t * TT:(t + 1) * TT], ps[4 + t][:NE, 0:TT]).then_inc(gt_copied, 1)
            for t in range(NT):
                dve.wait_ge(gates_used, NT + t + 1)
                dve.tensor_copy(acc[:, t, :], ps[4 + t][:TT, 0:H]).then_inc(y_added, 1)

            def add(e, slot):
                dve.wait_ge(gcol_ready, e + 1)
                dve.wait_ge(y_added, e * NT + NT)
                for t in range(NT):
                    if t % 2 == 0:
                        dve.wait_ge(y_done, e * 2 + t // 2 + 1)
                    dve.scalar_tensor_tensor(out=acc[:, t, :],
                                             in0=ps[4 + 2 * (slot % 2) + t // 2][:TT, (t % 2) * H:(t % 2 + 1) * H],
                                             scalar=gcol[slot % 2][:, t:t + 1], in1=acc[:, t, :],
                                             op0=ALU.mult, op1=ALU.add).then_inc(y_added, 1)

            split_second(0, 0)
            split_second(1, 1)
            hidden_low(0, 0)
            with dve.Fori(0, NE // RING) as i:
                for j in range(RING):
                    split(i * RING + (j + 2), (j + 2) % RING)
                    hidden_low(i * RING + (j + 1), (j + 1) % RING)
                    split_second(i * RING + (j + 2), (j + 2) % RING)
                    add(i * RING + j, j)
            hidden_low(NE - 1, 1)
            add(NE - 2, 0)
            add(NE - 1, 1)
            dve.wait_ge(y_added, NE * NT + NT)
            for t in range(NT):
                dve.scalar_tensor_tensor(out=x[:, t, :], in0=acc[:, t, :], scalar=gate[:TT, 3:4], in1=x[:, t, :],
                                         op0=ALU.mult, op1=ALU.add).then_inc(x_ready, 1)


def flamingo_program(nc, a, out):
    with ExitStack() as ctx:
        names = set()

        def sem(name):
            assert name not in names
            names.add(name)
            return ctx.enter_context(nc.semaphore(name))

        sb = lambda name, shape, dt=F32: ctx.enter_context(nc.sbuf_tensor(name, shape, dt))
        keep = {
            "x": sb("x", [TT, NT, H]),
            "ident": sb("ident", [P, P]),
            "mhalf": sb("minus_half", [P, 48]),
            "gate": sb("gate", [P, 4]),
        }
        place = shared_area(nc, sb, max(2 * KC * S2, NH * H + 2 * KC * W1))
        keep["wo"] = place("wo", 0, [NH, H])
        q_scratch = nc.dram_tensor("q_scratch", [B, P, NH, S], F32).ap()
        o_scratch = nc.dram_tensor("o_scratch", [NT, P, NH * TT], F32).ap()
        with ExitStack() as ctx0:
            sb0 = lambda name, shape, dt=F32: ctx0.enter_context(nc.sbuf_tensor(name, shape, dt))
            pre = attention0_inputs(sem, sb0, place, a["ctxT"], a["mask_f"], a["L0_xattn_Wk"], a["L0_xattn_bk"],
                                    a["L0_xattn_Wv"], a["L0_xattn_bv"])
            query_phase(nc, sem, keep, pre, a["x"], a["L0_xattn_Wq"], a["L0_xattn_bq"], a["L0_xattn_qn_w"],
                        a["L0_xattn_kn_w"], a["ident"], q_scratch)
            wo_loaded = sem("c_wo_loaded")

            def load_wo(sp):
                sp.dma_start(keep["wo"][:, :, :], a["L0_xattn_Wo"].rearrange("(h d) n -> d h n", d=HD)
                             ).then_inc(wo_loaded, 16)

            attention0_phase(nc, sem, keep, pre, load_wo, a["ctxT"], q_scratch, o_scratch)
        keep["q1T"] = sb("q1T", [P, KC, T])
        keep["o1T"] = sb("o1T", [GW, NG1, T])
        pre1 = attention1_inputs(sem, sb, place, a["ctxT"], a["mask_i"], a["L1_xattn_WkT"], a["L1_xattn_bk"],
                                 a["L1_xattn_WvT"], a["L1_xattn_bv"], a["eye8"], a["eye4"])
        ffn0_phase(nc, sem, keep, wo_loaded, pre1, o_scratch, a["gates"], a["ident_b"], a["hadamard"],
                   a["L0_ffn_w_gateT"], a["L0_ffn_w_upT"], a["L0_ffn_w_downT"], a["L1_xattn_WqT"], a["L1_xattn_bq"])
        pre2 = experts_inputs(sem, sb, a["L1_xattn_WoT"], a["L1_xattn_bo"], a["L1_xattn_ln_gamma"],
                              a["L1_xattn_ln_beta"], a["L1_xattn_residual_scale"])
        attention1_phase(nc, sem, keep, pre1, pre2["load"], a["ctxT"])
        experts_phase(nc, sem, keep, pre2, a["L1_ffn_router_w"], a["L1_ffn_router_b"], a["L1_ffn_w1"],
                      a["L1_ffn_b1"], a["L1_ffn_w2"], a["L1_ffn_b2"], out)


def laid_out(i):
    import numpy as np

    i = {k: np.asarray(v) for k, v in i.items()}
    a = {
        "x": i["x"].reshape(T, H),
        "ctxT": i["ctx_2048"].transpose(0, 2, 1),
        "mask_f": i["mask_1xSxS2_ff0"][0],
        "mask_i": i["mask_BxS2_ik0"].reshape(B, NC, CH).transpose(2, 0, 1),
        "gates": np.concatenate([i["g_xattn"], i["g_ffn"]]),
    }
    for n in ("Wq", "bq", "Wk", "bk", "Wv", "Wo"):
        a["L0_xattn_" + n] = i["L0_xattn_" + n]
    a["L0_xattn_bv"] = i["L0_xattn_bv"].reshape(NKV, HD).T
    for n in ("qn_w", "kn_w"):
        a["L0_xattn_" + n] = i["L0_xattn_" + n].reshape(HD, 1)
    for n in ("w_gate", "w_up", "w_down"):
        a["L0_ffn_" + n + "T"] = i["L0_ffn_" + n].T
    for n in ("Wq", "Wk", "Wv", "Wo"):
        a["L1_xattn_" + n + "T"] = i["L1_xattn_" + n].T
    for n in ("bq", "bk"):
        a["L1_xattn_" + n] = i["L1_xattn_" + n].reshape(KC, P).T
    a["L1_xattn_bv"] = i["L1_xattn_bv"].reshape(NG1, GW).T
    for n in ("bo", "ln_gamma", "ln_beta"):
        a["L1_xattn_" + n] = i["L1_xattn_" + n]
    a["L1_xattn_residual_scale"] = i["L1_xattn_residual_scale"].reshape(1)
    a["L1_ffn_router_w"] = i["L1_ffn_router_w"]
    a["L1_ffn_router_b"] = i["L1_ffn_router_b"]
    for n in ("w1", "b1", "w2", "b2"):
        a["L1_ffn_" + n] = np.concatenate([i["L1_ffn_r" + n], i["L1_ffn_s" + n]])
    b1 = a["L1_ffn_b1"]
    a["L1_ffn_b1"] = b1.reshape(b1.shape[0], 2, b1.shape[1] // 2).transpose(0, 2, 1)
    a["ident"] = np.eye(P, dtype=np.float32)
    a["ident_b"] = np.eye(P, dtype=mybir.dt.np(BF16))
    a["eye8"] = np.kron(np.eye(8, dtype=np.float32), np.ones((D1, 1), np.float32))
    a["eye4"] = np.kron(np.eye(HPG, dtype=np.float32), np.ones((D1, 1), np.float32))
    had = np.ones((1, 1), np.float32)
    while had.shape[0] < P:
        had = np.block([[had, had], [had, -had]])
    a["hadamard"] = had.astype(np.float32)
    return {"in_" + k: np.ascontiguousarray(v) for k, v in a.items()}


def kernel(**inputs):
    import numpy as np
    import concourse.bacc as bacc
    from concourse.bass_utils import run_bass_kernel_spmd

    nc = bacc.Bacc("TRN2", target_bir_lowering=False, num_devices=1)
    arrays = laid_out(inputs)
    a = {k[3:]: nc.dram_tensor(k, v.shape, mybir.dt.from_np(v.dtype), kind="ExternalInput").ap()
         for k, v in arrays.items()}
    out = nc.dram_tensor("out", (T, H), F32, kind="ExternalOutput").ap()
    flamingo_program(nc, a, out)
    r = run_bass_kernel_spmd(nc, [arrays], core_ids=[0])
    return r.results[0]["out"].reshape(B, S, H)
```
